# Optimizing a Trainium2 kernel written in Bass

```python
import numpy as np
import jax
import jax.numpy as jnp

def _softmax(x, axis=-1):
    return jax.nn.softmax(x, axis=axis)

def _gelu(x):
    return jax.nn.gelu(x, approximate=True)

def _silu(x):
    return jax.nn.silu(x)

def _sigmoid(x):
    return jax.nn.sigmoid(x)

def _layernorm(x, axis=-1, eps=1e-05):
    m = jnp.mean(x, axis=axis, keepdims=True)
    v = jnp.var(x, axis=axis, keepdims=True)
    return (x - m) / jnp.sqrt(v + eps)

def _scatter_add(tgt, idx, src, axis=0):
    return tgt.at[idx].add(src)

def _segment_sum(src, seg, n):
    return jax.ops.segment_sum(src, seg, n)
kernel_name = 'mk_gps_d1_gnn_r32_c020f4'

def setup_inputs(seed: int=0):
    np.random.seed(seed)
    _w = jnp.asarray

    def _rec_inputs():
        import jax
        import jax.numpy as jnp
        _gk = jax.random.key(seed)
        x = -0.0002117 + 1 * jax.random.normal(jax.random.fold_in(_gk, 1), (3125, 256), jnp.float32)
        src = jax.random.randint(jax.random.fold_in(_gk, 2), (50000,), 0, 3125, jnp.int32)
        dst = jnp.minimum((3125 * jax.random.uniform(jax.random.fold_in(_gk, 3), (50000,)) ** 2.0).astype(jnp.int32), 99999)
        _o = jnp.argsort(dst, stable=True)
        src = src[_o]
        dst = dst[_o]
        edge_weight = jax.random.uniform(jax.random.fold_in(_gk, 12), (50000,), jnp.float32, 0.0, 1)
        return (x, src, dst, edge_weight)
    x, src, dst, edge_weight = _rec_inputs()

    def _L0_gnn_setup():
        import jax, jax.numpy as jnp
        import numpy as np
        N_NODES = 3125
        N_EDGES = 100000
        D_IN = 256
        D_OUT = 256
        key = jax.random.key(seed)
        k1, k2, k3, k4, k5 = jax.random.split(key, 5)
        x = jax.random.normal(k1, (N_NODES, D_IN), dtype=jnp.float32)
        limit = float(np.sqrt(6.0 / (D_IN + D_OUT)))
        weight = jax.random.uniform(k2, (D_IN, D_OUT), dtype=jnp.float32, minval=-limit, maxval=limit)
        edge_val = jax.random.uniform(k3, (N_EDGES,), dtype=jnp.float32)
        edge_row = jax.random.randint(k4, (N_EDGES,), 0, N_NODES, dtype=jnp.int32)
        edge_col = jax.random.randint(k5, (N_EDGES,), 0, N_NODES, dtype=jnp.int32)
        return {'x': x, 'weight': weight, 'edge_val': edge_val, 'edge_row': edge_row, 'edge_col': edge_col}
    _L0_gnn_all = _L0_gnn_setup()
    _L0_gnn_in = {k: v for k, v in _L0_gnn_all.items() if k in ('weight',)}
    del _L0_gnn_all

    def _L0_mix_setup():
        import jax, jax.numpy as jnp
        import numpy as np
        B, N, C = (8, 256, 256)
        HEADS, DH, KR = (8, 32, 4)
        INNER = HEADS * DH
        FF = 4 * C
        EPS = 1e-05

        def layernorm(x, g, b):
            mu = jnp.mean(x, axis=-1, keepdims=True)
            var = jnp.mean((x - mu) ** 2, axis=-1, keepdims=True)
            return (x - mu) * jax.lax.rsqrt(var + EPS) * g + b
        key = jax.random.key(seed)
        ks = jax.random.split(key, 16)
        s = 0.02
        return {'x': jax.random.normal(ks[0], (B, N, C), jnp.float32), 'ln1_g': jnp.ones((C,), jnp.float32), 'ln1_b': jnp.zeros((C,), jnp.float32), 'Wx': jax.random.normal(ks[1], (C, INNER), jnp.float32) * s, 'bx': jnp.zeros((INNER,), jnp.float32), 'Wq': jax.random.normal(ks[2], (DH, KR), jnp.float32) * s, 'Wk': jax.random.normal(ks[3], (DH, KR), jnp.float32) * s, 'Wv': jax.random.normal(ks[4], (DH, DH), jnp.float32) * s, 'Wo': jax.random.normal(ks[5], (INNER, C), jnp.float32) * s, 'bo': jnp.zeros((C,), jnp.float32), 'ln2_g': jnp.ones((C,), jnp.float32), 'ln2_b': jnp.zeros((C,), jnp.float32), 'W1': jax.random.normal(ks[6], (C, FF), jnp.float32) * s, 'b1': jnp.zeros((FF,), jnp.float32), 'W2': jax.random.normal(ks[7], (FF, C), jnp.float32) * s, 'b2': jnp.zeros((C,), jnp.float32)}
    _L0_mix_all = _L0_mix_setup()
    _L0_mix_in = {k: v for k, v in _L0_mix_all.items() if k in ('ln1_g', 'ln1_b', 'Wx', 'bx', 'Wq', 'Wk', 'Wv', 'Wo', 'bo', 'ln2_g', 'ln2_b', 'W1', 'b1', 'W2', 'b2')}
    del _L0_mix_all

    def _L0_ffn_setup():
        import jax, jax.numpy as jnp
        import numpy as np
        N_EXPERTS = 8
        TOP_K = 2
        key = jax.random.key(seed)
        ks = jax.random.split(key, 5)
        B, T, C, E, H = (8, 64, 256, 8, 682)
        scale = 1.0 / np.sqrt(C)
        return {'x': jax.random.normal(ks[0], (B, T, C), dtype=jnp.float32), 'router_w': jax.random.normal(ks[1], (E, C), dtype=jnp.float32) * scale, 'w1': jax.random.normal(ks[2], (E, H, C), dtype=jnp.float32) * scale, 'w2': jax.random.normal(ks[3], (E, C, H), dtype=jnp.float32) * (1.0 / np.sqrt(H)), 'w3': jax.random.normal(ks[4], (E, H, C), dtype=jnp.float32) * scale}
    _L0_ffn_all = _L0_ffn_setup()
    _L0_ffn_in = {k: v for k, v in _L0_ffn_all.items() if k in ('router_w', 'w1', 'w2', 'w3')}
    del _L0_ffn_all
    return {'x': x, 'src': src, 'dst': dst, 'edge_weight': edge_weight, 'L0_gnn_weight': _L0_gnn_in['weight'], 'L0_mix_ln1_g': _L0_mix_in['ln1_g'], 'L0_mix_ln1_b': _L0_mix_in['ln1_b'], 'L0_mix_Wx': _L0_mix_in['Wx'], 'L0_mix_bx': _L0_mix_in['bx'], 'L0_mix_Wq': _L0_mix_in['Wq'], 'L0_mix_Wk': _L0_mix_in['Wk'], 'L0_mix_Wv': _L0_mix_in['Wv'], 'L0_mix_Wo': _L0_mix_in['Wo'], 'L0_mix_bo': _L0_mix_in['bo'], 'L0_mix_ln2_g': _L0_mix_in['ln2_g'], 'L0_mix_ln2_b': _L0_mix_in['ln2_b'], 'L0_mix_W1': _L0_mix_in['W1'], 'L0_mix_b1': _L0_mix_in['b1'], 'L0_mix_W2': _L0_mix_in['W2'], 'L0_mix_b2': _L0_mix_in['b2'], 'L0_ffn_router_w': _L0_ffn_in['router_w'], 'L0_ffn_w1': _L0_ffn_in['w1'], 'L0_ffn_w2': _L0_ffn_in['w2'], 'L0_ffn_w3': _L0_ffn_in['w3']}

def reference(x, src, dst, edge_weight, L0_gnn_weight, L0_mix_ln1_g, L0_mix_ln1_b, L0_mix_Wx, L0_mix_bx, L0_mix_Wq, L0_mix_Wk, L0_mix_Wv, L0_mix_Wo, L0_mix_bo, L0_mix_ln2_g, L0_mix_ln2_b, L0_mix_W1, L0_mix_b1, L0_mix_W2, L0_mix_b2, L0_ffn_router_w, L0_ffn_w1, L0_ffn_w2, L0_ffn_w3):
    import jax
    import jax.numpy as jnp

    def _L0_gnn_ref(x, weight, edge_val, edge_row, edge_col):
        import jax, jax.numpy as jnp
        import numpy as np
        N_NODES = 3125
        N_EDGES = 100000
        D_IN = 256
        D_OUT = 256
        support = x @ weight
        msgs = support[edge_col] * edge_val[:, None]
        out = jax.ops.segment_sum(msgs, edge_row, num_segments=N_NODES)
        return jax.nn.relu(out)

    def _L0_mix_ref(x, ln1_g, ln1_b, Wx, bx, Wq, Wk, Wv, Wo, bo, ln2_g, ln2_b, W1, b1, W2, b2):
        import jax, jax.numpy as jnp
        import numpy as np
        B, N, C = (8, 256, 256)
        HEADS, DH, KR = (8, 32, 4)
        INNER = HEADS * DH
        FF = 4 * C
        EPS = 1e-05

        def layernorm(x, g, b):
            mu = jnp.mean(x, axis=-1, keepdims=True)
            var = jnp.mean((x - mu) ** 2, axis=-1, keepdims=True)
            return (x - mu) * jax.lax.rsqrt(var + EPS) * g + b
        b, n, c = x.shape
        h = layernorm(x, ln1_g, ln1_b)
        xm = h @ Wx + bx
        xm = xm.reshape(b, n, HEADS, DH).transpose(0, 2, 1, 3)
        q = jax.nn.softmax(xm @ Wq, axis=-1)
        k = jax.nn.softmax(xm @ Wk, axis=-2)
        v = xm @ Wv
        kv = jnp.einsum('bhnr,bhnd->bhrd', k, v)
        qkv = jnp.einsum('bhnr,bhrd->bhnd', q, kv)
        attn = qkv.transpose(0, 2, 1, 3).reshape(b, n, INNER) @ Wo + bo
        fx = attn + x
        h2 = layernorm(fx, ln2_g, ln2_b)
        m = jax.nn.gelu(h2 @ W1 + b1, approximate=False) @ W2 + b2
        return m + fx

    def _L0_ffn_ref(x, router_w, w1, w2, w3):
        import jax, jax.numpy as jnp
        import numpy as np
        N_EXPERTS = 8
        TOP_K = 2
        B, T, C = x.shape
        flat = x.reshape(-1, C)
        logits = flat @ router_w.T
        probs = jax.nn.softmax(logits, axis=-1)
        topk_probs, topk_idx = jax.lax.top_k(probs, TOP_K)
        topk_probs = topk_probs / (jnp.sum(topk_probs, axis=-1, keepdims=True) + 1e-09)
        onehot = jax.nn.one_hot(topk_idx, N_EXPERTS, dtype=flat.dtype)
        gates = jnp.einsum('nk,nke->ne', topk_probs, onehot)
        h1 = jnp.einsum('nc,ehc->neh', flat, w1)
        h3 = jnp.einsum('nc,ehc->neh', flat, w3)
        h = jax.nn.silu(h1) * h3
        y = jnp.einsum('neh,ech->nec', h, w2)
        out = jnp.einsum('ne,nec->nc', gates, y)
        return out.reshape(B, T, C)
    xn = _layernorm(x, axis=-1)
    x = x + _L0_gnn_ref(xn, L0_gnn_weight, edge_weight, src, dst) + _L0_mix_ref(xn[None], L0_mix_ln1_g, L0_mix_ln1_b, L0_mix_Wx, L0_mix_bx, L0_mix_Wq, L0_mix_Wk, L0_mix_Wv, L0_mix_Wo, L0_mix_bo, L0_mix_ln2_g, L0_mix_ln2_b, L0_mix_W1, L0_mix_b1, L0_mix_W2, L0_mix_b2)[0]
    x = x + _L0_ffn_ref(_layernorm(x, axis=-1)[None], L0_ffn_router_w, L0_ffn_w1, L0_ffn_w2, L0_ffn_w3)[0]
    return x

_drawn_inputs = setup_inputs


def setup_inputs(seed=0):
    import zlib

    import numpy as np

    out = dict(_drawn_inputs(seed))
    spreads = {'L0_mix_ln1_g': (1.0, 0.6),
     'L0_mix_ln1_b': (0.0, 0.8),
     'L0_mix_bx': (0.0, 0.8),
     'L0_mix_bo': (0.0, 0.603),
     'L0_mix_ln2_g': (1.0, 0.6),
     'L0_mix_ln2_b': (0.0, 2.0),
     'L0_mix_b1': (0.0, 1.421),
     'L0_mix_b2': (0.0, 0.578)}
    factors = {'L0_mix_Wx': 8.0, 'L0_mix_Wq': 8.0, 'L0_mix_Wk': 8.0, 'L0_mix_Wv': 8.0, 'L0_mix_Wo': 8.0}
    for name, (base, spread) in spreads.items():
        noise = np.random.default_rng([zlib.crc32(name.encode()), seed]).standard_normal(out[name].shape)
        drawn = base * np.exp(spread * noise) if base else spread * noise
        out[name] = jnp.asarray(drawn.astype(out[name].dtype))
    for name, factor in factors.items():
        out[name] = (out[name] * factor).astype(out[name].dtype)
    return out
```

```python
import concourse.bass as bass
from concourse import mybir
from contextlib import ExitStack

P = 128
NODES, C, EDGES = 3125, 256, 50000
KC = C // P
TT = -(-NODES // P)
TOKENS = TT * P
LAST = NODES - (TT - 1) * P
EC = 392
HEADS, DH, KR = 8, 32, 4
HR = HEADS * KR
QKV = C + 2 * HR
FF = 4 * C
FT = FF // P
EXPERTS, H = 8, 682
HB = 114
NHB = 6
HH = HB * NHB // 2
W13 = 4 * HH
EPS = 1e-5
RECORD = 3
EDGE_SLOTS = (P * EC + TT * (P - 1)) // P
PICKS = 2 * TT
MOE_SLOTS = (P * PICKS + EXPERTS * (P - 1)) // P
HS = 28
HALF = 8
NEG = -1.0e30


def gps_layer(nc, x, src, dst, edge_w, w_gnn, wx_t, w_qkv, ln1_g, ln1_b, bx, w_o, b_o, ln2_g, ln2_b,
              w_1, b_1, w_2, b_2, router_t, w_13, w_down, out):
    fp32, i32, u32 = mybir.dt.float32, mybir.dt.int32, mybir.dt.uint32
    ALU = mybir.AluOpType
    ACT = mybir.ActivationFunctionType
    X = mybir.AxisListType.X
    ds = bass.ds

    support_d = nc.dram_tensor("support_scratch", (TOKENS, C), fp32).ap()
    records_d = nc.dram_tensor("records_scratch", (P * EDGE_SLOTS, RECORD), i32).ap()
    routed_d = nc.dram_tensor("routed_scratch", (MOE_SLOTS * P, C), fp32).ap()
    expert_d = nc.dram_tensor("expert_out_scratch", (MOE_SLOTS * P, C), fp32).ap()

    ctx = ExitStack()
    with ctx:
        def sb(name, shape, dt=fp32):
            return ctx.enter_context(nc.sbuf_tensor(name, shape, dt))

        def sem(name):
            return ctx.enter_context(nc.semaphore(name))

        XA = sb("XA", [P, 2 * TT * C])
        M = sb("M", [P, TT * C])
        R1 = sb("R1", [P, EXPERTS * KC * W13])
        xs = XA[:, 0:TT * C]
        acc = XA[:, TT * C:2 * TT * C]
        qkv = R1[:, 0:TT * QKV].rearrange("p (t c) -> p t c", c=QKV)
        z2T = R1[:, TT * QKV:TT * QKV + KC * TOKENS].rearrange("p (k n) -> p k n", k=KC)
        CH = 5
        CN = CH * P // 2
        hid0 = TT * QKV + KC * TOKENS
        hidT = R1[:, hid0:hid0 + FT * CH * P].rearrange("p (f n) -> p f n", f=FT)
        gathered = XA[:, 0:2 * HALF * C].rearrange("p (s c) -> p s c", c=C)
        S = XA[:, 2 * HALF * C:2 * HALF * C + 2 * HALF * P].rearrange("p (s c) -> p s c", c=P)
        sup_all = R1[:, TT * QKV:TT * QKV + TT * C]
        oh_e = R1[:, 0:2 * TT * EC]
        cum_e = R1[:, TT * EC:2 * TT * EC]
        dst_in = M[:, 0:EC].bitcast(i32)
        weight_in = M[:, EC:2 * EC]
        src_part = M[:, 2 * EC:3 * EC].bitcast(i32)
        key_e = M[:, 3 * EC:4 * EC]
        token_rings = R1[:, hid0:hid0 + FT * CH * P]
        xn_ring = token_rings[:, 0:512].rearrange("p (s c) -> p s c", s=2)
        z_ring = token_rings[:, 512:1024].rearrange("p (s c) -> p s c", s=2)
        tr_ring = token_rings[:, 1024:2048].rearrange("p (s q c) -> p s q c", s=2, c=P)
        q_ring = token_rings[:, 4096:4096 + 2 * P].rearrange("p (s c) -> p s c", s=2)
        qT_ring = token_rings[0:HR + 1, 2200:2456].rearrange("p (s c) -> p s c", s=2)
        wraw = token_rings[:, 2456:2456 + KC * QKV].rearrange("p (k n) -> p k n", k=KC)
        wfold = token_rings[:, 3096:3096 + KC * QKV].rearrange("p (k n) -> p k n", k=KC)
        bqkv = token_rings[:, 3736:3736 + QKV]
        tail = R1[:, 2 * TT * EC:]
        wxt = tail[:, 0:KC * C].rearrange("p (k n) -> p k n", k=KC)
        wqkv = tail[:, 512:512 + KC * QKV].rearrange("p (k n) -> p k n", k=KC)
        vbc = tail[:, 1152:1664].rearrange("p (v k c) -> p v k c", v=2, k=KC)
        wo = tail[:, 1664:2176].rearrange("p (k n) -> p k n", k=KC)

        ident = sb("ident", [P, P])
        upper = sb("upper", [P, P])
        ones = sb("ones", [P, P])
        iota_r = sb("iota_r", [P, EDGE_SLOTS])
        padneg = sb("padneg", [P, 1])
        kvmask = sb("kvmask", [P, KC, HEADS, KR])
        wg = sb("wg", [P, KC, C])
        vecs = sb("vecs", [P, 5, KC])
        kvT = sb("kvT", [P, KC, HR])
        attn_w = sb("attn_w", [HR + 1, C])
        WM = sb("WM", [P, KC * FF + FT * C])
        w1 = WM[:, 0:KC * FF].rearrange("p (k n) -> p k n", k=KC)
        w2 = WM[:, KC * FF:].rearrange("p (f n) -> p f n", f=FT)
        b1 = sb("b1", [P, FT])
        b2 = sb("b2", [P, C])
        rt = sb("rt", [P, KC, EXPERTS])
        rec = sb("rec", [P, EC, RECORD], i32)
        row_e = sb("row_e", [P, EC], i32)
        tab = sb("tab", [P, (EDGE_SLOTS + HALF) * RECORD], i32)
        stage_i = sb("stage_i", [P, 2, HS], i32)
        stage_r = sb("stage_r", [P, 2, HS, RECORD], i32)
        edge_owner = sb("edge_owner", [1, EDGE_SLOTS], i32)
        slot_expert = sb("slot_expert", [1, MOE_SLOTS], i32)
        stats = sb("stats", [P, TT, 6])
        ln = sb("ln", [P, 8, TT])
        mean, var, rstd, t0, t1, root = (ln[:, i, :] for i in range(6))
        small = sb("small", [P, 8, TT])
        probs = sb("probs", [P, TT, EXPERTS])
        pick = sb("pick", [P, 2, TT, EXPERTS])
        keys_m = sb("keys_m", [P, PICKS])
        row_m = sb("row_m", [P, PICKS], i32)
        gates = sb("gates", [P, 2, TT])
        q_red = sb("q_red", [P, TT, HEADS])
        kmax = sb("kmax", [P, HR])
        kmax_t = sb("kmax_t", [HR, 1])
        diag = sb("diag", [HR, HR])
        kden = sb("kden", [P, HR])
        x2_ring = WM[:, 0:512].rearrange("p (s c) -> p s c", s=2)
        x2T_ring = WM[:, 512:1024].rearrange("p (s k c) -> p s k c", s=2, k=KC)
        oh_m = WM[:, 1024:1024 + MOE_SLOTS * EXPERTS]
        cum_m = WM[:, 1600:1600 + EXPERTS * PICKS]
        ex_ring = WM[:, 0:512].rearrange("p (s c) -> p s c", s=2)
        exT_ring = WM[:, 512:1024].rearrange("p (s k c) -> p s k c", s=2, k=KC)
        h_ring = WM[:, 1024:1024 + 2 * HH].rearrange("p (a c) -> p a c", a=2)
        g_ring = WM[:, 1712:1712 + 2 * HH].rearrange("p (a c) -> p a c", a=2)
        hT_ring = WM[0:HB, 2400:2400 + NHB * P].rearrange("p (f c) -> p f c", f=NHB)
        y_ring = WM[:, 3200:3712].rearrange("p (s c) -> p s c", s=2)
        picked = R1[:, 0:2 * 10 * C].rearrange("p (s c) -> p s c", c=C)
        o_ring = R1[:, 20 * C:30 * C].rearrange("p (s c) -> p s c", c=C)

        B = [ctx.enter_context(nc.psum_tensor(f"bank{i}", [P, 512], fp32)) for i in range(8)]

        edges_in, x_in, weights_in, constants, acc_zeroed, records_zeroed = (
            sem(n) for n in "edges_in x_in weights_in constants acc_zeroed records_zeroed".split())
        routed_zeroed, rank_counts, rank_sums, edge_rows, staged, records_in = (
            sem(n) for n in "routed_zeroed rank_counts rank_sums edge_rows staged records_in".split())
        support_stored, gather_staged, edge_onehots, edge_products, acc_added, vector_step = (
            sem(n) for n in "support_stored gather_staged edge_onehots edge_products acc_added vector_step".split())
        x_stats, var_ready, root_ready, xn_ready, xn_copied, z_ready = (
            sem(n) for n in "x_stats var_ready root_ready xn_ready xn_copied z_ready".split())
        transposed, transposes_copied, token_products, support_ready, qkv_ready, x_plus_b2 = (
            sem(n) for n in "transposed transposes_copied token_products support_ready qkv_ready x_plus_b2".split())
        fold_products, fold_inputs, bias_product, folded, kmax_ready, kmax_transposed = (
            sem(n) for n in "fold_products fold_inputs bias_product folded kmax_ready kmax_transposed".split())
        kmax_diagonal, kmax_spread, exp_input, exp_done, kv_product, kv_ready = (
            sem(n) for n in "kmax_diagonal kmax_spread exp_input exp_done kv_product kv_ready".split())
        attn_product, attn_weights, q_ready, q_transposed, q_copied, attn_rows = (
            sem(n) for n in "attn_product attn_weights q_ready q_transposed q_copied attn_rows".split())
        residual_ready, z2_ready, z2_transposed, z2_copied, mix_residual, b1_product = (
            sem(n) for n in "residual_ready z2_ready z2_transposed z2_copied mix_residual b1_product".split())
        mlp_weights, up_product, gelu_done, down_product, down_added, x1_ready = (
            sem(n) for n in "mlp_weights up_product gelu_done down_product down_added x1_ready".split())
        xn2_ready, xn2_copied, xn2_transposed, xn2_transposes_copied, router_product, logits_copied = (
            sem(n) for n in "xn2_ready xn2_copied xn2_transposed xn2_transposes_copied router_product logits_copied".split())
        pick_rows, rows_routed, experts_up_in, experts_down_in, slot_transposed, slot_copied = (
            sem(n) for n in "pick_rows rows_routed experts_up_in experts_down_in slot_transposed slot_copied".split())
        half0_product, half1_product, half0_silu, half1_silu, half0_gated, half1_gated = (
            sem(n) for n in "half0_product half1_product half0_silu half1_silu half0_gated half1_gated".split())
        half0_transposed, half1_transposed, half0_copied, half1_copied, down_rows, down_copied = (
            sem(n) for n in "half0_transposed half1_transposed half0_copied half1_copied down_rows down_copied".split())
        out_rows = sem("out_rows")
        stages_seen = sem("stages_seen")
        records_scattered = [sem(f"records_scattered{h}") for h in range(2)]
        rows_gathered = [sem(f"rows_gathered{h}") for h in range(2)]
        slot_rows_in = [sem(f"slot_rows_in{h}") for h in range(2)]
        expert_rows_stored = [sem(f"expert_rows_stored{h}") for h in range(2)]
        picks_gathered = [sem(f"picks_gathered{h}") for h in range(2)]
        out_stored = [sem(f"out_stored{h}") for h in range(2)]

        def pairs(engine, body, n=TT):
            with engine.Fori(0, n // 2) as i:
                body(2 * i, 0)
                body(2 * i + 1, 1)
            if n % 2:
                body(n - 1, 0)

        def staggered(engine, ahead, behind, first=None):
            def both(t, s):
                steps = (lambda: ahead(t + 2, s)), (lambda: behind(t, s))
                for run in steps if first is ahead else steps[::-1]:
                    run()

            ahead(0, 0)
            ahead(1, 1)
            with engine.Fori(0, (TT - 3) // 2) as i:
                for s in range(2):
                    both(2 * i + s, s)
            both(TT - 3, 0)
            behind(TT - 2, 1)
            behind(TT - 1, 0)

        block = ctx.enter_context(nc.Block())

        @block.sync
        def _(sp):
            for dram, part in ((src, row_e[:, :]), (dst, dst_in), (edge_w, weight_in)):
                sp.dma_start(part, dram).then_inc(edges_in, 16)
            x_v = x.rearrange("(t p) c -> p t c", p=P)
            sp.dma_start(xs.rearrange("p (t c) -> p t c", c=C), x_v).then_inc(x_in, 16)
            kp = lambda w: w.rearrange("(k p) n -> p k n", p=P)
            for dram, part in ((kp(wx_t), wxt[:, :, :]), (kp(w_qkv), wqkv[:, :, :]), (ln1_g, vecs[:, 0, :]),
                               (ln1_b, vecs[:, 1, :]), (bx, vecs[:, 2, :]), (ln2_g, vecs[:, 3, :]),
                               (ln2_b, vecs[:, 4, :]), (kp(w_gnn), wg[:, :, :]), (kp(w_o), wo[:, :, :]),
                               (b_o, attn_w[HR:HR + 1, :]), (kp(w_1), w1[:, :, :]), (b_1, b1[:, :]),
                               (kp(w_2), w2[:, :, :]), (b_2.partition_broadcast(P), b2[:, :]),
                               (kp(router_t), rt[:, :, :])):
                sp.dma_start(part, dram).then_inc(weights_in, 16)
            sp.wait_ge(acc_zeroed, 1)
            sp.dma_start(records_d.rearrange("(p j) w -> p (j w)", p=P),
                         acc[:, 0:EDGE_SLOTS * RECORD].bitcast(i32)).then_inc(records_zeroed, 16)
            for j in range(0, MOE_SLOTS, TT):
                n = min(TT, MOE_SLOTS - j)
                sp.dma_start(routed_d[j * P:(j + n) * P, :].rearrange("(p r) c -> p (r c)", p=P),
                             acc[:, 0:n * C]).then_inc(routed_zeroed, 16)

            sp.wait_ge(support_ready, TT + 2)
            sp.dma_start(support_d.rearrange("(t p) c -> p t c", p=P),
                         sup_all.rearrange("p (t c) -> p t c", c=C)).then_inc(support_stored, 16)
            sp.wait_ge(records_scattered[0], 16 * (EC // 2))
            sp.wait_ge(records_scattered[1], 16 * (EC // 2))
            sp.dma_start(tab[:, 0:EDGE_SLOTS * RECORD],
                         records_d.rearrange("(p j) w -> p (j w)", p=P)).then_inc(records_in, 16)
            sp.wait_ge(down_added, 4 + TT)
            for e in range(EXPERTS):
                sp.dma_start(R1[:, e * KC * W13:(e + 1) * KC * W13], w_13[:, e, :]).then_inc(experts_up_in, 16)
            half_w2 = EXPERTS // 2 * NHB * C
            sp.wait_ge(acc_added, EDGE_SLOTS + HALF)
            sp.dma_start(XA[0:HB, 0:TT * C], w_down[:, 0:TT * C]).then_inc(experts_down_in, 16)
            sp.wait_ge(rows_routed, 16 * PICKS)
            sp.dma_start(XA[0:HB, TT * C:2 * half_w2], w_down[:, TT * C:2 * half_w2]).then_inc(experts_down_in, 16)

            def load_slot(j, s):
                sp.dma_start(ex_ring[:, s, :], routed_d[ds(j * P, P), :]).then_inc(slot_rows_in[s], 16)

            load_slot(0, 0)
            load_slot(1, 1)

            def next_slot(j, s):
                sp.wait_ge(slot_transposed, j + 1)
                load_slot(j + 2, s)

            pairs(sp, next_slot, MOE_SLOTS - 2)

            with sp.Fori(0, 2) as i:
                for s in range(2):
                    sp.wait_ge(out_rows, 2 * i + s + 1)
                    sp.dma_start(out[ds((2 * i + s) * 5 * P, 5 * P), :].rearrange("(t p) c -> p t c", p=P),
                                 o_ring[:, 5 * s:5 * s + 5, :]).then_inc(out_stored[s], 16)
            sp.wait_ge(out_rows, 5)
            sp.dma_start(out[20 * P:24 * P, :].rearrange("(t p) c -> p t c", p=P),
                         o_ring[:, 0:4, :]).then_inc(out_stored[0], 16)
            sp.dma_start(out[24 * P:NODES, :], o_ring[0:LAST, 4, :]).then_inc(out_stored[0], 16)
            sp.wait_ge(out_stored[0], 64)
            sp.wait_ge(out_stored[1], 32)

        @block.gpsimd
        def _(pool):
            pool.memset(acc, 0.0).then_inc(acc_zeroed, 1)
            pool.memset(tab[:, EDGE_SLOTS * RECORD:], 0).then_inc(constants, 1)
            pool.memset(ident[:, :], 0.0).then_inc(constants, 1)
            pool.memset(ones[:, :], 1.0).then_inc(constants, 1)
            pool.memset(padneg[:, :], 0.0).then_inc(constants, 1)
            pool.memset(kvmask[:, :, :, :], 1.0).then_inc(constants, 1)
            pool.iota(iota_r[:, :], pattern=[[1, EDGE_SLOTS]], base=0, channel_multiplier=0,
                      allow_small_or_imprecise_dtypes=True).then_inc(constants, 1)
            pool.wait_ge(constants, 6)
            pool.affine_select(out=ident[:, :], in_=ident[:, :], compare_op=ALU.not_equal, fill=1.0, base=0,
                               pattern=[[-1, P]], channel_multiplier=1).then_inc(constants, 1)
            pool.affine_select(out=upper[:, :], in_=ones[:, :], compare_op=ALU.is_gt, fill=0.0, base=0,
                               pattern=[[1, P]], channel_multiplier=-1).then_inc(constants, 1)
            pool.affine_select(out=padneg[:, :], in_=padneg[:, :], compare_op=ALU.is_ge, fill=NEG,
                               base=LAST - 1, pattern=[[0, 1]], channel_multiplier=-1).then_inc(constants, 1)
            pool.affine_select(out=kvmask[:, :, :, :], in_=kvmask[:, :, :, :], compare_op=ALU.is_ge, fill=0.0,
                               base=0, pattern=[[P, KC], [-DH, HEADS], [0, KR]],
                               channel_multiplier=1).then_inc(constants, 1)
            pool.wait_ge(constants, 10)
            pool.affine_select(out=kvmask[:, :, :, :], in_=kvmask[:, :, :, :], compare_op=ALU.is_ge, fill=0.0,
                               base=DH - 1, pattern=[[-P, KC], [DH, HEADS], [0, KR]],
                               channel_multiplier=-1).then_inc(constants, 1)

            pool.wait_ge(edge_rows, 1)
            pool.wait_ge(records_zeroed, 16)


            def scatter(i, h, first):
                col = (2 * i + h) * HS
                if not first:
                    pool.wait_ge(records_scattered[h], 16 * HS * i)
                pool.tensor_copy(stage_i[:, h, 0:HS], row_e[:, ds(col, HS)]).then_inc(staged, 1)
                pool.tensor_copy(stage_r[:, h, 0:HS, :], rec[:, ds(col, HS), :]).then_inc(staged, 1)
                pool.wait_ge(staged, 4 * i + 2 * h + 2)
                pool.sem_inc(stages_seen, 1)
                for k in range(HS):
                    pool.indirect_dma_start(
                        records_d, bass.IndirectOffsetOnAxis(ap=stage_i[:, h, k:k + 1].bitcast(u32), axis=0),
                        stage_r[:, h, k, :], None).then_inc(records_scattered[h], 16)

            for h in range(2):
                scatter(0, h, True)
            with pool.Fori(1, EC // (2 * HS)) as i:
                for h in range(2):
                    scatter(i, h, False)

            pool.wait_ge(records_in, 16)
            pool.wait_ge(support_stored, 16)
            pool.wait_ge(mix_residual, 1)
            tab3 = tab[:, :].rearrange("p (j w) -> p j w", w=RECORD)

            def gather(i, h, first):
                col = (2 * i + h) * HALF
                if not first:
                    pool.wait_ge(edge_products, HALF * (2 * i + h - 1))
                    pool.wait_ge(rows_gathered[h], 16 * HALF * i)
                pool.tensor_copy(stage_i[:, h, 0:HALF], tab3[:, ds(col, HALF), 0]).then_inc(gather_staged, 1)
                pool.wait_ge(gather_staged, 2 * i + h + 1)
                pool.sem_inc(stages_seen, 1)
                for k in range(HALF):
                    pool.indirect_dma_start(
                        gathered[:, h * HALF + k, :], None, support_d,
                        bass.IndirectOffsetOnAxis(ap=stage_i[:, h, k:k + 1].bitcast(u32), axis=0),
                    ).then_inc(rows_gathered[h], 16)

            for h in range(2):
                gather(0, h, True)
            with pool.Fori(1, EDGE_SLOTS // (2 * HALF)) as i:
                for h in range(2):
                    gather(i, h, False)

            pool.wait_ge(routed_zeroed, 16 * -(-MOE_SLOTS // TT))
            pool.wait_ge(xn2_ready, TT)
            pool.wait_ge(pick_rows, 1)
            for k in range(PICKS):
                t = k % TT
                pool.indirect_dma_start(
                    routed_d, bass.IndirectOffsetOnAxis(ap=row_m[:, k:k + 1].bitcast(u32), axis=0),
                    acc[:, t * C:(t + 1) * C], None).then_inc(rows_routed, 16)

            def store_rows(j, s):
                pool.wait_ge(down_copied, j + 2)
                pool.dma_start(expert_d[ds(j * P, P), :], y_ring[:, s, :]).then_inc(expert_rows_stored[s], 16)

            pairs(pool, store_rows, MOE_SLOTS)

            pool.wait_ge(expert_rows_stored[0], 16 * ((MOE_SLOTS + 1) // 2))
            pool.wait_ge(expert_rows_stored[1], 16 * (MOE_SLOTS // 2))
            for n in range(TT // 5):
                h = n % 2
                if n >= 2:
                    pool.wait_ge(out_rows, n - 1)
                for r in range(5):
                    for k in range(2):
                        col = k * TT + n * 5 + r
                        pool.indirect_dma_start(
                            picked[:, h * 10 + 2 * r + k, :], None, expert_d,
                            bass.IndirectOffsetOnAxis(ap=row_m[:, col:col + 1].bitcast(u32), axis=0),
                        ).then_inc(picks_gathered[h], 16)

        @block.vector
        def _(dve):
            step = [0]

            def link(ins):
                step[0] += 1
                ins.then_inc(vector_step, 1)
                dve.wait_ge(vector_step, step[0])

            ranks = [0]

            def rank(keys, K, T, slots, area, cum, row, swizzle, owner, scale):
                n = ranks[0]
                ranks[0] += 1
                cnt, tot, tiles, tinc, d, tmp = (small[:, i, 0:K] for i in range(6))
                oh = area[:, 0:K * T]
                ohv = oh.rearrange("p (k t) -> p k t", t=T)
                cumv = cum.rearrange("p (k t) -> p k t", t=T)
                kb = iota_r[:, 0:K].unsqueeze(2).to_broadcast([P, K, T])
                link(nc.vector.tensor_tensor(ohv, keys.unsqueeze(1).to_broadcast([P, K, T]), kb, ALU.is_equal))
                link(nc.vector.tensor_tensor_scan(cum, oh, oh, 0.0, ALU.add, ALU.max))
                ends = cumv[:, :, T - 1]
                link(nc.vector.tensor_copy(cnt, ends))
                link(nc.vector.tensor_tensor(tmp[:, 1:K], cnt[:, 1:K], cnt[:, 0:K - 1], ALU.subtract))
                link(nc.vector.tensor_copy(tmp[:, 0:1], cnt[:, 0:1]))
                link(nc.vector.tensor_tensor(d, cnt, tmp, ALU.subtract))
                nc.vector.tensor_copy(cnt, tmp).then_inc(rank_counts, 1)
                dve.wait_ge(rank_sums, n + 1)
                link(nc.vector.scalar_tensor_tensor(d, B[7][:, 0:K], -1.0, d, ALU.add, ALU.subtract))
                ti = tot.bitcast(i32)
                link(nc.vector.tensor_scalar(ti, B[7][:, K:2 * K], float(P - 1), None, ALU.add))
                link(nc.vector.tensor_scalar(ti, ti, 7, None, ALU.arith_shift_right))
                link(nc.vector.tensor_copy(tiles, ti))
                link(nc.vector.tensor_tensor_scan(tinc, tiles, tiles, 0.0, ALU.add, ALU.max))
                link(nc.vector.tensor_tensor(tmp, tinc, tiles, ALU.subtract))
                link(nc.vector.scalar_tensor_tensor(d, tmp, float(P), d, ALU.mult, ALU.add))
                link(nc.vector.tensor_tensor(cumv, cumv, d.unsqueeze(2).to_broadcast([P, K, T]), ALU.add))
                link(nc.vector.tensor_tensor(cum, cum, oh, ALU.mult))
                link(nc.vector.tensor_reduce(row.bitcast(fp32), cumv.rearrange("p k t -> p t k"), X, ALU.add))
                link(nc.vector.tensor_copy(row, row.bitcast(fp32)))
                if swizzle:
                    lo = oh[:, 0:T].bitcast(i32)
                    hi = oh[:, T:2 * T].bitcast(i32)
                    link(nc.vector.tensor_scalar(lo, row, P - 1, None, ALU.bitwise_and))
                    link(nc.vector.tensor_scalar(hi, row, 7, None, ALU.arith_shift_right))
                    link(nc.vector.scalar_tensor_tensor(row, lo, float(slots), hi, ALU.mult, ALU.add))
                yield
                own = area[0:1, 0:slots * K].rearrange("p (j k) -> p j k", k=K)
                link(nc.vector.tensor_tensor(own, iota_r[0:1, 0:slots].unsqueeze(2).to_broadcast([1, slots, K]),
                                             tinc[0:1, :].unsqueeze(1).to_broadcast([1, slots, K]), ALU.is_ge))
                own_f = cum[0:1, K * T - slots:K * T]
                link(nc.vector.tensor_reduce(own_f, own, X, ALU.add))
                link(nc.vector.tensor_scalar(owner, own_f, float(K - 1), float(scale), ALU.min, ALU.mult))

            lns = [0]

            def norm_columns():
                me, ve, mo, vo = (stats[:, :, i] for i in (1, 2, 4, 5))
                link(nc.vector.tensor_tensor(t0, me, mo, ALU.add))
                link(nc.vector.tensor_scalar(mean, t0, 0.5, None, ALU.mult))
                link(nc.vector.tensor_tensor(t1, me, mo, ALU.subtract))
                link(nc.vector.scalar_tensor_tensor(t1, t1, 0.25, t1, ALU.mult, ALU.mult))
                link(nc.vector.tensor_tensor(t0, ve, vo, ALU.add))
                link(nc.vector.scalar_tensor_tensor(t0, t0, 1.0 / C, t1, ALU.mult, ALU.add))
                nc.vector.tensor_scalar(var, t0, EPS, None, ALU.add).then_inc(var_ready, 1)
                lns[0] += 1
                dve.wait_ge(root_ready, lns[0])
                link(nc.vector.reciprocal(t0, root))
                link(nc.vector.tensor_tensor(t1, t0, t0, ALU.mult))
                link(nc.vector.scalar_tensor_tensor(t1, var, -0.5, t1, ALU.mult, ALU.mult))
                link(nc.vector.scalar_tensor_tensor(rstd, t1, 1.5, t0, ALU.add, ALU.mult))

            def normalise(o, i, t):
                return nc.vector.tensor_scalar(o, i, mean[:, ds(t, 1)], rstd[:, ds(t, 1)], ALU.subtract, ALU.mult)

            def tile_of(a, t):
                return a[:, ds(t * C, C)]

            dve.wait_ge(edges_in, 48)
            dve.wait_ge(constants, 11)
            link(nc.vector.tensor_scalar(src_part, row_e[:, :], P - 1, None, ALU.bitwise_and))
            link(nc.vector.tensor_copy(rec[:, :, 1].bitcast(fp32), src_part))
            link(nc.vector.tensor_scalar(src_part, row_e[:, :], 7, None, ALU.arith_shift_right))
            link(nc.vector.tensor_copy(key_e, src_part))
            link(nc.vector.tensor_copy(rec[:, :, 0], dst_in))
            link(nc.vector.tensor_copy(rec[:, :, 2].bitcast(fp32), weight_in))
            r = rank(key_e, TT, EC, EDGE_SLOTS, oh_e, cum_e, row_e[:, :], True, edge_owner[:, :], C)
            next(r)
            dve.sem_inc(edge_rows, 1)
            for _ in r:
                pass

            dve.wait_ge(weights_in, 16 * 15)
            for v in range(2):
                for k in range(KC):
                    nc.vector.tensor_copy(vbc[:, v, k, :], vecs[:, 1 + v, k:k + 1].to_broadcast([P, P])) \
                        .then_inc(fold_inputs, 1)
            for k in range(KC):
                dve.wait_ge(fold_products, k + 1)
                nc.vector.tensor_copy(wraw[:, k, :], B[k][:, 0:QKV]).then_inc(fold_inputs, 1)
            dve.wait_ge(fold_inputs, 6)
            for k in range(KC):
                link(nc.vector.tensor_scalar(wfold[:, k, :], wraw[:, k, :], vecs[:, 0, k:k + 1], None, ALU.mult))
            dve.wait_ge(bias_product, 1)
            nc.vector.tensor_copy(bqkv[:, :], B[2][:, 0:QKV]).then_inc(folded, 1)
            dve.wait_ge(b1_product, 1)
            link(nc.vector.tensor_tensor(b1[:, :], B[6][:, 0:FT], b1[:, :], ALU.add))
            for k in range(KC):
                link(nc.vector.tensor_scalar(w1[:, k, :], w1[:, k, :], vecs[:, 3, k:k + 1], None, ALU.mult))
            nc.vector.memset(q_ring[:, :, HR:P], 1.0).then_inc(mlp_weights, 1)

            dve.wait_ge(x_in, 16)
            with dve.Fori(0, TT) as t:
                nc.vector.bn_stats(stats[:, ds(t, 1), :], tile_of(xs, t)).then_inc(x_stats, 1)
            dve.wait_ge(x_stats, TT)
            norm_columns()
            with dve.Fori(0, TT) as t:
                normalise(tile_of(M, t), tile_of(xs, t), t).then_inc(xn_ready, 1)
                dve.wait_ge(xn_ready, t + 1)
                nc.vector.bn_stats(stats[:, ds(t, 1), :], tile_of(M, t)).then_inc(x_stats, 1)
            dve.wait_ge(x_stats, 2 * TT)
            norm_columns()

            def z_tile(t, s):
                dve.wait_ge(transposed, t + 1)
                normalise(z_ring[:, s, :], tile_of(M, t), t).then_inc(z_ready, 1)

            def products_out(t, s):
                dve.wait_ge(token_products, t + 1)
                nc.vector.tensor_copy(tile_of(sup_all, t), B[2 + s][:, 0:C]).then_inc(support_ready, 1)
                nc.vector.tensor_tensor(qkv[:, ds(t, 1), :], B[4 + s][:, 0:QKV].unsqueeze(1), bqkv.unsqueeze(1),
                                        ALU.add).then_inc(qkv_ready, 1)
                nc.vector.tensor_tensor(tile_of(xs, t), tile_of(xs, t), b2[:, :], ALU.add).then_inc(x_plus_b2, 1)

            dve.wait_ge(folded, 1)
            dve.sem_inc(transposed, 2)
            dve.sem_inc(support_ready, 2)
            dve.sem_inc(qkv_ready, 2)
            staggered(dve, z_tile, products_out, first=z_tile)
            dve.wait_ge(qkv_ready, TT + 2)

            q_v = qkv[:, :, C:C + HR]
            k_v = qkv[:, :, C + HR:QKV]
            link(nc.vector.tensor_scalar(k_v[:, TT - 1, :], k_v[:, TT - 1, :], padneg[:, 0:1], None, ALU.add))
            nc.vector.tensor_reduce(kmax[:, :], k_v.rearrange("p t c -> p c t"), X, ALU.max).then_inc(kmax_ready, 1)
            dve.wait_ge(kmax_transposed, 1)
            link(nc.vector.tensor_reduce(kmax_t[:, :], B[6][0:HR, 0:P], X, ALU.max))
            nc.vector.tensor_scalar(diag[:, :], ident[0:HR, 0:HR], kmax_t[:, 0:1], None, ALU.mult).then_inc(kmax_diagonal, 1)
            q4 = q_v.rearrange("p t (h r) -> p t h r", r=KR)
            link(nc.vector.tensor_reduce(q_red[:, :, :], q4, X, ALU.max))
            nc.vector.tensor_tensor(q4, q4, q_red[:, :, :].unsqueeze(3).to_broadcast([P, TT, HEADS, KR]),
                                    ALU.subtract).then_inc(exp_input, 1)
            dve.wait_ge(kmax_spread, 1)
            nc.vector.tensor_tensor(k_v, k_v, B[7][:, 0:HR].unsqueeze(1).to_broadcast([P, TT, HR]),
                                    ALU.subtract).then_inc(exp_input, 1)
            dve.wait_ge(exp_done, 1)
            link(nc.vector.tensor_reduce(q_red[:, :, :], q4, X, ALU.add))
            link(nc.vector.reciprocal(q_red[:, :, :], q_red[:, :, :]))
            dve.wait_ge(kv_product, 1)
            link(nc.vector.reciprocal(kden[:, :], B[4][:, 0:HR]))
            for k in range(KC):
                link(nc.vector.tensor_tensor(kvT[:, k, :], B[2 + k][:, 0:HR],
                                             kvmask[:, k, :, :].rearrange("p h r -> p (h r)"), ALU.mult))
                nc.vector.tensor_tensor(kvT[:, k, :], kvT[:, k, :], kden[:, :], ALU.mult).then_inc(kv_ready, 1)
            dve.wait_ge(attn_product, 1)
            nc.vector.tensor_copy(attn_w[0:HR, :], B[5][0:HR, 0:C]).then_inc(attn_weights, 1)

            def q_tile(t, s):
                dve.wait_ge(q_transposed, t + 1)
                nc.vector.tensor_tensor(q_ring[:, s, 0:HR].rearrange("p (h r) -> p h r", r=KR),
                                        qkv[:, ds(t, 1), C:C + HR].rearrange("p o (h r) -> p (o h) r", r=KR),
                                        q_red[:, ds(t, 1), :].rearrange("p o h -> p (o h)").unsqueeze(2)
                                        .to_broadcast([P, HEADS, KR]), ALU.mult).then_inc(q_ready, 1)

            def fx_tile(t, s):
                dve.wait_ge(attn_rows, t + 1)
                nc.vector.tensor_tensor(tile_of(M, t), B[2 + s][:, 0:C], tile_of(M, t), ALU.add).then_inc(residual_ready, 1)
                dve.wait_ge(residual_ready, t + 3)
                nc.vector.bn_stats(stats[:, ds(t, 1), :], tile_of(M, t)).then_inc(x_stats, 1)

            dve.sem_inc(q_transposed, 2)
            dve.sem_inc(residual_ready, 2)
            staggered(dve, q_tile, fx_tile, first=q_tile)
            dve.wait_ge(x_stats, 3 * TT)
            norm_columns()

            def z2_tile(t, s):
                dve.wait_ge(z2_transposed, t + 1)
                normalise(z_ring[:, s, :], tile_of(M, t), t).then_inc(z2_ready, 1)

            dve.wait_ge(x_plus_b2, TT)
            dve.sem_inc(z2_transposed, 2)
            pairs(dve, z2_tile)
            dve.wait_ge(z2_ready, TT)
            nc.vector.tensor_tensor(M[:, :], M[:, :], xs, ALU.add).then_inc(mix_residual, 1)
            dve.wait_ge(mix_residual, 1)

            dve.sem_inc(down_added, 4)
            with dve.Fori(0, TT // CH) as c:
                for i in range(CH):
                    dve.wait_ge(down_product, c * CH + i + 1)
                    nc.vector.tensor_tensor(tile_of(M, c * CH + i), B[4 + i % 4][:, 0:C], tile_of(M, c * CH + i),
                                            ALU.add).then_inc(down_added, 1)
            dve.wait_ge(down_added, 4 + TT)

            dve.wait_ge(records_in, 16)

            tabw = tab[:, :].bitcast(fp32)

            def onehots(col, h):
                for k in range(HALF):
                    at = (col + k) * RECORD
                    nc.vector.tensor_scalar(S[:, h * HALF + k, :], iota_r[:, 0:P], tabw[:, ds(at + 1, 1)],
                                            tabw[:, ds(at + 2, 1)], ALU.is_equal, ALU.mult).then_inc(edge_onehots, 1)

            def add_up(col, h):
                _, offsets = nc.values_load_multi_w_load_instructions(
                    edge_owner[0:1, ds(col, HALF)], engines=[mybir.EngineType.DVE], min_val=0, max_val=(TT - 1) * C)
                for k in range(HALF):
                    dve.wait_ge(edge_products, col + k + 1)
                    part = acc[:, ds(offsets[k], C)]
                    nc.vector.tensor_tensor(part, B[k][:, 0:C], part, ALU.add) \
                        .then_inc(acc_added, 1)
                    dve.wait_ge(acc_added, col + k + 1 + HALF)

            dve.wait_ge(routed_zeroed, 16 * -(-MOE_SLOTS // TT))
            dve.wait_ge(records_zeroed, 16)
            dve.sem_inc(acc_added, HALF)
            onehots(0, 0)
            with dve.Fori(0, EDGE_SLOTS // (2 * HALF)) as i:
                onehots(2 * i * HALF + HALF, 1)
                add_up(2 * i * HALF, 0)
                onehots(2 * i * HALF + 2 * HALF, 0)
                add_up(2 * i * HALF + HALF, 1)

            with dve.Fori(0, TT) as t:
                nc.vector.scalar_tensor_tensor(tile_of(M, t), tile_of(acc, t), 0.0, tile_of(M, t), ALU.max, ALU.add) \
                    .then_inc(x1_ready, 1)
                dve.wait_ge(x1_ready, t + 1)
                nc.vector.bn_stats(stats[:, ds(t, 1), :], tile_of(M, t)).then_inc(x_stats, 1)
            dve.wait_ge(x_stats, 4 * TT)
            norm_columns()
            with dve.Fori(0, TT) as t:
                normalise(tile_of(acc, t), tile_of(M, t), t).then_inc(xn2_ready, 1)

            def logits_out(t, s):
                dve.wait_ge(router_product, t + 1)
                nc.vector.tensor_copy(probs[:, ds(t, 1), :], B[2 + s][:, 0:EXPERTS].unsqueeze(1)).then_inc(logits_copied, 1)

            dve.sem_inc(logits_copied, 2)
            pairs(dve, logits_out)
            dve.wait_ge(logits_copied, TT + 2)
            top, total = small[:, 0:2, :], small[:, 2, :]

            def wide(a):
                return a.unsqueeze(2).to_broadcast([P, TT, EXPERTS])

            experts = iota_r[:, 0:EXPERTS].unsqueeze(1).to_broadcast([P, TT, EXPERTS])
            link(nc.vector.tensor_reduce(top[:, 0, :], probs[:, :, :], X, ALU.max))
            nc.vector.tensor_tensor(probs[:, :, :], probs[:, :, :], wide(top[:, 0, :]), ALU.subtract).then_inc(exp_input, 1)
            dve.wait_ge(exp_done, 2)
            link(nc.vector.tensor_reduce(total, probs[:, :, :], X, ALU.add))
            link(nc.vector.reciprocal(total, total))
            link(nc.vector.tensor_tensor(probs[:, :, :], probs[:, :, :], wide(total), ALU.mult))
            for k in range(2):
                key = keys_m[:, k * TT:(k + 1) * TT]
                link(nc.vector.tensor_reduce(top[:, k, :], probs[:, :, :], X, ALU.max))
                link(nc.vector.tensor_tensor(pick[:, 0, :, :], probs[:, :, :], wide(top[:, k, :]), ALU.is_lt))
                link(nc.vector.scalar_tensor_tensor(pick[:, 0, :, :], pick[:, 0, :, :], float(EXPERTS), experts,
                                                    ALU.mult, ALU.add))
                link(nc.vector.tensor_reduce(key, pick[:, 0, :, :], X, ALU.min))
                if k == 0:
                    link(nc.vector.tensor_tensor(pick[:, 1, :, :], experts, wide(key), ALU.is_equal))
                    link(nc.vector.scalar_tensor_tensor(probs[:, :, :], pick[:, 1, :, :], -2.0, probs[:, :, :],
                                                        ALU.mult, ALU.add))
            link(nc.vector.tensor_tensor(total, top[:, 0, :], top[:, 1, :], ALU.add))
            link(nc.vector.tensor_scalar(total, total, 1e-9, None, ALU.add))
            link(nc.vector.reciprocal(total, total))
            for k in range(2):
                link(nc.vector.tensor_tensor(gates[:, k, :], top[:, k, :], total, ALU.mult))
            r = rank(keys_m[:, :], EXPERTS, PICKS, MOE_SLOTS, oh_m, cum_m, row_m[:, :], False, slot_expert[:, :], 1)
            next(r)
            dve.sem_inc(pick_rows, 1)
            for _ in r:
                pass
            dve.sem_inc(pick_rows, 1)

            dve.sem_inc(half1_copied, 1)
            dve.sem_inc(down_copied, 1)

            def gate(j, a):
                dve.wait_ge((half0_silu, half1_silu)[a], j + 1)
                nc.vector.tensor_tensor(h_ring[:, a, :], g_ring[:, a, :], B[2 * a + 1][:, 0:HH], ALU.mult) \
                    .then_inc((half0_gated, half1_gated)[a], 1)

            def expert_rows(j, s, stores, more=True):
                if more:
                    dve.wait_ge(half0_transposed, j + 1)
                    gate(j + 1, 0)
                dve.wait_ge(half1_transposed, j + 1)
                nc.vector.tensor_copy(hT_ring[:, 3:6, :].rearrange("p f c -> p (f c)"), B[5][0:HB, 0:3 * P]) \
                    .then_inc(half1_copied, 1)
                if more:
                    gate(j + 1, 1)
                dve.wait_ge(down_rows, j + 1)
                if stores is not None:
                    dve.wait_ge(expert_rows_stored[s], 16 * stores)
                nc.vector.tensor_copy(y_ring[:, s, :], B[7][:, 0:C]).then_inc(down_copied, 1)

            gate(0, 0)
            gate(0, 1)
            expert_rows(0, 0, None)
            expert_rows(1, 1, None)
            with dve.Fori(1, MOE_SLOTS // 2) as i:
                for s in range(2):
                    expert_rows(2 * i + s, s, i)
            expert_rows(MOE_SLOTS - 1, 0, MOE_SLOTS // 2, more=False)

            for n in range(TT // 5):
                h = n % 2
                dve.wait_ge(picks_gathered[h], 160 * (n // 2 + 1))
                if n >= 2:
                    dve.wait_ge(out_stored[h], 16 * (n // 2))
                for r in range(5):
                    t = 5 * n + r
                    o = o_ring[:, h * 5 + r, :]
                    link(nc.vector.scalar_tensor_tensor(o, picked[:, h * 10 + 2 * r, :], gates[:, 0, t:t + 1],
                                                        M[:, t * C:(t + 1) * C], ALU.mult, ALU.add))
                    link(nc.vector.scalar_tensor_tensor(o, picked[:, h * 10 + 2 * r + 1, :], gates[:, 1, t:t + 1],
                                                        o, ALU.mult, ALU.add))
                dve.sem_inc(out_rows, 1)

        @block.scalar
        def _(act):
            roots = [0]

            def square_root():
                roots[0] += 1
                act.wait_ge(var_ready, roots[0])
                nc.scalar.activation(root, var, ACT.Sqrt).then_inc(root_ready, 1)

            square_root()
            square_root()

            def copy_xn(t, s):
                act.wait_ge(transposed, t + 1)
                nc.scalar.activation(xn_ring[:, s, :], M[:, ds(t * C, C)], ACT.Copy).then_inc(xn_copied, 1)

            def copy_transposes(t, s):
                act.wait_ge(transposed, t + 3)
                nc.scalar.activation(tr_ring[:, s, :, :].rearrange("p q c -> p (q c)"), B[s][:, :], ACT.Copy) \
                    .then_inc(transposes_copied, 1)

            act.wait_ge(folded, 1)
            act.sem_inc(transposes_copied, 2)
            staggered(act, copy_xn, copy_transposes)

            act.wait_ge(exp_input, 2)
            nc.scalar.activation(qkv[:, :, C:QKV], qkv[:, :, C:QKV], ACT.Exp).then_inc(exp_done, 1)

            def copy_q(t, s):
                act.wait_ge(q_transposed, t + 3)
                nc.scalar.activation(qT_ring[:, s, :], B[s][0:HR + 1, 0:P], ACT.Copy).then_inc(q_copied, 1)

            act.sem_inc(q_copied, 2)
            pairs(act, copy_q)
            square_root()
            act.wait_ge(support_stored, 16)

            def copy_z2(t, s):
                act.wait_ge(z2_transposed, t + 3)
                nc.scalar.activation(z2T[:, :, ds(t * P, P)], B[s][:, 0:C].rearrange("p (k n) -> p k n", k=KC),
                                     ACT.Copy).then_inc(z2_copied, 1)

            act.sem_inc(z2_copied, 2)
            pairs(act, copy_z2)

            act.wait_ge(mlp_weights, 1)
            act.sem_inc(gelu_done, 4)
            with act.Fori(0, TT // CH) as c:
                for f in range(FT):
                    for half in range(2):
                        act.wait_ge(up_product, 16 * c + 2 * f + half + 1)
                        nc.scalar.activation(hidT[:, f, half * CN:(half + 1) * CN], B[(2 * f + half) % 4][:, 0:CN],
                                             ACT.Gelu, bias=b1[:, f:f + 1]).then_inc(gelu_done, 1)

            square_root()

            def copy_x2(t, s):
                act.wait_ge(xn2_ready, t + 1)
                act.wait_ge(xn2_transposed, t + 1)
                nc.scalar.activation(x2_ring[:, s, :], acc[:, ds(t * C, C)], ACT.Copy).then_inc(xn2_copied, 1)

            def copy_x2T(t, s):
                act.wait_ge(xn2_transposed, t + 3)
                nc.scalar.activation(x2T_ring[:, s, :, :].rearrange("p k c -> p (k c)"), B[s][:, 0:C], ACT.Copy) \
                    .then_inc(xn2_transposes_copied, 1)

            act.sem_inc(xn2_transposed, 2)
            act.sem_inc(xn2_transposes_copied, 2)
            staggered(act, copy_x2, copy_x2T)
            act.wait_ge(exp_input, 3)
            nc.scalar.activation(probs[:, :, :], probs[:, :, :], ACT.Exp).then_inc(exp_done, 1)

            act.sem_inc(half0_copied, 1)

            def copy_slot(j, s):
                act.wait_ge(slot_transposed, j + 1)
                nc.scalar.activation(exT_ring[:, s, :, :].rearrange("p k c -> p (k c)"), B[6][:, 0:C], ACT.Copy) \
                    .then_inc(slot_copied, 1)

            def silu(j, a, first=False):
                act.wait_ge((half0_product, half1_product)[a], j + 1)
                if not first:
                    act.wait_ge((half0_gated, half1_gated)[a], j)
                nc.scalar.activation(g_ring[:, a, :], B[2 * a][:, 0:HH], ACT.Silu) \
                    .then_inc((half0_silu, half1_silu)[a], 1)

            def expert_copies(j, s, more=2):
                if more:
                    silu(j + 1, 0)
                act.wait_ge(half0_transposed, j + 1)
                nc.scalar.activation(hT_ring[:, 0:3, :].rearrange("p f c -> p (f c)"), B[4][0:HB, 0:3 * P],
                                     ACT.Copy).then_inc(half0_copied, 1)
                if more == 2:
                    copy_slot(j + 2, s)
                if more:
                    silu(j + 1, 1)

            copy_slot(0, 0)
            copy_slot(1, 1)
            silu(0, 0, first=True)
            silu(0, 1, first=True)
            pairs(act, expert_copies, MOE_SLOTS - 3)
            expert_copies(MOE_SLOTS - 3, 0)
            expert_copies(MOE_SLOTS - 2, 1, more=1)
            expert_copies(MOE_SLOTS - 1, 0, more=0)

        @block.tensor
        def _(pe):
            mm = nc.tensor.matmul
            ranked = [0]

            def count_sums(K):
                ranked[0] += 1
                pe.wait_ge(rank_counts, ranked[0])
                mm(B[7][:, 0:K], upper[:, :], small[:, 0, 0:K], start=True, stop=True)
                mm(B[7][:, K:2 * K], ones[:, :], small[:, 0, 0:K], start=True, stop=True).then_inc(rank_sums, 1)

            pe.wait_ge(constants, 11)
            count_sums(TT)

            pe.wait_ge(weights_in, 16 * 15)
            for m in range(KC):
                for k in range(KC):
                    ins = mm(B[m][:, 0:QKV], wxt[:, k, m * P:(m + 1) * P], wqkv[:, k, :],
                             start=(k == 0), stop=(k == KC - 1))
                ins.then_inc(fold_products, 1)
            pe.wait_ge(fold_inputs, 6)
            for k in range(KC):
                mm(B[2][:, 0:QKV], vbc[:, 0, k, :], wraw[:, k, :], start=(k == 0), stop=False)
            for k in range(KC):
                ins = mm(B[2][:, 0:QKV], vbc[:, 1, k, :], wqkv[:, k, :], start=False, stop=(k == KC - 1))
            ins.then_inc(bias_product, 1)
            for f in range(FT):
                for k in range(KC):
                    ins = mm(B[6][:, f:f + 1], w1[:, k, f * P:(f + 1) * P], vecs[:, 4, k:k + 1],
                             start=(k == 0), stop=(k == KC - 1))
            ins.then_inc(b1_product, 1)
            pe.wait_ge(folded, 1)

            def transpose_tokens(t, s):
                pe.wait_ge(xn_copied, t + 1)
                pe.wait_ge(z_ready, t + 1)
                pe.wait_ge(transposes_copied, t + 1)
                for q, ring in enumerate((xn_ring, xn_ring, z_ring, z_ring)):
                    c = q % 2 * P
                    ins = nc.tensor.transpose(B[s][:, q * P:(q + 1) * P], ring[:, s, c:c + P], ident[:, :])
                ins.then_inc(transposed, 1)

            def token_product(t, s):
                pe.wait_ge(transposes_copied, t + 3)
                pe.wait_ge(support_ready, t + 1)
                pe.wait_ge(qkv_ready, t + 1)
                for k in range(KC):
                    mm(B[2 + s][:, 0:C], tr_ring[:, s, k, :], wg[:, k, :], start=(k == 0), stop=(k == KC - 1))
                for k in range(KC):
                    ins = mm(B[4 + s][:, 0:QKV], tr_ring[:, s, KC + k, :], wfold[:, k, :],
                             start=(k == 0), stop=(k == KC - 1))
                ins.then_inc(token_products, 1)

            staggered(pe, transpose_tokens, token_product)

            pe.wait_ge(kmax_ready, 1)
            nc.tensor.transpose(B[6][0:HR, 0:P], kmax[:, :], ident[:, :]).then_inc(kmax_transposed, 1)
            pe.wait_ge(kmax_diagonal, 1)
            mm(B[7][:, 0:HR], ones[0:HR, :], diag[:, :], start=True, stop=True).then_inc(kmax_spread, 1)
            pe.wait_ge(exp_done, 1)
            pe.wait_ge(qkv_ready, TT + 2)
            for t in range(TT):
                kt = qkv[:, t, C + HR:QKV]
                for b, left in ((2, qkv[:, t, 0:P]), (3, qkv[:, t, P:C]), (4, ones[:, :])):
                    ins = mm(B[b][:, 0:HR], left, kt, start=(t == 0), stop=(t == TT - 1))
            ins.then_inc(kv_product, 1)
            pe.wait_ge(kv_ready, KC)
            for k in range(KC):
                ins = mm(B[5][0:HR, 0:C], kvT[:, k, :], wo[:, k, :], start=(k == 0), stop=(k == KC - 1))
            ins.then_inc(attn_product, 1)
            pe.wait_ge(attn_weights, 1)

            def transpose_q(t, s):
                pe.wait_ge(q_ready, t + 1)
                pe.wait_ge(q_copied, t + 1)
                nc.tensor.transpose(B[s][:, 0:P], q_ring[:, s, :], ident[:, :]).then_inc(q_transposed, 1)

            def attn_product_of(t, s):
                pe.wait_ge(q_copied, t + 3)
                pe.wait_ge(residual_ready, t + 1)
                mm(B[2 + s][:, 0:C], qT_ring[:, s, :], attn_w[:, :], start=True, stop=True).then_inc(attn_rows, 1)

            staggered(pe, transpose_q, attn_product_of)

            def transpose_z2(t, s):
                pe.wait_ge(z2_ready, t + 1)
                pe.wait_ge(z2_copied, t + 1)
                for k in range(KC):
                    ins = nc.tensor.transpose(B[s][:, k * P:(k + 1) * P], z_ring[:, s, k * P:(k + 1) * P], ident[:, :])
                ins.then_inc(z2_transposed, 1)

            pairs(pe, transpose_z2)

            pe.wait_ge(mlp_weights, 1)
            pe.wait_ge(z2_copied, TT + 2)
            with pe.Fori(0, TT // CH) as c:
                for g in range(2 * FT):
                    f, half = g // 2, g % 2
                    pe.wait_ge(gelu_done, 2 * FT * c + g + 1)
                    for k in range(KC):
                        ins = mm(B[g % 4][:, 0:CN], w1[:, k, f * P:(f + 1) * P],
                                 z2T[:, k, ds(c * 2 * CN + half * CN, CN)], start=(k == 0), stop=(k == KC - 1))
                    ins.then_inc(up_product, 1)
                pe.wait_ge(gelu_done, 2 * FT * c + 2 * FT + 4)
                for i in range(CH):
                    pe.wait_ge(down_added, CH * c + (i + 1 if i else 4))
                    for f in range(FT):
                        ins = mm(B[4 + i % 4][:, 0:C], hidT[:, f, i * P:(i + 1) * P], w2[:, f, :],
                                 start=(f == 0), stop=(f == FT - 1))
                    ins.then_inc(down_product, 1)

            pe.wait_ge(down_added, 4 + TT)
            with pe.Fori(0, EDGE_SLOTS // (2 * HALF)) as i:
                for n in range(2 * HALF):
                    j, k = 2 * HALF * i + n, n % HALF
                    if k == 0:
                        pe.wait_ge(rows_gathered[n // HALF], 16 * HALF * (i + 1))
                    pe.wait_ge(edge_onehots, j + 1)
                    pe.wait_ge(acc_added, j + 1)
                    mm(B[k][:, 0:C], S[:, n, :], gathered[:, n, :], start=True, stop=True) \
                        .then_inc(edge_products, 1)

            def transpose_x2(t, s):
                pe.wait_ge(xn2_copied, t + 1)
                pe.wait_ge(xn2_transposes_copied, t + 1)
                for k in range(KC):
                    ins = nc.tensor.transpose(B[s][:, k * P:(k + 1) * P], x2_ring[:, s, k * P:(k + 1) * P], ident[:, :])
                ins.then_inc(xn2_transposed, 1)

            def router(t, s):
                pe.wait_ge(xn2_transposes_copied, t + 3)
                pe.wait_ge(logits_copied, t + 1)
                for k in range(KC):
                    ins = mm(B[2 + s][:, 0:EXPERTS], x2T_ring[:, s, k, :], rt[:, k, :],
                             start=(k == 0), stop=(k == KC - 1))
                ins.then_inc(router_product, 1)

            staggered(pe, transpose_x2, router)
            count_sums(EXPERTS)
            pe.wait_ge(pick_rows, 2)

            def transpose_slot(j, s, arrivals, first=False):
                pe.wait_ge(slot_rows_in[s], 16 * arrivals)
                if not first:
                    pe.wait_ge(slot_copied, j)
                for k in range(KC):
                    ins = nc.tensor.transpose(B[6][:, k * P:(k + 1) * P], ex_ring[:, s, k * P:(k + 1) * P], ident[:, :])
                ins.then_inc(slot_transposed, 1)

            def up_half(e, j, s, a, first=False):
                pe.wait_ge(slot_copied, j + 1)
                if not first:
                    pe.wait_ge((half0_gated, half1_gated)[a], j)
                for part in (2 * a, 2 * a + 1):
                    for k in range(KC):
                        ins = mm(B[part][:, 0:HH], exT_ring[:, s, k, :],
                                 R1[:, ds(e * (KC * W13) + (k * W13 + part * HH), HH)],
                                 start=(k == 0), stop=(k == KC - 1))
                ins.then_inc((half0_product, half1_product)[a], 1)

            def transpose_half(j, a):
                pe.wait_ge((half0_gated, half1_gated)[a], j + 1)
                pe.wait_ge((half0_copied, half1_copied)[a], j + 1)
                for f in range(3):
                    ins = nc.tensor.transpose(B[4 + a][0:HB, f * P:(f + 1) * P], h_ring[:, a, f * HB:(f + 1) * HB],
                                              ident[:, :])
                ins.then_inc((half0_transposed, half1_transposed)[a], 1)

            def expert_of(j):
                return pe.value_load(slot_expert[0:1, ds(j, 1)], min_val=0, max_val=EXPERTS - 1)

            def down(j):
                e = expert_of(j)
                pe.wait_ge(half0_copied, j + 2)
                pe.wait_ge(half1_copied, j + 2)
                pe.wait_ge(down_copied, j + 1)
                for f in range(NHB):
                    ins = mm(B[7][:, 0:C], hT_ring[:, f, :], XA[0:HB, ds(e * (NHB * C) + f * C, C)],
                             start=(f == 0), stop=(f == NHB - 1))
                ins.then_inc(down_rows, 1)

            def expert(j, s, i=None, more=2):
                if more:
                    e = expert_of(j + 1)
                    up_half(e, j + 1, 1 - s, 0)
                for a in range(2):
                    transpose_half(j, a)
                if more == 2:
                    transpose_slot(j + 2, s, i + 2)
                if more:
                    up_half(e, j + 1, 1 - s, 1)
                down(j)

            pe.wait_ge(experts_up_in, 16 * EXPERTS)
            transpose_slot(0, 0, 1, first=True)
            transpose_slot(1, 1, 1)
            e0 = expert_of(0)
            up_half(e0, 0, 0, 0, first=True)
            up_half(e0, 0, 0, 1, first=True)
            pe.wait_ge(experts_down_in, 32)
            with pe.Fori(0, (MOE_SLOTS - 3) // 2) as i:
                for s in range(2):
                    expert(2 * i + s, s, i)
            expert(MOE_SLOTS - 3, 0, (MOE_SLOTS - 3) // 2)
            expert(MOE_SLOTS - 2, 1, more=1)
            expert(MOE_SLOTS - 1, 0, more=0)


def kernel(**inputs):
    import numpy as np
    import concourse.bacc as bacc
    from concourse.bass_utils import run_bass_kernel_spmd

    a = {k: np.asarray(v) for k, v in inputs.items()}

    def by_partition(v, dt=np.float32):
        return np.ascontiguousarray(v.reshape(-1, P).T)

    xp = np.zeros((TOKENS, C), np.float32)
    xp[:NODES] = a["x"]

    def edges(v):
        e = np.zeros(P * EC, v.dtype)
        e[:EDGES] = v
        return e.reshape(P, EC)

    w_qkv = np.zeros((C, QKV), np.float32)
    for h in range(HEADS):
        rows = slice(h * DH, (h + 1) * DH)
        w_qkv[rows, h * DH:(h + 1) * DH] = a["L0_mix_Wv"]
        w_qkv[rows, C + h * KR:C + (h + 1) * KR] = a["L0_mix_Wq"]
        w_qkv[rows, C + HR + h * KR:C + HR + (h + 1) * KR] = a["L0_mix_Wk"]

    up = np.zeros((2, EXPERTS, 2 * HH, C), np.float32)
    up[0, :, :H], up[1, :, :H] = a["L0_ffn_w1"], a["L0_ffn_w3"]
    up = up.reshape(2, EXPERTS, 2, HH, KC, P)
    w_13 = np.ascontiguousarray(up.transpose(5, 1, 4, 2, 0, 3)).reshape(P, EXPERTS, KC * W13)
    down = np.zeros((EXPERTS, C, 2 * HH), np.float32)
    down[:, :, :H] = a["L0_ffn_w2"]
    w_down = np.ascontiguousarray(down.reshape(EXPERTS, C, NHB, HB).transpose(3, 0, 2, 1)).reshape(HB, -1)

    arrays = {
        "x": xp, "src": edges(a["src"]), "dst": edges(a["dst"]), "edge_w": edges(a["edge_weight"]),
        "w_gnn": a["L0_gnn_weight"], "wx_t": np.ascontiguousarray(a["L0_mix_Wx"].T), "w_qkv": w_qkv,
        "ln1_g": by_partition(a["L0_mix_ln1_g"]), "ln1_b": by_partition(a["L0_mix_ln1_b"]),
        "bx": by_partition(a["L0_mix_bx"]), "w_o": a["L0_mix_Wo"], "b_o": a["L0_mix_bo"].reshape(1, C),
        "ln2_g": by_partition(a["L0_mix_ln2_g"]), "ln2_b": by_partition(a["L0_mix_ln2_b"]),
        "w_1": a["L0_mix_W1"], "b_1": by_partition(a["L0_mix_b1"]), "w_2": a["L0_mix_W2"], "b_2": a["L0_mix_b2"],
        "router_t": np.ascontiguousarray(a["L0_ffn_router_w"].T), "w_13": w_13, "w_down": w_down,
    }
    nc = bacc.Bacc("TRN2", target_bir_lowering=False, num_devices=1)
    aps = {k: nc.dram_tensor(f"in_{k}", v.shape, mybir.dt.from_np(v.dtype), kind="ExternalInput").ap()
           for k, v in arrays.items()}
    out = nc.dram_tensor("out_rows_dram", (NODES, C), mybir.dt.float32, kind="ExternalOutput").ap()
    gps_layer(nc, out=out, **aps)
    r = run_bass_kernel_spmd(nc, [{f"in_{k}": v for k, v in arrays.items()}], core_ids=[0])
    return r.results[0]["out_rows_dram"]
```

```python
import concourse.bass as bass
from concourse import mybir
from contextlib import ExitStack

P = 128
NODES, C, EDGES = 3125, 256, 50000
KC = C // P
TT = -(-NODES // P)
TOKENS = TT * P
LAST = NODES - (TT - 1) * P
EC = 392
HEADS, DH, KR = 8, 32, 4
HR = HEADS * KR
QKV = C + 2 * HR
FF = 4 * C
FT = FF // P
EXPERTS, H = 8, 682
HB = 114
NHB = 6
HH = HB * NHB // 2
W13 = 4 * HH
EPS = 1e-5
RECORD = 3
EDGE_SLOTS = (P * EC + TT * (P - 1)) // P
PICKS = 2 * TT
MOE_SLOTS = (2 * NODES + EXPERTS * (P - 1)) // P
HS = 28
HALF = 8
NEG = -1.0e30
CONSTANTS = 17
ROW = C + 2
UP_LOADS = 16
FIRST = 17


def gps_layer(nc, x, src, dst, edge_w, w_gnn, wx_t, w_qkv, ln1_g, ln1_b, bx, w_o, b_o, ln2_g, ln2_b,
              w_1, b_1, w_2, b_2, router_t, w_13, w_down, out):
    fp32, i32, u32 = mybir.dt.float32, mybir.dt.int32, mybir.dt.uint32
    ALU = mybir.AluOpType
    ACT = mybir.ActivationFunctionType
    X = mybir.AxisListType.X
    ds = bass.ds
    ZERO_TILES = TT * C // ROW
    zero_stores = -(-MOE_SLOTS // ZERO_TILES) + 1

    support_d = nc.dram_tensor("support_scratch", (TOKENS, C), fp32).ap()
    records_d = nc.dram_tensor("records_scratch", (P * EDGE_SLOTS, RECORD), i32).ap()
    routed_d = nc.dram_tensor("routed_scratch", ((MOE_SLOTS + 2) * P, ROW), fp32).ap()
    sum_d = nc.dram_tensor("sum_scratch", (TOKENS + P, C), fp32).ap()

    ctx = ExitStack()
    with ctx:
        def sb(name, shape, dt=fp32):
            return ctx.enter_context(nc.sbuf_tensor(name, shape, dt))

        def sem(name):
            return ctx.enter_context(nc.semaphore(name))

        MXA = sb("MXA", [P, 3 * TT * C])
        M = MXA[:, 0:TT * C]
        XA = MXA[:, TT * C:]
        w2_e = MXA[0:HB, 0:EXPERTS * NHB * C]
        R1 = sb("R1", [P, EXPERTS * KC * W13])
        xs = XA[:, 0:TT * C]
        acc = XA[:, TT * C:2 * TT * C]
        qkv = R1[:, 0:TT * QKV].rearrange("p (t c) -> p t c", c=QKV)
        z2T = R1[:, TT * QKV:TT * QKV + KC * TOKENS].rearrange("p (k n) -> p k n", k=KC)
        CH = 5
        CN = CH * P // 2
        hid0 = TT * QKV + KC * TOKENS
        hidT = R1[:, hid0:hid0 + FT * CH * P].rearrange("p (f n) -> p f n", f=FT)
        odd0 = EXPERTS * KC * W13 - TT * C
        assert odd0 % UP_LOADS == 0
        acc_odd = R1[:, odd0:]
        gathered = XA[:, 0:2 * HALF * C].rearrange("p (s c) -> p s c", c=C)
        S = XA[:, 2 * HALF * C:2 * HALF * C + 2 * HALF * P].rearrange("p (s c) -> p s c", c=P)
        routed = XA[:, 2 * TT * C - TT * ROW:].rearrange("p (t c) -> p t c", c=ROW)
        sup_all = R1[:, TT * QKV:TT * QKV + TT * C]
        oh_e = R1[:, 0:2 * TT * EC]
        cum_e = R1[:, TT * EC:2 * TT * EC]
        dst_in = M[:, 0:EC].bitcast(i32)
        weight_in = M[:, EC:2 * EC]
        src_part = M[:, 2 * EC:3 * EC].bitcast(i32)
        key_e = M[:, 3 * EC:4 * EC]
        token_rings = R1[:, hid0:hid0 + FT * CH * P]
        xn_ring = token_rings[:, 0:512].rearrange("p (s c) -> p s c", s=2)
        z_ring = token_rings[:, 512:1024].rearrange("p (s c) -> p s c", s=2)
        tr_ring = token_rings[:, 1024:2048].rearrange("p (s q c) -> p s q c", s=2, c=P)
        q_ring = token_rings[:, 4096:4096 + 2 * P].rearrange("p (s c) -> p s c", s=2)
        qT_ring = token_rings[0:HR + 1, 2200:2456].rearrange("p (s c) -> p s c", s=2)
        wraw = token_rings[:, 2456:2456 + KC * QKV].rearrange("p (k n) -> p k n", k=KC)
        wfold = token_rings[:, 3096:3096 + KC * QKV].rearrange("p (k n) -> p k n", k=KC)
        bqkv = token_rings[:, 3736:3736 + QKV]
        tail = R1[:, 2 * TT * EC:]
        wxt = tail[:, 0:KC * C].rearrange("p (k n) -> p k n", k=KC)
        wqkv = tail[:, 512:512 + KC * QKV].rearrange("p (k n) -> p k n", k=KC)
        vbc = tail[:, 1152:1664].rearrange("p (v k c) -> p v k c", v=2, k=KC)
        wo = tail[:, 1664:2176].rearrange("p (k n) -> p k n", k=KC)

        ident = sb("ident", [P, P])
        upper = sb("upper", [P, P])
        ones = sb("ones", [P, P])
        iota_r = sb("iota_r", [P, EDGE_SLOTS])
        padneg = sb("padneg", [P, 1])
        kvmask = sb("kvmask", [P, KC, HEADS, KR])
        wg = sb("wg", [P, KC, C])
        vecs = sb("vecs", [P, 5, KC])
        kvT = sb("kvT", [P, KC, HR])
        attn_w = sb("attn_w", [HR + 1, C])
        WM = sb("WM", [P, KC * FF + FT * C])
        w1 = WM[:, 0:KC * FF].rearrange("p (k n) -> p k n", k=KC)
        w2 = WM[:, KC * FF:].rearrange("p (f n) -> p f n", f=FT)
        b1 = sb("b1", [P, FT])
        b2 = sb("b2", [P, C])
        rt = sb("rt", [P, KC, EXPERTS])
        rec = sb("rec", [P, EC, RECORD], i32)
        row_e = sb("row_e", [P, EC], i32)
        tab = sb("tab", [P, (EDGE_SLOTS + HALF) * RECORD], i32)
        stage_i = sb("stage_i", [P, 2, HS], i32)
        stage_r = sb("stage_r", [P, 2, HS, RECORD], i32)
        edge_owner = sb("edge_owner", [1, EDGE_SLOTS], i32)
        slot_expert = sb("slot_expert", [1, MOE_SLOTS], i32)
        stats = sb("stats", [P, TT, 6])
        ln = sb("ln", [P, 8, TT])
        mean, var, rstd, t0, t1, root, shift = (ln[:, i, :] for i in range(7))
        small = sb("small", [P, 8, TT])
        probs = sb("probs", [P, TT, EXPERTS])
        pick = sb("pick", [P, 2, TT, EXPERTS])
        keys_m = sb("keys_m", [P, PICKS])
        row_m = sb("row_m", [P, PICKS], i32)
        gates = sb("gates", [P, 2, TT])
        q_red = sb("q_red", [P, TT, HEADS])
        kmax = sb("kmax", [P, HR])
        kmax_t = sb("kmax_t", [HR, 1])
        diag = sb("diag", [HR, HR])
        kden = sb("kden", [P, HR])
        token_ids = sb("token_ids", [P, TT])
        pad_key = sb("pad_key", [P, 1])
        pad_rows = sb("pad_rows", [P, 2])
        trash = sb("trash", [P, 1])
        slot_meta = sb("slot_meta", [P, MOE_SLOTS, 2])
        slot_fill = sb("slot_fill", [P, 2])
        slot_token = sb("slot_token", [P, 2], i32)
        RP = -(-TT // 2)
        x1T_ring = WM[:, 0:4 * C].rearrange("p (s t k c) -> p s t k c", s=2, t=2, k=KC)
        oh_m = WM[:, 1024:1024 + MOE_SLOTS * EXPERTS]
        cum_m = WM[:, 1600:1600 + EXPERTS * PICKS]
        ex_ring = WM[:, 0:2 * ROW].rearrange("p (s c) -> p s c", s=2)
        exT_ring = WM[:, 516:1028].rearrange("p (s k c) -> p s k c", s=2, k=KC)
        h_ring = WM[:, 1028:1028 + 2 * HH].rearrange("p (a c) -> p a c", a=2)
        g_ring = WM[:, 1712:1712 + 2 * HH].rearrange("p (a c) -> p a c", a=2)
        hT_ring = WM[0:HB, 2400:2400 + NHB * P].rearrange("p (f c) -> p f c", f=NHB)
        y_ring = WM[:, 3200:3712].rearrange("p (s c) -> p s c", s=2)

        B = [ctx.enter_context(nc.psum_tensor(f"bank{i}", [P, 512], fp32)) for i in range(8)]

        edges_in, x_in, weights_in, constants, acc_zeroed, records_zeroed = (
            sem(n) for n in "edges_in x_in weights_in constants acc_zeroed records_zeroed".split())
        routed_zeroed, rank_counts, rank_sums, edge_rows, staged, records_in = (
            sem(n) for n in "routed_zeroed rank_counts rank_sums edge_rows staged records_in".split())
        support_stored, gather_staged, edge_onehots, edge_products, acc_added, vector_step = (
            sem(n) for n in "support_stored gather_staged edge_onehots edge_products acc_added vector_step".split())
        x_stats, var_ready, root_ready, xn_ready, xn_copied, z_ready = (
            sem(n) for n in "x_stats var_ready root_ready xn_ready xn_copied z_ready".split())
        transposed, transposes_copied, token_products, support_ready, qkv_ready, x_plus_b2 = (
            sem(n) for n in "transposed transposes_copied token_products support_ready qkv_ready x_plus_b2".split())
        fold_products, fold_inputs, bias_product, folded, kmax_ready, kmax_transposed = (
            sem(n) for n in "fold_products fold_inputs bias_product folded kmax_ready kmax_transposed".split())
        kmax_diagonal, kmax_spread, exp_input, exp_done, kv_product, kv_ready = (
            sem(n) for n in "kmax_diagonal kmax_spread exp_input exp_done kv_product kv_ready".split())
        attn_product, attn_weights, q_ready, q_transposed, q_copied, attn_rows = (
            sem(n) for n in "attn_product attn_weights q_ready q_transposed q_copied attn_rows".split())
        residual_ready, z2_ready, z2_transposed, z2_copied, mix_residual, b1_product = (
            sem(n) for n in "residual_ready z2_ready z2_transposed z2_copied mix_residual b1_product".split())
        mlp_weights, up_product, gelu_done, down_product, down_added, x1_ready = (
            sem(n) for n in "mlp_weights up_product gelu_done down_product down_added x1_ready".split())
        xn2_ready, x1_transposed, x1_transposes_copied, router_product = (
            sem(n) for n in "xn2_ready x1_transposed x1_transposes_copied router_product".split())
        pick_rows, second_gates, experts_up_in, experts_down_in, slot_transposed, slot_copied = (
            sem(n) for n in "pick_rows second_gates experts_up_in experts_down_in slot_transposed slot_copied".split())
        half0_product, half1_product, half0_silu, half1_silu, half0_gated, half1_gated = (
            sem(n) for n in "half0_product half1_product half0_silu half1_silu half0_gated half1_gated".split())
        half0_transposed, half1_transposed, half0_copied, half1_copied, down_rows, down_copied = (
            sem(n) for n in "half0_transposed half1_transposed half0_copied half1_copied down_rows down_copied".split())
        norm2_columns, x1_stored, rows_added, out_stored, meta_saved = (
            sem(n) for n in "norm2_columns x1_stored rows_added out_stored meta_saved".split())
        stages_seen = sem("stages_seen")
        slot_filled, acc_odd_zeroed, sums_joined, k_summed = sem("slot_filled"), sem("acc_odd_zeroed"), sem("sums_joined"), sem("k_summed")
        src_in = sem("src_in")
        records_scattered = [sem(f"records_scattered{h}") for h in range(2)]
        rows_gathered = [sem(f"rows_gathered{h}") for h in range(2)]
        slot_rows_in = [sem(f"slot_rows_in{h}") for h in range(2)]
        rows_routed = [sem(f"rows_routed{g}") for g in range(2)]

        def pairs(engine, body, n=TT):
            with engine.Fori(0, n // 2) as i:
                body(2 * i, 0)
                body(2 * i + 1, 1)
            if n % 2:
                body(n - 1, 0)

        def staggered(engine, ahead, behind, first=None):
            def both(t, s):
                steps = (lambda: ahead(t + 2, s)), (lambda: behind(t, s))
                for run in steps if first is ahead else steps[::-1]:
                    run()

            ahead(0, 0)
            ahead(1, 1)
            with engine.Fori(0, (TT - 3) // 2) as i:
                for s in range(2):
                    both(2 * i + s, s)
            both(TT - 3, 0)
            behind(TT - 2, 1)
            behind(TT - 1, 0)

        assert MOE_SLOTS % 2 == 0
        block = ctx.enter_context(nc.Block())

        @block.sync
        def _(sp):
            sp.dma_start(row_e[:, :], src).then_inc(src_in, 16)
            for dram, part in ((dst, dst_in), (edge_w, weight_in)):
                sp.dma_start(part, dram).then_inc(edges_in, 16)
            x_v = x.rearrange("(t p) c -> p t c", p=P)
            sp.dma_start(xs.rearrange("p (t c) -> p t c", c=C), x_v).then_inc(x_in, 16)
            kp = lambda w: w.rearrange("(k p) n -> p k n", p=P)
            for dram, part in ((kp(wx_t), wxt[:, :, :]), (kp(w_qkv), wqkv[:, :, :]), (ln1_g, vecs[:, 0, :]),
                               (ln1_b, vecs[:, 1, :]), (bx, vecs[:, 2, :]), (ln2_g, vecs[:, 3, :]),
                               (ln2_b, vecs[:, 4, :]), (kp(w_gnn), wg[:, :, :]), (kp(w_o), wo[:, :, :]),
                               (b_o, attn_w[HR:HR + 1, :]), (kp(w_1), w1[:, :, :]), (b_1, b1[:, :]),
                               (kp(w_2), w2[:, :, :]), (b_2.partition_broadcast(P), b2[:, :]),
                               (kp(router_t), rt[:, :, :])):
                sp.dma_start(part, dram).then_inc(weights_in, 16)
            sp.wait_ge(acc_zeroed, 1)
            sp.dma_start(records_d.rearrange("(p j) w -> p (j w)", p=P),
                         acc[:, 0:EDGE_SLOTS * RECORD].bitcast(i32)).then_inc(records_zeroed, 16)
            for j in range(0, MOE_SLOTS, ZERO_TILES):
                n = min(ZERO_TILES, MOE_SLOTS - j)
                sp.dma_start(routed_d[j * P:(j + n) * P, :].rearrange("(p r) c -> p (r c)", p=P),
                             acc[:, 0:n * ROW]).then_inc(routed_zeroed, 16)
            sp.dma_start(sum_d[TOKENS:, :], acc[:, 0:C]).then_inc(routed_zeroed, 16)

            sp.wait_ge(support_ready, TT + 2)
            sp.dma_start(support_d.rearrange("(t p) c -> p t c", p=P),
                         sup_all.rearrange("p (t c) -> p t c", c=C)).then_inc(support_stored, 16)
            sp.wait_ge(records_scattered[0], 16 * (EC // 2))
            sp.wait_ge(records_scattered[1], 16 * (EC // 2))
            sp.dma_start(tab[:, 0:EDGE_SLOTS * RECORD],
                         records_d.rearrange("(p j) w -> p (j w)", p=P)).then_inc(records_in, 16)
            sp.wait_ge(down_added, 4 + TT)
            w_13f = w_13.rearrange("p e n -> p (e n)")
            step_cols, step_tiles = odd0 // UP_LOADS, EDGE_SLOTS // UP_LOADS
            with sp.Fori(0, UP_LOADS) as i:
                sp.wait_ge(acc_added, i * step_tiles + 1 + HALF)
                sp.dma_start(R1[:, ds(i * step_cols, step_cols)],
                             w_13f[:, ds(i * step_cols, step_cols)]).then_inc(experts_up_in, 16)
            sp.wait_ge(x1_ready, TT // CH)
            sp.dma_start(R1[:, odd0:], w_13f[:, odd0:]).then_inc(experts_up_in, 16)
            sp.dma_start(sum_d[0:TOKENS, :].rearrange("(t p) c -> p t c", p=P),
                         M.rearrange("p (t c) -> p t c", c=C)).then_inc(x1_stored, 16)
            sp.dma_start(w2_e[:, TT * C:], w_down[:, TT * C:]).then_inc(experts_down_in, 16)
            sp.wait_ge(x1_stored, 16)
            sp.wait_ge(router_product, RP + 2)
            sp.wait_ge(xn2_ready, TT)
            sp.dma_start(w2_e[:, 0:TT * C], w_down[:, 0:TT * C]).then_inc(experts_down_in, 16)

            def load_slot(j, s):
                sp.dma_start(ex_ring[:, s, :], routed_d[ds(j * P, P), :]).then_inc(slot_rows_in[s], 16)

            sp.wait_ge(rows_routed[0], 32 * FIRST)
            sp.wait_ge(rows_routed[1], 32 * (TT - FIRST))
            load_slot(0, 0)
            load_slot(1, 1)

            def next_slot(j, s):
                sp.wait_ge(slot_transposed, j + 1)
                sp.wait_ge(meta_saved, j + 1)
                load_slot(j + 2, s)

            pairs(sp, next_slot, MOE_SLOTS - 2)

            sp.wait_ge(rows_added, 16 * MOE_SLOTS)
            sp.dma_start(out, sum_d[0:NODES, :]).then_inc(out_stored, 16)
            sp.wait_ge(out_stored, 16)

        @block.gpsimd
        def _(pool):
            pool.memset(tab[:, EDGE_SLOTS * RECORD:], 0).then_inc(constants, 1)
            pool.memset(ident[:, :], 0.0).then_inc(constants, 1)
            pool.memset(ones[:, :], 1.0).then_inc(constants, 1)
            pool.memset(padneg[:, :], 0.0).then_inc(constants, 1)
            pool.memset(kvmask[:, :, :, :], 1.0).then_inc(constants, 1)
            pool.iota(iota_r[:, :], pattern=[[1, EDGE_SLOTS]], base=0, channel_multiplier=0,
                      allow_small_or_imprecise_dtypes=True).then_inc(constants, 1)
            pool.iota(token_ids[:, :], pattern=[[P, TT]], base=1, channel_multiplier=1,
                      allow_small_or_imprecise_dtypes=True).then_inc(constants, 1)
            pool.iota(trash[:, :], pattern=[[0, 1]], base=TOKENS + 1, channel_multiplier=1,
                      allow_small_or_imprecise_dtypes=True).then_inc(constants, 1)
            pool.memset(pad_key[:, :], 0.0).then_inc(constants, 1)
            pool.iota(pad_rows[:, :], pattern=[[P, 2]], base=MOE_SLOTS * P, channel_multiplier=1,
                      allow_small_or_imprecise_dtypes=True).then_inc(constants, 1)
            pool.wait_ge(constants, 10)
            pool.affine_select(out=pad_key[:, :], in_=pad_key[:, :], compare_op=ALU.is_ge, fill=float(EXPERTS),
                               base=LAST - 1, pattern=[[0, 1]], channel_multiplier=-1).then_inc(constants, 1)
            pool.affine_select(out=pad_rows[:, :], in_=pad_rows[:, :], compare_op=ALU.is_ge, fill=0.0,
                               base=-LAST, pattern=[[0, 2]], channel_multiplier=1).then_inc(constants, 1)
            pool.affine_select(out=ident[:, :], in_=ident[:, :], compare_op=ALU.not_equal, fill=1.0, base=0,
                               pattern=[[-1, P]], channel_multiplier=1).then_inc(constants, 1)
            pool.affine_select(out=upper[:, :], in_=ones[:, :], compare_op=ALU.is_gt, fill=0.0, base=0,
                               pattern=[[1, P]], channel_multiplier=-1).then_inc(constants, 1)
            pool.affine_select(out=padneg[:, :], in_=padneg[:, :], compare_op=ALU.is_ge, fill=NEG,
                               base=LAST - 1, pattern=[[0, 1]], channel_multiplier=-1).then_inc(constants, 1)
            pool.affine_select(out=kvmask[:, :, :, :], in_=kvmask[:, :, :, :], compare_op=ALU.is_ge, fill=0.0,
                               base=0, pattern=[[P, KC], [-DH, HEADS], [0, KR]],
                               channel_multiplier=1).then_inc(constants, 1)
            pool.wait_ge(constants, 16)
            pool.affine_select(out=kvmask[:, :, :, :], in_=kvmask[:, :, :, :], compare_op=ALU.is_ge, fill=0.0,
                               base=DH - 1, pattern=[[-P, KC], [DH, HEADS], [0, KR]],
                               channel_multiplier=-1).then_inc(constants, 1)

            pool.memset(acc, 0.0).then_inc(acc_zeroed, 1)

            pool.wait_ge(edge_rows, 1)
            pool.wait_ge(records_zeroed, 16)


            def scatter(i, h, first):
                col = (2 * i + h) * HS
                if not first:
                    pool.wait_ge(records_scattered[h], 16 * HS * i)
                pool.tensor_copy(stage_i[:, h, 0:HS], row_e[:, ds(col, HS)]).then_inc(staged, 1)
                pool.tensor_copy(stage_r[:, h, 0:HS, :], rec[:, ds(col, HS), :]).then_inc(staged, 1)
                pool.wait_ge(staged, 4 * i + 2 * h + 2)
                pool.sem_inc(stages_seen, 1)
                for k in range(HS):
                    pool.indirect_dma_start(
                        records_d, bass.IndirectOffsetOnAxis(ap=stage_i[:, h, k:k + 1].bitcast(u32), axis=0),
                        stage_r[:, h, k, :], None).then_inc(records_scattered[h], 16)

            for h in range(2):
                scatter(0, h, True)
            pool.wait_ge(edge_rows, 2)
            with pool.Fori(1, EC // (2 * HS)) as i:
                for h in range(2):
                    scatter(i, h, False)

            pool.wait_ge(records_in, 16)
            pool.wait_ge(support_stored, 16)
            pool.wait_ge(mix_residual, 1)
            tab3 = tab[:, :].rearrange("p (j w) -> p j w", w=RECORD)

            def gather(i, h, first):
                col = (2 * i + h) * HALF
                if not first:
                    pool.wait_ge(edge_products, HALF * (2 * i + h - 1))
                    pool.wait_ge(rows_gathered[h], 16 * HALF * i)
                pool.tensor_copy(stage_i[:, h, 0:HALF], tab3[:, ds(col, HALF), 0]).then_inc(gather_staged, 1)
                pool.wait_ge(gather_staged, 2 * i + h + 1)
                pool.sem_inc(stages_seen, 1)
                for k in range(HALF):
                    pool.indirect_dma_start(
                        gathered[:, h * HALF + k, :], None, support_d,
                        bass.IndirectOffsetOnAxis(ap=stage_i[:, h, k:k + 1].bitcast(u32), axis=0),
                    ).then_inc(rows_gathered[h], 16)

            for h in range(2):
                gather(0, h, True)
            with pool.Fori(1, EDGE_SLOTS // (2 * HALF)) as i:
                for h in range(2):
                    gather(i, h, False)

            pool.wait_ge(routed_zeroed, 16 * zero_stores)
            pool.wait_ge(xn2_ready, TT)
            pool.wait_ge(pick_rows, 1)
            for k in range(2):
                for group, tiles in enumerate((range(FIRST), range(FIRST, TT))):
                    if k:
                        pool.wait_ge(second_gates, group + 1)
                    for t in tiles:
                        col = k * TT + t
                        pool.indirect_dma_start(
                            routed_d, bass.IndirectOffsetOnAxis(ap=row_m[:, col:col + 1].bitcast(u32), axis=0),
                            routed[:, t, :], None).then_inc(rows_routed[group], 16)

            def add_rows(j, s, first=False):
                pool.wait_ge(down_copied, j + 2)
                if not first:
                    pool.wait_ge(rows_added, 16 * j)
                pool.sem_inc(stages_seen, 1)
                pool.indirect_dma_start(
                    sum_d, bass.IndirectOffsetOnAxis(ap=slot_token[:, s:s + 1].bitcast(u32), axis=0),
                    y_ring[:, s, :], None, compute_op=ALU.add).then_inc(rows_added, 16)

            pool.wait_ge(x1_stored, 16)
            add_rows(0, 0, first=True)
            add_rows(1, 1)
            with pool.Fori(1, MOE_SLOTS // 2) as i:
                for s in range(2):
                    add_rows(2 * i + s, s)

        @block.vector
        def _(dve):
            step = [0]

            def link(ins):
                step[0] += 1
                ins.then_inc(vector_step, 1)
                dve.wait_ge(vector_step, step[0])

            ranks = [0]

            def rank(keys, K, T, slots, area, cum, row, swizzle, owner, scale, cuts=(), filling=None):
                n = ranks[0]
                ranks[0] += 1
                cnt, tot, tiles, tinc, d, tmp = (small[:, i, 0:K] for i in range(6))
                oh = area[:, 0:K * T]
                ohv = oh.rearrange("p (k t) -> p k t", t=T)
                cumv = cum.rearrange("p (k t) -> p k t", t=T)
                kb = iota_r[:, 0:K].unsqueeze(2).to_broadcast([P, K, T])
                link(nc.vector.tensor_tensor(ohv, keys.unsqueeze(1).to_broadcast([P, K, T]), kb, ALU.is_equal))
                link(nc.vector.tensor_tensor_scan(cum, oh, oh, 0.0, ALU.add, ALU.max))
                ends = cumv[:, :, T - 1]
                link(nc.vector.tensor_copy(cnt, ends))
                link(nc.vector.tensor_tensor(tmp[:, 1:K], cnt[:, 1:K], cnt[:, 0:K - 1], ALU.subtract))
                link(nc.vector.tensor_copy(tmp[:, 0:1], cnt[:, 0:1]))
                link(nc.vector.tensor_tensor(d, cnt, tmp, ALU.subtract))
                nc.vector.tensor_copy(cnt, tmp).then_inc(rank_counts, 1)
                yield
                dve.wait_ge(rank_sums, n + 1)
                link(nc.vector.scalar_tensor_tensor(d, B[7][:, 0:K], -1.0, d, ALU.add, ALU.subtract))
                ti = tot.bitcast(i32)
                link(nc.vector.tensor_scalar(ti, B[7][:, K:2 * K], float(P - 1), None, ALU.add))
                link(nc.vector.tensor_scalar(ti, ti, 7, None, ALU.arith_shift_right))
                link(nc.vector.tensor_copy(tiles, ti))
                link(nc.vector.tensor_tensor_scan(tinc, tiles, tiles, 0.0, ALU.add, ALU.max))
                link(nc.vector.tensor_tensor(tmp, tinc, tiles, ALU.subtract))
                link(nc.vector.scalar_tensor_tensor(d, tmp, float(P), d, ALU.mult, ALU.add))
                for lo, hi in zip((0,) + cuts, cuts + (T,)):
                    c, o, r, n = cumv[:, :, lo:hi], ohv[:, :, lo:hi], row[:, lo:hi], hi - lo
                    link(nc.vector.tensor_tensor(c, c, d.unsqueeze(2).to_broadcast([P, K, n]), ALU.add))
                    link(nc.vector.tensor_tensor(c, c, o, ALU.mult))
                    link(nc.vector.tensor_reduce(r.bitcast(fp32), c.rearrange("p k t -> p t k"), X, ALU.add))
                    if filling is not None:
                        last = r[:, n // 2 - 1::n // 2].bitcast(fp32)
                        link(nc.vector.tensor_tensor(last, last, filling, ALU.add))
                    link(nc.vector.tensor_copy(r, r.bitcast(fp32)))
                    if swizzle:
                        q, j = ohv[:, 0, lo:hi].bitcast(i32), ohv[:, 1, lo:hi].bitcast(i32)
                        link(nc.vector.tensor_scalar(q, r, P - 1, None, ALU.bitwise_and))
                        link(nc.vector.tensor_scalar(j, r, 7, None, ALU.arith_shift_right))
                        link(nc.vector.scalar_tensor_tensor(r, q, float(slots), j, ALU.mult, ALU.add))
                    yield
                own = area[0:1, 0:slots * K].rearrange("p (j k) -> p j k", k=K)
                link(nc.vector.tensor_tensor(own, iota_r[0:1, 0:slots].unsqueeze(2).to_broadcast([1, slots, K]),
                                             tinc[0:1, :].unsqueeze(1).to_broadcast([1, slots, K]), ALU.is_ge))
                own_f = cum[0:1, K * T - slots:K * T]
                link(nc.vector.tensor_reduce(own_f, own, X, ALU.add))
                link(nc.vector.tensor_scalar(owner, own_f, float(K - 1), float(scale), ALU.min, ALU.mult))

            lns = [0]

            def norm_columns():
                me, ve, mo, vo = (stats[:, :, i] for i in (1, 2, 4, 5))
                link(nc.vector.tensor_tensor(t0, me, mo, ALU.add))
                link(nc.vector.tensor_scalar(mean, t0, 0.5, None, ALU.mult))
                link(nc.vector.tensor_tensor(t1, me, mo, ALU.subtract))
                link(nc.vector.scalar_tensor_tensor(t1, t1, 0.25, t1, ALU.mult, ALU.mult))
                link(nc.vector.tensor_tensor(t0, ve, vo, ALU.add))
                link(nc.vector.scalar_tensor_tensor(t0, t0, 1.0 / C, t1, ALU.mult, ALU.add))
                nc.vector.tensor_scalar(var, t0, EPS, None, ALU.add).then_inc(var_ready, 1)
                lns[0] += 1
                dve.wait_ge(root_ready, lns[0])
                link(nc.vector.reciprocal(t0, root))
                link(nc.vector.tensor_tensor(t1, t0, t0, ALU.mult))
                link(nc.vector.scalar_tensor_tensor(t1, var, -0.5, t1, ALU.mult, ALU.mult))
                link(nc.vector.scalar_tensor_tensor(rstd, t1, 1.5, t0, ALU.add, ALU.mult))

            def normalise(o, i, t):
                return nc.vector.tensor_scalar(o, i, mean[:, ds(t, 1)], rstd[:, ds(t, 1)], ALU.subtract, ALU.mult)

            def tile_of(a, t):
                return a[:, ds(t * C, C)]

            dve.wait_ge(src_in, 16)
            dve.wait_ge(constants, CONSTANTS)
            link(nc.vector.tensor_scalar(src_part, row_e[:, :], P - 1, None, ALU.bitwise_and))
            link(nc.vector.tensor_copy(rec[:, :, 1].bitcast(fp32), src_part))
            link(nc.vector.tensor_scalar(src_part, row_e[:, :], 7, None, ALU.arith_shift_right))
            link(nc.vector.tensor_copy(key_e, src_part))
            r = rank(key_e, TT, EC, EDGE_SLOTS, oh_e, cum_e, row_e[:, :], True, edge_owner[:, :], C, cuts=(2 * HS,))
            next(r)
            dve.wait_ge(edges_in, 32)
            link(nc.vector.tensor_copy(rec[:, :, 0], dst_in))
            link(nc.vector.tensor_copy(rec[:, :, 2].bitcast(fp32), weight_in))
            for _ in range(2):
                next(r)
                dve.sem_inc(edge_rows, 1)
            for _ in r:
                pass

            dve.wait_ge(weights_in, 16 * 15)
            for v in range(2):
                for k in range(KC):
                    nc.vector.tensor_copy(vbc[:, v, k, :], vecs[:, 1 + v, k:k + 1].to_broadcast([P, P])) \
                        .then_inc(fold_inputs, 1)
            for k in range(KC):
                dve.wait_ge(fold_products, k + 1)
                nc.vector.tensor_copy(wraw[:, k, :], B[k][:, 0:QKV]).then_inc(fold_inputs, 1)
            dve.wait_ge(fold_inputs, 6)
            for k in range(KC):
                link(nc.vector.tensor_scalar(wfold[:, k, :], wraw[:, k, :], vecs[:, 0, k:k + 1], None, ALU.mult))
            dve.wait_ge(bias_product, 1)
            nc.vector.tensor_copy(bqkv[:, :], B[2][:, 0:QKV]).then_inc(folded, 1)
            dve.wait_ge(b1_product, 1)
            link(nc.vector.tensor_tensor(b1[:, :], B[6][:, 0:FT], b1[:, :], ALU.add))
            for k in range(KC):
                link(nc.vector.tensor_scalar(w1[:, k, :], w1[:, k, :], vecs[:, 3, k:k + 1], None, ALU.mult))
            nc.vector.memset(q_ring[:, :, HR:P], 1.0).then_inc(mlp_weights, 1)

            dve.wait_ge(x_in, 16)
            with dve.Fori(0, TT // CH) as c:
                for i in range(CH):
                    t = c * CH + i
                    nc.vector.bn_stats(stats[:, ds(t, 1), :], tile_of(xs, t)).then_inc(x_stats, 1)
            dve.wait_ge(x_stats, TT)
            norm_columns()
            with dve.Fori(0, TT // CH) as c:
                for i in range(CH):
                    normalise(tile_of(M, c * CH + i), tile_of(xs, c * CH + i), c * CH + i).then_inc(xn_ready, 1)
                for i in range(CH):
                    t = c * CH + i
                    dve.wait_ge(xn_ready, t + 1)
                    nc.vector.bn_stats(stats[:, ds(t, 1), :], tile_of(M, t)).then_inc(x_stats, 1)
            dve.wait_ge(x_stats, 2 * TT)
            norm_columns()

            def z_tile(t, s):
                dve.wait_ge(transposed, t + 1)
                normalise(z_ring[:, s, :], tile_of(M, t), t).then_inc(z_ready, 1)

            def products_out(t, s):
                dve.wait_ge(token_products, t + 1)
                nc.vector.tensor_copy(tile_of(sup_all, t), B[2 + s][:, 0:C]).then_inc(support_ready, 1)
                nc.vector.tensor_tensor(qkv[:, ds(t, 1), :], B[4 + s][:, 0:QKV].unsqueeze(1), bqkv.unsqueeze(1),
                                        ALU.add).then_inc(qkv_ready, 1)
                nc.vector.tensor_tensor(tile_of(xs, t), tile_of(xs, t), b2[:, :], ALU.add).then_inc(x_plus_b2, 1)

            dve.wait_ge(folded, 1)
            dve.sem_inc(transposed, 2)
            dve.sem_inc(support_ready, 2)
            dve.sem_inc(qkv_ready, 2)
            staggered(dve, z_tile, products_out, first=z_tile)
            dve.wait_ge(qkv_ready, TT + 2)

            q_v = qkv[:, :, C:C + HR]
            k_v = qkv[:, :, C + HR:QKV]
            link(nc.vector.tensor_scalar(k_v[:, TT - 1, :], k_v[:, TT - 1, :], padneg[:, 0:1], None, ALU.add))
            nc.vector.tensor_reduce(kmax[:, :], k_v.rearrange("p t c -> p c t"), X, ALU.max).then_inc(kmax_ready, 1)
            dve.wait_ge(kmax_transposed, 1)
            link(nc.vector.tensor_reduce(kmax_t[:, :], B[6][0:HR, 0:P], X, ALU.max))
            nc.vector.tensor_scalar(diag[:, :], ident[0:HR, 0:HR], kmax_t[:, 0:1], None, ALU.mult).then_inc(kmax_diagonal, 1)
            q4 = q_v.rearrange("p t (h r) -> p t h r", r=KR)
            link(nc.vector.tensor_reduce(q_red[:, :, :], q4, X, ALU.max))
            nc.vector.tensor_tensor(q4, q4, q_red[:, :, :].unsqueeze(3).to_broadcast([P, TT, HEADS, KR]),
                                    ALU.subtract).then_inc(exp_input, 1)
            dve.wait_ge(kmax_spread, 1)
            nc.vector.tensor_tensor(k_v, k_v, B[7][:, 0:HR].unsqueeze(1).to_broadcast([P, TT, HR]),
                                    ALU.subtract).then_inc(exp_input, 1)
            dve.wait_ge(exp_done, 1)
            nc.vector.tensor_reduce(kmax[:, :], k_v.rearrange("p t c -> p c t"), X, ALU.add).then_inc(k_summed, 1)
            link(nc.vector.tensor_reduce(q_red[:, :, :], q4, X, ALU.add))
            link(nc.vector.reciprocal(q_red[:, :, :], q_red[:, :, :]))
            dve.wait_ge(kv_product, 1)
            link(nc.vector.reciprocal(kden[:, :], B[4][:, 0:HR]))
            for k in range(KC):
                link(nc.vector.tensor_tensor(kvT[:, k, :], B[2 + k][:, 0:HR],
                                             kvmask[:, k, :, :].rearrange("p h r -> p (h r)"), ALU.mult))
                nc.vector.tensor_tensor(kvT[:, k, :], kvT[:, k, :], kden[:, :], ALU.mult).then_inc(kv_ready, 1)
            dve.wait_ge(attn_product, 1)
            nc.vector.tensor_copy(attn_w[0:HR, :], B[5][0:HR, 0:C]).then_inc(attn_weights, 1)

            def q_tile(t, s):
                dve.wait_ge(q_transposed, t + 1)
                nc.vector.tensor_tensor(q_ring[:, s, 0:HR].rearrange("p (h r) -> p h r", r=KR),
                                        qkv[:, ds(t, 1), C:C + HR].rearrange("p o (h r) -> p (o h) r", r=KR),
                                        q_red[:, ds(t, 1), :].rearrange("p o h -> p (o h)").unsqueeze(2)
                                        .to_broadcast([P, HEADS, KR]), ALU.mult).then_inc(q_ready, 1)

            def fx_tile(t, s):
                dve.wait_ge(attn_rows, t + 1)
                nc.vector.tensor_tensor(tile_of(M, t), B[2 + s][:, 0:C], tile_of(M, t), ALU.add).then_inc(residual_ready, 1)
                dve.wait_ge(residual_ready, t + 3)
                nc.vector.bn_stats(stats[:, ds(t, 1), :], tile_of(M, t)).then_inc(x_stats, 1)

            dve.sem_inc(q_transposed, 2)
            dve.sem_inc(residual_ready, 2)
            staggered(dve, q_tile, fx_tile, first=q_tile)
            dve.wait_ge(x_stats, 3 * TT)
            norm_columns()

            def z2_tile(t, s):
                dve.wait_ge(z2_transposed, t + 1)
                normalise(z_ring[:, s, :], tile_of(M, t), t).then_inc(z2_ready, 1)

            dve.wait_ge(x_plus_b2, TT)
            dve.sem_inc(z2_transposed, 2)
            pairs(dve, z2_tile)
            dve.wait_ge(z2_ready, TT)
            nc.vector.tensor_tensor(M[:, :], M[:, :], xs, ALU.add).then_inc(mix_residual, 1)
            dve.wait_ge(mix_residual, 1)

            dve.sem_inc(down_added, 4)
            with dve.Fori(0, TT // CH) as c:
                for i in range(CH):
                    dve.wait_ge(down_product, c * CH + i + 1)
                    nc.vector.tensor_tensor(tile_of(M, c * CH + i), B[4 + i % 4][:, 0:C], tile_of(M, c * CH + i),
                                            ALU.add).then_inc(down_added, 1)
            dve.wait_ge(down_added, 4 + TT)

            tabw = tab[:, :].bitcast(fp32)

            def onehots(col, h):
                for k in range(HALF):
                    at = (col + k) * RECORD
                    nc.vector.tensor_scalar(S[:, h * HALF + k, :], iota_r[:, 0:P], tabw[:, ds(at + 1, 1)],
                                            tabw[:, ds(at + 2, 1)], ALU.is_equal, ALU.mult).then_inc(edge_onehots, 1)

            def add_up(col, offsets):
                for k in range(HALF):
                    dve.wait_ge(edge_products, col + k + 1)
                    dve.wait_ge(acc_added, col + k - 1 + HALF)
                    part = (acc, acc_odd)[k % 2][:, ds(offsets[k], C)]
                    nc.vector.tensor_tensor(part, B[k][:, 0:C], part, ALU.add).then_inc(acc_added, 1)

            nc.vector.memset(acc_odd, 0.0).then_inc(acc_odd_zeroed, 1)
            dve.wait_ge(acc_odd_zeroed, 1)
            dve.wait_ge(records_in, 16)
            dve.wait_ge(routed_zeroed, 16 * zero_stores)
            dve.wait_ge(records_zeroed, 16)
            dve.sem_inc(acc_added, HALF)
            onehots(0, 0)
            with dve.Fori(0, EDGE_SLOTS // (2 * HALF)) as i:
                onehots(2 * i * HALF + HALF, 1)
                _, offsets = nc.values_load_multi_w_load_instructions(
                    edge_owner[0:1, ds(2 * i * HALF, 2 * HALF)], engines=[mybir.EngineType.DVE],
                    min_val=0, max_val=(TT - 1) * C)
                add_up(2 * i * HALF, offsets[:HALF])
                onehots(2 * i * HALF + 2 * HALF, 0)
                add_up(2 * i * HALF + HALF, offsets[HALF:])
            dve.wait_ge(acc_added, EDGE_SLOTS + HALF)

            with dve.Fori(0, TT // CH) as c:
                part = ds(c * CH * C, CH * C)
                nc.vector.tensor_tensor(acc[:, part], acc[:, part], acc_odd[:, part], ALU.add).then_inc(sums_joined, 1)
                dve.wait_ge(sums_joined, c + 1)
                nc.vector.scalar_tensor_tensor(M[:, part], acc[:, part], 0.0, M[:, part], ALU.max, ALU.add) \
                    .then_inc(x1_ready, 1)
                dve.wait_ge(x1_ready, c + 1)
                for i in range(CH):
                    nc.vector.bn_stats(stats[:, ds(c * CH + i, 1), :], tile_of(M, c * CH + i)).then_inc(x_stats, 1)
            dve.wait_ge(x_stats, 4 * TT)
            norm_columns()
            nc.vector.scalar_tensor_tensor(shift, mean, -1.0, rstd, ALU.mult, ALU.mult).then_inc(norm2_columns, 1)
            link(nc.vector.tensor_copy(routed[:, :, C], token_ids[:, :]))

            dve.wait_ge(router_product, RP + 2)
            top, total = small[:, 0:2, :], small[:, 2, :]

            def wide(a):
                return a.unsqueeze(2).to_broadcast([P, TT, EXPERTS])

            experts = iota_r[:, 0:EXPERTS].unsqueeze(1).to_broadcast([P, TT, EXPERTS])
            products = B[3][:, 0:TT * EXPERTS].rearrange("p (t e) -> p t e", e=EXPERTS)
            r_sums = B[3][:, TT * EXPERTS:(TT + 1) * EXPERTS].unsqueeze(1).to_broadcast([P, TT, EXPERTS])
            link(nc.vector.tensor_tensor(pick[:, 0, :, :], wide(mean), r_sums, ALU.mult))
            link(nc.vector.tensor_tensor(probs[:, :, :], products, pick[:, 0, :, :], ALU.subtract))
            link(nc.vector.tensor_tensor(probs[:, :, :], probs[:, :, :], wide(rstd), ALU.mult))
            link(nc.vector.tensor_reduce(top[:, 0, :], probs[:, :, :], X, ALU.max))
            nc.vector.tensor_tensor(probs[:, :, :], probs[:, :, :], wide(top[:, 0, :]), ALU.subtract).then_inc(exp_input, 1)
            dve.wait_ge(exp_done, 2)
            link(nc.vector.tensor_reduce(total, probs[:, :, :], X, ALU.add))
            link(nc.vector.reciprocal(total, total))
            link(nc.vector.tensor_tensor(probs[:, :, :], probs[:, :, :], wide(total), ALU.mult))
            for k in range(2):
                key = keys_m[:, k * TT:(k + 1) * TT]
                link(nc.vector.tensor_reduce(top[:, k, :], probs[:, :, :], X, ALU.max))
                link(nc.vector.tensor_tensor(pick[:, 0, :, :], probs[:, :, :], wide(top[:, k, :]), ALU.is_lt))
                link(nc.vector.scalar_tensor_tensor(pick[:, 0, :, :], pick[:, 0, :, :], float(EXPERTS), experts,
                                                    ALU.mult, ALU.add))
                link(nc.vector.tensor_reduce(key, pick[:, 0, :, :], X, ALU.min))
                if k == 0:
                    link(nc.vector.tensor_tensor(pick[:, 1, :, :], experts, wide(key), ALU.is_equal))
                    link(nc.vector.scalar_tensor_tensor(probs[:, :, :], pick[:, 1, :, :], -2.0, probs[:, :, :],
                                                        ALU.mult, ALU.add))
            link(nc.vector.tensor_tensor(total, top[:, 0, :], top[:, 1, :], ALU.add))
            link(nc.vector.tensor_scalar(total, total, 1e-9, None, ALU.add))
            link(nc.vector.reciprocal(total, total))
            for k in range(2):
                link(nc.vector.tensor_tensor(gates[:, k, :], top[:, k, :], total, ALU.mult))
            link(nc.vector.tensor_copy(routed[:, :, C + 1], gates[:, 0, :]))
            last_keys = keys_m[:, TT - 1::TT]
            link(nc.vector.tensor_scalar(last_keys, last_keys, pad_key[:, 0:1], None, ALU.add))
            r = rank(keys_m[:, :], EXPERTS, PICKS, MOE_SLOTS, oh_m, cum_m, row_m[:, :], False, slot_expert[:, :], 1, filling=pad_rows[:, :])
            next(r)
            next(r)
            dve.sem_inc(pick_rows, 1)
            for _ in r:
                pass
            dve.sem_inc(pick_rows, 1)
            for group, (lo, hi) in enumerate(((0, FIRST), (FIRST, TT))):
                dve.wait_ge(rows_routed[group], 16 * (hi - lo))
                nc.vector.tensor_copy(routed[:, lo:hi, C + 1], gates[:, 1, lo:hi]).then_inc(second_gates, 1)

            dve.sem_inc(half1_copied, 1)
            dve.sem_inc(down_copied, 1)

            def gate(j, a):
                dve.wait_ge((half0_silu, half1_silu)[a], j + 1)
                nc.vector.tensor_tensor(h_ring[:, a, :], g_ring[:, a, :], B[2 * a + 1][:, 0:HH], ALU.mult) \
                    .then_inc((half0_gated, half1_gated)[a], 1)

            def save_meta(j, s, arrivals):
                dve.wait_ge(slot_rows_in[s], 16 * arrivals)
                nc.vector.tensor_copy(slot_meta[:, ds(j, 1), :], ex_ring[:, s:s + 1, C:ROW]).then_inc(meta_saved, 1)

            def expert_rows(j, s, i, free=True, more=2):
                if more:
                    dve.wait_ge(half0_transposed, j + 1)
                    gate(j + 1, 0)
                dve.wait_ge(half1_transposed, j + 1)
                nc.vector.tensor_copy(hT_ring[:, 3:6, :].rearrange("p f c -> p (f c)"), B[5][0:HB, 0:3 * P]) \
                    .then_inc(half1_copied, 1)
                if more:
                    gate(j + 1, 1)
                if more == 2:
                    save_meta(j + 2, s, i + 2)
                if free:
                    dve.wait_ge(rows_added, 16 * (j - 1))
                nc.vector.tensor_scalar(slot_fill[:, s:s + 1], slot_meta[:, ds(j, 1), 0], 0.0, trash[:, 0:1],
                                        ALU.is_equal, ALU.mult).then_inc(slot_filled, 1)
                dve.wait_ge(slot_filled, 2 * j + 1)
                nc.vector.scalar_tensor_tensor(slot_token[:, s:s + 1], slot_meta[:, ds(j, 1), 0], -1.0,
                                               slot_fill[:, s:s + 1], ALU.add, ALU.add).then_inc(slot_filled, 1)
                dve.wait_ge(slot_filled, 2 * j + 2)
                dve.wait_ge(down_rows, j + 1)
                nc.vector.tensor_scalar(y_ring[:, s, :], B[7][:, 0:C], slot_meta[:, ds(j, 1), 1], None,
                                        ALU.mult).then_inc(down_copied, 1)

            save_meta(0, 0, 1)
            save_meta(1, 1, 1)
            gate(0, 0)
            gate(0, 1)
            expert_rows(0, 0, 0, free=False)
            expert_rows(1, 1, 0, free=False)
            with dve.Fori(1, MOE_SLOTS // 2 - 1) as i:
                for s in range(2):
                    expert_rows(2 * i + s, s, i)
            expert_rows(MOE_SLOTS - 2, 0, None, more=1)
            expert_rows(MOE_SLOTS - 1, 1, None, more=0)

        @block.scalar
        def _(act):
            roots = [0]

            def square_root():
                roots[0] += 1
                act.wait_ge(var_ready, roots[0])
                nc.scalar.activation(root, var, ACT.Sqrt).then_inc(root_ready, 1)

            square_root()
            square_root()

            def copy_xn(t, s):
                act.wait_ge(transposed, t + 1)
                nc.scalar.activation(xn_ring[:, s, :], M[:, ds(t * C, C)], ACT.Copy).then_inc(xn_copied, 1)

            def copy_transposes(t, s):
                act.wait_ge(transposed, t + 3)
                nc.scalar.activation(tr_ring[:, s, :, :].rearrange("p q c -> p (q c)"), B[s][:, :], ACT.Copy) \
                    .then_inc(transposes_copied, 1)

            act.wait_ge(folded, 1)
            act.sem_inc(transposes_copied, 2)
            staggered(act, copy_xn, copy_transposes)

            act.wait_ge(exp_input, 2)
            nc.scalar.activation(qkv[:, :, C:QKV], qkv[:, :, C:QKV], ACT.Exp).then_inc(exp_done, 1)

            def copy_q(t, s):
                act.wait_ge(q_transposed, t + 3)
                nc.scalar.activation(qT_ring[:, s, :], B[s][0:HR + 1, 0:P], ACT.Copy).then_inc(q_copied, 1)

            act.sem_inc(q_copied, 2)
            pairs(act, copy_q)
            square_root()
            act.wait_ge(support_stored, 16)

            def copy_z2(t, s):
                act.wait_ge(z2_transposed, t + 3)
                nc.scalar.activation(z2T[:, :, ds(t * P, P)], B[s][:, 0:C].rearrange("p (k n) -> p k n", k=KC),
                                     ACT.Copy).then_inc(z2_copied, 1)

            act.sem_inc(z2_copied, 2)
            pairs(act, copy_z2)

            act.wait_ge(mlp_weights, 1)
            act.sem_inc(gelu_done, 4)
            with act.Fori(0, TT // CH) as c:
                for f in range(FT):
                    for half in range(2):
                        act.wait_ge(up_product, 16 * c + 2 * f + half + 1)
                        nc.scalar.activation(hidT[:, f, half * CN:(half + 1) * CN], B[(2 * f + half) % 4][:, 0:CN],
                                             ACT.Gelu, bias=b1[:, f:f + 1]).then_inc(gelu_done, 1)


            def copy_x1T(r, s, n=2):
                act.wait_ge(x1_transposed, r + 1)
                act.wait_ge(router_product, r + 1)
                nc.scalar.activation(x1T_ring[:, s, 0:n, :, :].rearrange("p t k c -> p (t k c)"),
                                     B[s][:, 0:n * C], ACT.Copy).then_inc(x1_transposes_copied, 1)

            act.sem_inc(router_product, 2)
            act.sem_inc(x1_transposes_copied, 2)
            pairs(act, copy_x1T, TT // 2)
            copy_x1T(RP - 1, (RP - 1) % 2, n=TT % 2)
            square_root()
            act.wait_ge(exp_input, 3)
            nc.scalar.activation(probs[:, :, :], probs[:, :, :], ACT.Exp).then_inc(exp_done, 1)

            act.wait_ge(norm2_columns, 1)
            with act.Fori(0, TT // CH) as c:
                for i in range(CH):
                    t = c * CH + i
                    nc.scalar.activation(routed[:, ds(t, 1), 0:C], M[:, ds(t * C, C)].unsqueeze(1), ACT.Identity,
                                         scale=rstd[:, ds(t, 1)], bias=shift[:, ds(t, 1)]).then_inc(xn2_ready, 1)

            act.sem_inc(half0_copied, 1)

            def copy_slot(j, s):
                act.wait_ge(slot_transposed, j + 1)
                nc.scalar.activation(exT_ring[:, s, :, :].rearrange("p k c -> p (k c)"), B[6][:, 0:C], ACT.Copy) \
                    .then_inc(slot_copied, 1)

            def silu(j, a, first=False):
                act.wait_ge((half0_product, half1_product)[a], j + 1)
                if not first:
                    act.wait_ge((half0_gated, half1_gated)[a], j)
                nc.scalar.activation(g_ring[:, a, :], B[2 * a][:, 0:HH], ACT.Silu) \
                    .then_inc((half0_silu, half1_silu)[a], 1)

            def expert_copies(j, s, more=2):
                if more:
                    silu(j + 1, 0)
                act.wait_ge(half0_transposed, j + 1)
                nc.scalar.activation(hT_ring[:, 0:3, :].rearrange("p f c -> p (f c)"), B[4][0:HB, 0:3 * P],
                                     ACT.Copy).then_inc(half0_copied, 1)
                if more == 2:
                    copy_slot(j + 2, s)
                if more:
                    silu(j + 1, 1)

            copy_slot(0, 0)
            copy_slot(1, 1)
            silu(0, 0, first=True)
            silu(0, 1, first=True)
            pairs(act, expert_copies, MOE_SLOTS - 2)
            expert_copies(MOE_SLOTS - 2, 0, more=1)
            expert_copies(MOE_SLOTS - 1, 1, more=0)

        @block.tensor
        def _(pe):
            mm = nc.tensor.matmul
            ranked = [0]

            def count_sums(K):
                ranked[0] += 1
                pe.wait_ge(rank_counts, ranked[0])
                mm(B[7][:, 0:K], upper[:, :], small[:, 0, 0:K], start=True, stop=True)
                mm(B[7][:, K:2 * K], ones[:, :], small[:, 0, 0:K], start=True, stop=True).then_inc(rank_sums, 1)

            pe.wait_ge(constants, CONSTANTS)
            count_sums(TT)

            pe.wait_ge(weights_in, 16 * 15)
            for m in range(KC):
                for k in range(KC):
                    ins = mm(B[m][:, 0:QKV], wxt[:, k, m * P:(m + 1) * P], wqkv[:, k, :],
                             start=(k == 0), stop=(k == KC - 1))
                ins.then_inc(fold_products, 1)
            pe.wait_ge(fold_inputs, 6)
            for k in range(KC):
                mm(B[2][:, 0:QKV], vbc[:, 0, k, :], wraw[:, k, :], start=(k == 0), stop=False)
            for k in range(KC):
                ins = mm(B[2][:, 0:QKV], vbc[:, 1, k, :], wqkv[:, k, :], start=False, stop=(k == KC - 1))
            ins.then_inc(bias_product, 1)
            for f in range(FT):
                for k in range(KC):
                    ins = mm(B[6][:, f:f + 1], w1[:, k, f * P:(f + 1) * P], vecs[:, 4, k:k + 1],
                             start=(k == 0), stop=(k == KC - 1))
            ins.then_inc(b1_product, 1)
            pe.wait_ge(folded, 1)

            def transpose_tokens(t, s):
                pe.wait_ge(xn_copied, t + 1)
                pe.wait_ge(z_ready, t + 1)
                pe.wait_ge(transposes_copied, t + 1)
                for q, ring in enumerate((xn_ring, xn_ring, z_ring, z_ring)):
                    c = q % 2 * P
                    ins = nc.tensor.transpose(B[s][:, q * P:(q + 1) * P], ring[:, s, c:c + P], ident[:, :])
                ins.then_inc(transposed, 1)

            def token_product(t, s):
                pe.wait_ge(transposes_copied, t + 3)
                pe.wait_ge(support_ready, t + 1)
                pe.wait_ge(qkv_ready, t + 1)
                for k in range(KC):
                    mm(B[2 + s][:, 0:C], tr_ring[:, s, k, :], wg[:, k, :], start=(k == 0), stop=(k == KC - 1))
                for k in range(KC):
                    ins = mm(B[4 + s][:, 0:QKV], tr_ring[:, s, KC + k, :], wfold[:, k, :],
                             start=(k == 0), stop=(k == KC - 1))
                ins.then_inc(token_products, 1)

            staggered(pe, transpose_tokens, token_product)

            pe.wait_ge(kmax_ready, 1)
            nc.tensor.transpose(B[6][0:HR, 0:P], kmax[:, :], ident[:, :]).then_inc(kmax_transposed, 1)
            pe.wait_ge(kmax_diagonal, 1)
            mm(B[7][:, 0:HR], ones[0:HR, :], diag[:, :], start=True, stop=True).then_inc(kmax_spread, 1)
            pe.wait_ge(exp_done, 1)
            pe.wait_ge(qkv_ready, TT + 2)
            for t in range(TT):
                kt = qkv[:, t, C + HR:QKV]
                for b, left in ((2, qkv[:, t, 0:P]), (3, qkv[:, t, P:C])):
                    ins = mm(B[b][:, 0:HR], left, kt, start=(t == 0), stop=(t == TT - 1))
            pe.wait_ge(k_summed, 1)
            mm(B[4][:, 0:HR], ones[:, :], kmax[:, :], start=True, stop=True).then_inc(kv_product, 1)
            pe.wait_ge(kv_ready, KC)
            for k in range(KC):
                ins = mm(B[5][0:HR, 0:C], kvT[:, k, :], wo[:, k, :], start=(k == 0), stop=(k == KC - 1))
            ins.then_inc(attn_product, 1)
            pe.wait_ge(attn_weights, 1)

            def transpose_q(t, s):
                pe.wait_ge(q_ready, t + 1)
                pe.wait_ge(q_copied, t + 1)
                nc.tensor.transpose(B[s][:, 0:P], q_ring[:, s, :], ident[:, :]).then_inc(q_transposed, 1)

            def attn_product_of(t, s):
                pe.wait_ge(q_copied, t + 3)
                pe.wait_ge(residual_ready, t + 1)
                mm(B[2 + s][:, 0:C], qT_ring[:, s, :], attn_w[:, :], start=True, stop=True).then_inc(attn_rows, 1)

            staggered(pe, transpose_q, attn_product_of)

            def transpose_z2(t, s):
                pe.wait_ge(z2_ready, t + 1)
                pe.wait_ge(z2_copied, t + 1)
                for k in range(KC):
                    ins = nc.tensor.transpose(B[s][:, k * P:(k + 1) * P], z_ring[:, s, k * P:(k + 1) * P], ident[:, :])
                ins.then_inc(z2_transposed, 1)

            pairs(pe, transpose_z2)

            pe.wait_ge(mlp_weights, 1)
            pe.wait_ge(z2_copied, TT + 2)
            with pe.Fori(0, TT // CH) as c:
                for g in range(2 * FT):
                    f, half = g // 2, g % 2
                    pe.wait_ge(gelu_done, 2 * FT * c + g + 1)
                    for k in range(KC):
                        ins = mm(B[g % 4][:, 0:CN], w1[:, k, f * P:(f + 1) * P],
                                 z2T[:, k, ds(c * 2 * CN + half * CN, CN)], start=(k == 0), stop=(k == KC - 1))
                    ins.then_inc(up_product, 1)
                pe.wait_ge(gelu_done, 2 * FT * c + 2 * FT + 4)
                for i in range(CH):
                    pe.wait_ge(down_added, CH * c + (i + 1 if i else 4))
                    for f in range(FT):
                        ins = mm(B[4 + i % 4][:, 0:C], hidT[:, f, i * P:(i + 1) * P], w2[:, f, :],
                                 start=(f == 0), stop=(f == FT - 1))
                    ins.then_inc(down_product, 1)

            pe.wait_ge(down_added, 4 + TT)
            with pe.Fori(0, EDGE_SLOTS // (2 * HALF)) as i:
                for n in range(2 * HALF):
                    j, k = 2 * HALF * i + n, n % HALF
                    if k == 0:
                        pe.wait_ge(rows_gathered[n // HALF], 16 * HALF * (i + 1))
                    pe.wait_ge(edge_onehots, j + 1)
                    pe.wait_ge(acc_added, j + 1)
                    mm(B[k][:, 0:C], S[:, n, :], gathered[:, n, :], start=True, stop=True) \
                        .then_inc(edge_products, 1)

            def transpose_x1(r):
                tiles = range(2 * r, min(2 * r + 2, TT))
                pe.wait_ge(x1_ready, tiles[-1] // CH + 1)
                pe.wait_ge(x1_transposes_copied, r + 1)
                for i, t in enumerate(tiles):
                    for k in range(KC):
                        ins = nc.tensor.transpose(B[r % 2][:, (i * KC + k) * P:(i * KC + k + 1) * P],
                                                  M[:, t * C + k * P:t * C + (k + 1) * P], ident[:, :])
                ins.then_inc(x1_transposed, 1)

            def route(r):
                pe.wait_ge(x1_transposes_copied, r + 3)
                for i, t in enumerate(range(2 * r, min(2 * r + 2, TT))):
                    for k in range(KC):
                        ins = mm(B[3][:, t * EXPERTS:(t + 1) * EXPERTS], x1T_ring[:, r % 2, i, k, :], rt[:, k, :],
                                 start=(k == 0), stop=(k == KC - 1))
                ins.then_inc(router_product, 1)

            transpose_x1(0)
            for k in range(KC):
                mm(B[3][:, TT * EXPERTS:(TT + 1) * EXPERTS], ones[:, :], rt[:, k, :], start=(k == 0), stop=(k == KC - 1))
            for r in range(1, RP):
                transpose_x1(r)
                route(r - 1)
            route(RP - 1)
            count_sums(EXPERTS)
            pe.wait_ge(pick_rows, 2)

            def transpose_slot(j, s, arrivals, first=False):
                pe.wait_ge(slot_rows_in[s], 16 * arrivals)
                if not first:
                    pe.wait_ge(slot_copied, j)
                for k in range(KC):
                    ins = nc.tensor.transpose(B[6][:, k * P:(k + 1) * P], ex_ring[:, s, k * P:(k + 1) * P], ident[:, :])
                ins.then_inc(slot_transposed, 1)

            def up_half(e, j, s, a, first=False):
                pe.wait_ge(slot_copied, j + 1)
                if not first:
                    pe.wait_ge((half0_gated, half1_gated)[a], j)
                for part in (2 * a, 2 * a + 1):
                    for k in range(KC):
                        ins = mm(B[part][:, 0:HH], exT_ring[:, s, k, :],
                                 R1[:, ds(e * (KC * W13) + (k * W13 + part * HH), HH)],
                                 start=(k == 0), stop=(k == KC - 1))
                ins.then_inc((half0_product, half1_product)[a], 1)

            def transpose_half(j, a):
                pe.wait_ge((half0_gated, half1_gated)[a], j + 1)
                pe.wait_ge((half0_copied, half1_copied)[a], j + 1)
                for f in range(3):
                    ins = nc.tensor.transpose(B[4 + a][0:HB, f * P:(f + 1) * P], h_ring[:, a, f * HB:(f + 1) * HB],
                                              ident[:, :])
                ins.then_inc((half0_transposed, half1_transposed)[a], 1)

            def expert_of(j):
                return pe.value_load(slot_expert[0:1, ds(j, 1)], min_val=0, max_val=EXPERTS - 1)

            def down(j):
                e = expert_of(j)
                pe.wait_ge(half0_copied, j + 2)
                pe.wait_ge(half1_copied, j + 2)
                pe.wait_ge(down_copied, j + 1)
                for f in range(NHB):
                    ins = mm(B[7][:, 0:C], hT_ring[:, f, :], w2_e[:, ds(e * (NHB * C) + f * C, C)],
                             start=(f == 0), stop=(f == NHB - 1))
                ins.then_inc(down_rows, 1)

            def expert(j, s, i=None, more=2):
                if more:
                    e = expert_of(j + 1)
                    up_half(e, j + 1, 1 - s, 0)
                for a in range(2):
                    transpose_half(j, a)
                if more == 2:
                    transpose_slot(j + 2, s, i + 2)
                if more:
                    up_half(e, j + 1, 1 - s, 1)
                down(j)

            pe.wait_ge(experts_up_in, 16 * (UP_LOADS + 1))
            transpose_slot(0, 0, 1, first=True)
            transpose_slot(1, 1, 1)
            e0 = expert_of(0)
            up_half(e0, 0, 0, 0, first=True)
            up_half(e0, 0, 0, 1, first=True)
            pe.wait_ge(experts_down_in, 32)
            with pe.Fori(0, MOE_SLOTS // 2 - 1) as i:
                for s in range(2):
                    expert(2 * i + s, s, i)
            expert(MOE_SLOTS - 2, 0, more=1)
            expert(MOE_SLOTS - 1, 1, more=0)


def kernel(**inputs):
    import numpy as np
    import concourse.bacc as bacc
    from concourse.bass_utils import run_bass_kernel_spmd

    a = {k: np.asarray(v) for k, v in inputs.items()}

    def by_partition(v, dt=np.float32):
        return np.ascontiguousarray(v.reshape(-1, P).T)

    xp = np.zeros((TOKENS, C), np.float32)
    xp[:NODES] = a["x"]

    def edges(v):
        e = np.zeros(P * EC, v.dtype)
        e[:EDGES] = v
        return e.reshape(P, EC)

    w_qkv = np.zeros((C, QKV), np.float32)
    for h in range(HEADS):
        rows = slice(h * DH, (h + 1) * DH)
        w_qkv[rows, h * DH:(h + 1) * DH] = a["L0_mix_Wv"]
        w_qkv[rows, C + h * KR:C + (h + 1) * KR] = a["L0_mix_Wq"]
        w_qkv[rows, C + HR + h * KR:C + HR + (h + 1) * KR] = a["L0_mix_Wk"]

    up = np.zeros((2, EXPERTS, 2 * HH, C), np.float32)
    up[0, :, :H], up[1, :, :H] = a["L0_ffn_w1"], a["L0_ffn_w3"]
    up = up.reshape(2, EXPERTS, 2, HH, KC, P)
    w_13 = np.ascontiguousarray(up.transpose(5, 1, 4, 2, 0, 3)).reshape(P, EXPERTS, KC * W13)
    down = np.zeros((EXPERTS, C, 2 * HH), np.float32)
    down[:, :, :H] = a["L0_ffn_w2"]
    w_down = np.ascontiguousarray(down.reshape(EXPERTS, C, NHB, HB).transpose(3, 0, 2, 1)).reshape(HB, -1)

    arrays = {
        "x": xp, "src": edges(a["src"]), "dst": edges(a["dst"]), "edge_w": edges(a["edge_weight"]),
        "w_gnn": a["L0_gnn_weight"], "wx_t": np.ascontiguousarray(a["L0_mix_Wx"].T), "w_qkv": w_qkv,
        "ln1_g": by_partition(a["L0_mix_ln1_g"]), "ln1_b": by_partition(a["L0_mix_ln1_b"]),
        "bx": by_partition(a["L0_mix_bx"]), "w_o": a["L0_mix_Wo"], "b_o": a["L0_mix_bo"].reshape(1, C),
        "ln2_g": by_partition(a["L0_mix_ln2_g"]), "ln2_b": by_partition(a["L0_mix_ln2_b"]),
        "w_1": a["L0_mix_W1"], "b_1": by_partition(a["L0_mix_b1"]), "w_2": a["L0_mix_W2"], "b_2": a["L0_mix_b2"],
        "router_t": np.ascontiguousarray(a["L0_ffn_router_w"].T), "w_13": w_13, "w_down": w_down,
    }
    nc = bacc.Bacc("TRN2", target_bir_lowering=False, num_devices=1)
    aps = {k: nc.dram_tensor(f"in_{k}", v.shape, mybir.dt.from_np(v.dtype), kind="ExternalInput").ap()
           for k, v in arrays.items()}
    out = nc.dram_tensor("out_rows_dram", (NODES, C), mybir.dt.float32, kind="ExternalOutput").ap()
    gps_layer(nc, out=out, **aps)
    r = run_bass_kernel_spmd(nc, [{f"in_{k}": v for k, v in arrays.items()}], core_ids=[0])
    return r.results[0]["out_rows_dram"]
```

```python
import concourse.bass as bass
from concourse import mybir
from contextlib import ExitStack

P = 128
NODES, C, EDGES = 3125, 256, 50000
KC = C // P
TT = -(-NODES // P)
TOKENS = TT * P
LAST = NODES - (TT - 1) * P
EC = 392
HEADS, DH, KR = 8, 32, 4
HR = HEADS * KR
QKV = C + 2 * HR
FF = 4 * C
FT = FF // P
EXPERTS, H = 8, 682
HB = 114
NHB = 6
HH = HB * NHB // 2
W13 = 4 * HH
EPS = 1e-5
RECORD = 3
EDGE_SLOTS = (P * EC + TT * (P - 1)) // P
PICKS = 2 * TT
MOE_SLOTS = (2 * NODES + EXPERTS * (P - 1)) // P
HS = 49
HALF = 8
NEG = -1.0e30
CONSTANTS = 16
UP_LOADS = 16
SPREAD = 8


def gps_layer(nc, x, src, dst, edge_w, w_gnn, wx_t, w_qkv, ln1_g, ln1_b, bx, w_o, b_o, ln2_g, ln2_b,
              w_1, b_1, w_2, b_2, router_t, w_13, w_down, out):
    fp32, i32, u32 = mybir.dt.float32, mybir.dt.int32, mybir.dt.uint32
    ALU = mybir.AluOpType
    ACT = mybir.ActivationFunctionType
    X = mybir.AxisListType.X
    ds = bass.ds

    support_d = nc.dram_tensor("support_scratch", (TOKENS, C), fp32).ap()
    records_d = nc.dram_tensor("records_scratch", (P * EDGE_SLOTS, RECORD), i32).ap()
    xn2_d = nc.dram_tensor("normalised_scratch", (TOKENS, C), fp32).ap()
    sum_d = nc.dram_tensor("sum_scratch", (TOKENS + P, C), fp32).ap()

    ctx = ExitStack()
    with ctx:
        def sb(name, shape, dt=fp32):
            return ctx.enter_context(nc.sbuf_tensor(name, shape, dt))

        def sem(name):
            return ctx.enter_context(nc.semaphore(name))

        MXA = sb("MXA", [P, 3 * TT * C])
        M = MXA[:, 0:TT * C]
        XA = MXA[:, TT * C:]
        w2_e = MXA[0:HB, 0:EXPERTS * NHB * C]
        R1 = sb("R1", [P, EXPERTS * KC * W13])
        xs = XA[:, 0:TT * C]
        acc = XA[:, TT * C:2 * TT * C]
        qkv = R1[:, 0:TT * QKV].rearrange("p (t c) -> p t c", c=QKV)
        z2T = R1[:, TT * QKV:TT * QKV + KC * TOKENS].rearrange("p (k n) -> p k n", k=KC)
        CH = 5
        CN = CH * P // 2
        hid0 = TT * QKV + KC * TOKENS
        hidT = R1[:, hid0:hid0 + FT * CH * P].rearrange("p (f n) -> p f n", f=FT)
        odd0 = EXPERTS * KC * W13 - TT * C
        behind = hid0 + FT * CH * P
        assert odd0 % UP_LOADS == 0 and odd0 < behind
        acc_odd = R1[:, odd0:]
        gathered = XA[:, 0:2 * HALF * C].rearrange("p (s c) -> p s c", c=C)
        S = XA[:, 2 * HALF * C:2 * HALF * C + 2 * HALF * P].rearrange("p (s c) -> p s c", c=P)
        sup_all = R1[:, TT * QKV:TT * QKV + TT * C]
        oh_e = R1[:, 0:2 * TT * EC]
        cum_e = R1[:, TT * EC:2 * TT * EC]
        dst_in = M[:, 0:EC].bitcast(i32)
        weight_in = M[:, EC:2 * EC]
        src_part = M[:, 2 * EC:3 * EC].bitcast(i32)
        key_e = M[:, 3 * EC:4 * EC]
        token_rings = R1[:, hid0:hid0 + FT * CH * P]
        xn_ring = token_rings[:, 0:512].rearrange("p (s c) -> p s c", s=2)
        z_ring = token_rings[:, 512:1024].rearrange("p (s c) -> p s c", s=2)
        tr_ring = token_rings[:, 1024:2048].rearrange("p (s q c) -> p s q c", s=2, c=P)
        q_ring = token_rings[:, 4096:4096 + 2 * P].rearrange("p (s c) -> p s c", s=2)
        qT_ring = token_rings[0:HR + 1, 2200:2456].rearrange("p (s c) -> p s c", s=2)
        wraw = token_rings[:, 2456:2456 + KC * QKV].rearrange("p (k n) -> p k n", k=KC)
        wfold = token_rings[:, 3096:3096 + KC * QKV].rearrange("p (k n) -> p k n", k=KC)
        bqkv = token_rings[:, 3736:3736 + QKV]
        tail = R1[:, 2 * TT * EC:]
        wxt = tail[:, 0:KC * C].rearrange("p (k n) -> p k n", k=KC)
        wqkv = tail[:, 512:512 + KC * QKV].rearrange("p (k n) -> p k n", k=KC)
        vbc = tail[:, 1152:1664].rearrange("p (v k c) -> p v k c", v=2, k=KC)
        wo = tail[:, 1664:2176].rearrange("p (k n) -> p k n", k=KC)

        ident = sb("ident", [P, P])
        upper = sb("upper", [P, P])
        ones = sb("ones", [P, P])
        iota_r = sb("iota_r", [P, EDGE_SLOTS])
        padneg = sb("padneg", [P, 1])
        kvmask = sb("kvmask", [P, KC, HEADS, KR])
        wg = sb("wg", [P, KC, C])
        vecs = sb("vecs", [P, 5, KC])
        kvT = sb("kvT", [P, KC, HR])
        attn_w = sb("attn_w", [HR + 1, C])
        WM = sb("WM", [P, KC * FF + FT * C])
        w1 = WM[:, 0:KC * FF].rearrange("p (k n) -> p k n", k=KC)
        w2 = WM[:, KC * FF:].rearrange("p (f n) -> p f n", f=FT)
        b1 = sb("b1", [P, FT])
        b2 = sb("b2", [P, C])
        rt = sb("rt", [P, KC, EXPERTS])
        rec = sb("rec", [P, EC, RECORD], i32)
        row_e = sb("row_e", [P, EC], i32)
        tab = sb("tab", [P, EDGE_SLOTS * RECORD], i32)
        stage_i = sb("stage_i", [P, 2, HS], i32)
        turn_rows = sb("turn_rows", [P, 2, 2 * HALF], i32)
        stage_r = sb("stage_r", [P, 2, HS, RECORD], i32)
        edge_owner = sb("edge_owner", [1, EDGE_SLOTS], i32)
        slot_expert = sb("slot_expert", [1, MOE_SLOTS], i32)
        stats = sb("stats", [P, TT, 6])
        ln = sb("ln", [P, 8, TT])
        mean, var, rstd, t0, t1, root, shift = (ln[:, i, :] for i in range(7))
        small = sb("small", [P, 8, TT])
        probs = sb("probs", [P, TT, EXPERTS])
        pick = sb("pick", [P, 2, TT, EXPERTS])
        keys_m = sb("keys_m", [P, PICKS])
        row_m = sb("row_m", [P, PICKS], i32)
        gates = sb("gates", [P, 2, TT])
        q_red = sb("q_red", [P, TT, HEADS])
        kmax = sb("kmax", [P, HR])
        kmax_t = sb("kmax_t", [HR, 1])
        diag = sb("diag", [HR, HR])
        kden = sb("kden", [P, HR])
        token_ids = sb("token_ids", [P, TT])
        pad_key = sb("pad_key", [P, 1])
        pad_rows = sb("pad_rows", [P, 2])
        trash = sb("trash", [P, 1])
        slot_q = sb("slot_q", [P, PICKS])
        slot_j = sb("slot_j", [P, PICKS])
        slot_src = sb("slot_src", [P, MOE_SLOTS], i32)
        slot_dst = sb("slot_dst", [P, MOE_SLOTS], i32)
        slot_gate = sb("slot_gate", [P, MOE_SLOTS])
        slot_fill = sb("slot_fill", [P, MOE_SLOTS])
        warm = sb("warm", [P, 2])
        src_ring = sb("src_ring", [P, 2], i32)
        dst_ring = sb("dst_ring", [P, 2], i32)
        RP = -(-TT // 2)
        x1T_ring = WM[:, 0:4 * C].rearrange("p (s t k c) -> p s t k c", s=2, t=2, k=KC)
        oh_m = WM[:, 1024:1024 + MOE_SLOTS * EXPERTS]
        cum_m = WM[:, 1600:1600 + EXPERTS * PICKS]
        pick_q = WM[:, 0:2 * SPREAD * P].rearrange("p (n q) -> p n q", q=P)
        pick_j = acc[:, 0:PICKS * 2 * MOE_SLOTS].rearrange("p (n a j) -> p n a j", a=2, j=MOE_SLOTS)
        ex_ring = WM[:, 0:2 * C].rearrange("p (s c) -> p s c", s=2)
        exT_ring = WM[:, 512:1024].rearrange("p (s k c) -> p s k c", s=2, k=KC)
        h_ring = WM[:, 1024:1024 + 2 * HH].rearrange("p (a c) -> p a c", a=2)
        g_ring = WM[:, 1712:1712 + 2 * HH].rearrange("p (a c) -> p a c", a=2)
        hT_ring = WM[0:HB, 2400:2400 + NHB * P].rearrange("p (f c) -> p f c", f=NHB)
        y_ring = WM[:, 3200:3712].rearrange("p (s c) -> p s c", s=2)

        B = [ctx.enter_context(nc.psum_tensor(f"bank{i}", [P, 512], fp32)) for i in range(8)]

        edges_in, x_in, weights_in, constants, acc_zeroed, records_zeroed = (
            sem(n) for n in "edges_in x_in weights_in constants acc_zeroed records_zeroed".split())
        trash_zeroed, rank_counts, rank_sums, edge_rows, staged, records_in = (
            sem(n) for n in "trash_zeroed rank_counts rank_sums edge_rows staged records_in".split())
        support_stored, gather_staged, edge_onehots, edge_products, acc_added, vector_step = (
            sem(n) for n in "support_stored gather_staged edge_onehots edge_products acc_added vector_step".split())
        x_stats, var_ready, root_ready, xn_ready, xn_copied, z_ready = (
            sem(n) for n in "x_stats var_ready root_ready xn_ready xn_copied z_ready".split())
        transposed, transposes_copied, token_products, support_ready, qkv_ready, x_plus_b2 = (
            sem(n) for n in "transposed transposes_copied token_products support_ready qkv_ready x_plus_b2".split())
        fold_products, fold_inputs, bias_product, folded, kmax_ready, kmax_transposed = (
            sem(n) for n in "fold_products fold_inputs bias_product folded kmax_ready kmax_transposed".split())
        kmax_diagonal, kmax_spread, exp_input, exp_done, kv_product, kv_ready = (
            sem(n) for n in "kmax_diagonal kmax_spread exp_input exp_done kv_product kv_ready".split())
        attn_product, attn_weights, q_ready, q_transposed, q_copied, attn_rows = (
            sem(n) for n in "attn_product attn_weights q_ready q_transposed q_copied attn_rows".split())
        residual_ready, z2_ready, z2_transposed, z2_copied, mix_residual, b1_product = (
            sem(n) for n in "residual_ready z2_ready z2_transposed z2_copied mix_residual b1_product".split())
        mlp_weights, up_product, gelu_done, down_product, down_added, x1_ready = (
            sem(n) for n in "mlp_weights up_product gelu_done down_product down_added x1_ready".split())
        xn2_ready, x1_transposed, x1_transposes_copied, router_product = (
            sem(n) for n in "xn2_ready x1_transposed x1_transposes_copied router_product".split())
        picks_spread, pick_onehots, experts_up_in, experts_down_in, slot_transposed, slot_copied = (
            sem(n) for n in "picks_spread pick_onehots experts_up_in experts_down_in slot_transposed slot_copied".split())
        half0_product, half1_product, half0_silu, half1_silu, half0_gated, half1_gated = (
            sem(n) for n in "half0_product half1_product half0_silu half1_silu half0_gated half1_gated".split())
        half0_transposed, half1_transposed, half0_copied, half1_copied, down_rows, down_copied = (
            sem(n) for n in "half0_transposed half1_transposed half0_copied half1_copied down_rows down_copied".split())
        norm2_columns, x1_stored, rows_added, out_stored, xn2_stored = (
            sem(n) for n in "norm2_columns x1_stored rows_added out_stored xn2_stored".split())
        stages_seen = sem("stages_seen")
        acc_odd_zeroed, sums_joined, k_summed, map_products, slots_known, slot_places, rows_staged = (
            sem(n) for n in "acc_odd_zeroed sums_joined k_summed map_products slots_known slot_places rows_staged".split())
        src_in, dst_staged, x_free, second_spread, picks_by_tile, slot_filled = (
            sem(n) for n in ("src_in dst_staged x_free second_spread picks_by_tile"
                             " slot_filled").split())
        records_scattered = [sem(f"records_scattered{h}") for h in range(2)]
        rows_gathered = [sem(f"rows_gathered{h}") for h in range(2)]
        slot_rows_in = [sem(f"slot_rows_in{h}") for h in range(2)]

        def pairs(engine, body, n=TT):
            with engine.Fori(0, n // 2) as i:
                body(2 * i, 0)
                body(2 * i + 1, 1)
            if n % 2:
                body(n - 1, 0)

        def staggered(engine, ahead, behind, first=None):
            def both(t, s):
                steps = (lambda: ahead(t + 2, s)), (lambda: behind(t, s))
                for run in steps if first is ahead else steps[::-1]:
                    run()

            ahead(0, 0)
            ahead(1, 1)
            with engine.Fori(0, (TT - 3) // 2) as i:
                for s in range(2):
                    both(2 * i + s, s)
            both(TT - 3, 0)
            behind(TT - 2, 1)
            behind(TT - 1, 0)

        turns = EDGE_SLOTS // (2 * HALF)
        assert EDGE_SLOTS == turns * 2 * HALF and turns % 2 == 0
        assert MOE_SLOTS % 2 == 0
        block = ctx.enter_context(nc.Block())

        @block.sync
        def _(sp):
            sp.dma_start(row_e[:, :], src).then_inc(src_in, 16)
            for dram, part in ((dst, dst_in), (edge_w, weight_in)):
                sp.dma_start(part, dram).then_inc(edges_in, 16)
            x_v = x.rearrange("(t p) c -> p t c", p=P)
            sp.dma_start(xs.rearrange("p (t c) -> p t c", c=C), x_v).then_inc(x_in, 16)
            kp = lambda w: w.rearrange("(k p) n -> p k n", p=P)
            for dram, part in ((kp(wx_t), wxt[:, :, :]), (kp(w_qkv), wqkv[:, :, :]), (ln1_g, vecs[:, 0, :]),
                               (ln1_b, vecs[:, 1, :]), (bx, vecs[:, 2, :]), (ln2_g, vecs[:, 3, :]),
                               (ln2_b, vecs[:, 4, :]), (kp(w_gnn), wg[:, :, :]), (kp(w_o), wo[:, :, :]),
                               (b_o, attn_w[HR:HR + 1, :]), (kp(w_1), w1[:, :, :]), (b_1, b1[:, :]),
                               (kp(w_2), w2[:, :, :]), (b_2.partition_broadcast(P), b2[:, :]),
                               (kp(router_t), rt[:, :, :])):
                sp.dma_start(part, dram).then_inc(weights_in, 16)
            sp.wait_ge(acc_zeroed, 1)
            sp.dma_start(records_d.rearrange("(p j) w -> p (j w)", p=P),
                         acc[:, 0:EDGE_SLOTS * RECORD].bitcast(i32)).then_inc(records_zeroed, 16)
            sp.dma_start(sum_d[TOKENS:, :], acc[:, 0:C]).then_inc(trash_zeroed, 16)

            sp.wait_ge(support_ready, TT + 2)
            sp.dma_start(support_d.rearrange("(t p) c -> p t c", p=P),
                         sup_all.rearrange("p (t c) -> p t c", c=C)).then_inc(support_stored, 16)
            sp.wait_ge(records_scattered[0], 16 * (EC // 2))
            sp.wait_ge(records_scattered[1], 16 * (EC // 2))
            sp.dma_start(tab[:, 0:EDGE_SLOTS * RECORD],
                         records_d.rearrange("(p j) w -> p (j w)", p=P)).then_inc(records_in, 16)
            sp.wait_ge(down_added, 4 + TT)
            w_13f = w_13.rearrange("p e n -> p (e n)")
            step_cols, step_tiles = odd0 // UP_LOADS, EDGE_SLOTS // UP_LOADS
            with sp.Fori(0, UP_LOADS) as i:
                sp.wait_ge(acc_added, i * step_tiles + 1 + HALF)
                sp.dma_start(R1[:, ds(i * step_cols, step_cols)],
                             w_13f[:, ds(i * step_cols, step_cols)]).then_inc(experts_up_in, 16)
            with sp.Fori(0, TT // CH) as c:
                sp.wait_ge(x1_ready, c + 1)
                sp.dma_start(sum_d[ds(c * CH * P, CH * P), :].rearrange("(t p) c -> p t c", p=P),
                             M[:, ds(c * CH * C, CH * C)].rearrange("p (t c) -> p t c", c=C)).then_inc(x1_stored, 16)
            sp.dma_start(R1[:, odd0:], w_13f[:, odd0:]).then_inc(experts_up_in, 16)
            sp.dma_start(w2_e[:, TT * C:], w_down[:, TT * C:]).then_inc(experts_down_in, 16)
            sp.wait_ge(xn2_ready, TT)
            sp.dma_start(xn2_d.rearrange("(t p) c -> p t c", p=P),
                         M.rearrange("p (t c) -> p t c", c=C)).then_inc(xn2_stored, 16)
            sp.wait_ge(xn2_stored, 16)
            sp.dma_start(w2_e[:, 0:TT * C], w_down[:, 0:TT * C]).then_inc(experts_down_in, 16)

            sp.wait_ge(rows_added, 16 * MOE_SLOTS)
            sp.dma_start(out, sum_d[0:NODES, :]).then_inc(out_stored, 16)
            sp.wait_ge(out_stored, 16)

        @block.gpsimd
        def _(pool):
            pool.memset(ident[:, :], 0.0).then_inc(constants, 1)
            pool.memset(ones[:, :], 1.0).then_inc(constants, 1)
            pool.memset(padneg[:, :], 0.0).then_inc(constants, 1)
            pool.memset(kvmask[:, :, :, :], 1.0).then_inc(constants, 1)
            pool.iota(iota_r[:, :], pattern=[[1, EDGE_SLOTS]], base=0, channel_multiplier=0,
                      allow_small_or_imprecise_dtypes=True).then_inc(constants, 1)
            pool.iota(token_ids[:, :], pattern=[[P, TT]], base=1, channel_multiplier=1,
                      allow_small_or_imprecise_dtypes=True).then_inc(constants, 1)
            pool.iota(trash[:, :], pattern=[[0, 1]], base=TOKENS + 1, channel_multiplier=1,
                      allow_small_or_imprecise_dtypes=True).then_inc(constants, 1)
            pool.memset(pad_key[:, :], 0.0).then_inc(constants, 1)
            pool.iota(pad_rows[:, :], pattern=[[P, 2]], base=MOE_SLOTS * P, channel_multiplier=1,
                      allow_small_or_imprecise_dtypes=True).then_inc(constants, 1)
            pool.wait_ge(constants, 9)
            pool.affine_select(out=pad_key[:, :], in_=pad_key[:, :], compare_op=ALU.is_ge, fill=float(EXPERTS),
                               base=LAST - 1, pattern=[[0, 1]], channel_multiplier=-1).then_inc(constants, 1)
            pool.affine_select(out=pad_rows[:, :], in_=pad_rows[:, :], compare_op=ALU.is_ge, fill=0.0,
                               base=-LAST, pattern=[[0, 2]], channel_multiplier=1).then_inc(constants, 1)
            pool.affine_select(out=ident[:, :], in_=ident[:, :], compare_op=ALU.not_equal, fill=1.0, base=0,
                               pattern=[[-1, P]], channel_multiplier=1).then_inc(constants, 1)
            pool.affine_select(out=upper[:, :], in_=ones[:, :], compare_op=ALU.is_gt, fill=0.0, base=0,
                               pattern=[[1, P]], channel_multiplier=-1).then_inc(constants, 1)
            pool.affine_select(out=padneg[:, :], in_=padneg[:, :], compare_op=ALU.is_ge, fill=NEG,
                               base=LAST - 1, pattern=[[0, 1]], channel_multiplier=-1).then_inc(constants, 1)
            pool.affine_select(out=kvmask[:, :, :, :], in_=kvmask[:, :, :, :], compare_op=ALU.is_ge, fill=0.0,
                               base=0, pattern=[[P, KC], [-DH, HEADS], [0, KR]],
                               channel_multiplier=1).then_inc(constants, 1)
            pool.wait_ge(constants, 15)
            pool.affine_select(out=kvmask[:, :, :, :], in_=kvmask[:, :, :, :], compare_op=ALU.is_ge, fill=0.0,
                               base=DH - 1, pattern=[[-P, KC], [DH, HEADS], [0, KR]],
                               channel_multiplier=-1).then_inc(constants, 1)

            pool.memset(acc, 0.0).then_inc(acc_zeroed, 1)

            pool.wait_ge(edge_rows, 1)
            pool.wait_ge(records_zeroed, 16)

            def scatter(i, h, first):
                col = (2 * i + h) * HS
                if not first:
                    pool.wait_ge(records_scattered[h], 16 * HS * i)
                pool.tensor_copy(stage_i[:, h, 0:HS], row_e[:, ds(col, HS)]).then_inc(staged, 1)
                pool.tensor_copy(stage_r[:, h, 0:HS, :], rec[:, ds(col, HS), :]).then_inc(staged, 1)
                pool.wait_ge(staged, 4 * i + 2 * h + 2)
                pool.sem_inc(stages_seen, 1)
                for k in range(HS):
                    pool.indirect_dma_start(
                        records_d, bass.IndirectOffsetOnAxis(ap=stage_i[:, h, k:k + 1].bitcast(u32), axis=0),
                        stage_r[:, h, k, :], None).then_inc(records_scattered[h], 16)

            scatter(0, 0, True)
            pool.wait_ge(edge_rows, 2)
            scatter(0, 1, True)
            with pool.Fori(1, EC // (2 * HS)) as i:
                for h in range(2):
                    scatter(i, h, False)

            pool.wait_ge(records_in, 16)
            pool.wait_ge(support_stored, 16)
            pool.wait_ge(x_free, 1)
            tab3 = tab[:, :].rearrange("p (j w) -> p j w", w=RECORD)

            def stage_rows(turn, u):
                pool.tensor_copy(turn_rows[:, u, :], tab3[:, ds(turn * 2 * HALF, 2 * HALF), 0]) \
                    .then_inc(gather_staged, 1)

            def gather(turn, u, first=False, last=False):
                for h in range(2):
                    if h == 1 and not last:
                        if not first:
                            for half in range(2):
                                pool.wait_ge(rows_gathered[half], 16 * HALF * turn)
                        stage_rows(turn + 1, 1 - u)
                    if not first:
                        pool.wait_ge(edge_products, HALF * (2 * turn + h - 1))
                    pool.wait_ge(gather_staged, turn + 1)
                    pool.sem_inc(stages_seen, 1)
                    for k in range(HALF):
                        n = h * HALF + k
                        pool.indirect_dma_start(
                            gathered[:, n, :], None, support_d,
                            bass.IndirectOffsetOnAxis(ap=turn_rows[:, u, n:n + 1].bitcast(u32), axis=0),
                        ).then_inc(rows_gathered[h], 16)

            stage_rows(0, 0)
            gather(0, 0, first=True)
            gather(1, 1)
            with pool.Fori(1, turns // 2 - 1) as i:
                gather(2 * i, 0)
                gather(2 * i + 1, 1)
            gather(turns - 2, 0)
            gather(turns - 1, 1, last=True)

            def over_tiles(a):
                return a.unsqueeze(2).to_broadcast([P, TT, MOE_SLOTS])

            pool.wait_ge(slot_places, 1)
            tokens, gated = pick_j[:, TT:PICKS, 0, :], pick_j[:, TT:PICKS, 1, :]
            pool.tensor_tensor(tokens, gated, over_tiles(token_ids[:, :]), ALU.mult).then_inc(picks_by_tile, 1)
            pool.wait_ge(picks_by_tile, 1)
            pool.tensor_tensor(gated, gated, over_tiles(gates[:, 1, :]), ALU.mult).then_inc(second_spread, 1)

            def gather_rows(j, s):
                pool.tensor_copy(src_ring[:, s:s + 1], slot_src[:, ds(j, 1)]).then_inc(rows_staged, 1)
                pool.wait_ge(rows_staged, j + 1)
                pool.sem_inc(stages_seen, 1)
                pool.indirect_dma_start(
                    ex_ring[:, s, :], None, xn2_d,
                    bass.IndirectOffsetOnAxis(ap=src_ring[:, s:s + 1].bitcast(u32), axis=0),
                ).then_inc(slot_rows_in[s], 16)

            pool.wait_ge(xn2_stored, 16)
            pool.wait_ge(slots_known, 1)
            gather_rows(0, 0)
            gather_rows(1, 1)
            for j in range(2):
                pool.wait_ge(slot_transposed, j + 1)
                gather_rows(j + 2, j)

            def add_rows(j, s, first=False, more=True):
                if more:
                    pool.wait_ge(slot_transposed, j + 3)
                    gather_rows(j + 4, s)
                pool.wait_ge(down_copied, j + 2)
                if not first:
                    pool.wait_ge(rows_added, 16 * j)
                pool.tensor_copy(dst_ring[:, s:s + 1], slot_dst[:, ds(j, 1)]).then_inc(dst_staged, 1)
                pool.wait_ge(dst_staged, j + 1)
                pool.sem_inc(stages_seen, 1)
                pool.indirect_dma_start(
                    sum_d, bass.IndirectOffsetOnAxis(ap=dst_ring[:, s:s + 1].bitcast(u32), axis=0),
                    y_ring[:, s, :], None, compute_op=ALU.add).then_inc(rows_added, 16)

            pool.wait_ge(x1_stored, 16 * (TT // CH))
            pool.wait_ge(trash_zeroed, 16)
            pool.wait_ge(slots_known, 3)
            add_rows(0, 0, first=True)
            add_rows(1, 1)
            with pool.Fori(1, MOE_SLOTS // 2 - 2) as i:
                for s in range(2):
                    add_rows(2 * i + s, s)
            for j in range(MOE_SLOTS - 4, MOE_SLOTS):
                add_rows(j, j % 2, more=False)

        @block.vector
        def _(dve):
            step = [0]

            def link(ins):
                step[0] += 1
                ins.then_inc(vector_step, 1)
                dve.wait_ge(vector_step, step[0])

            ranks = [0]

            def rank(keys, K, T, slots, area, cum, row, swizzle, cuts=(), filling=None):
                n = ranks[0]
                ranks[0] += 1
                cnt, tot, tiles, tinc, d, tmp = (small[:, i, 0:K] for i in range(6))
                oh = area[:, 0:K * T]
                ohv = oh.rearrange("p (k t) -> p k t", t=T)
                cumv = cum.rearrange("p (k t) -> p k t", t=T)
                kb = iota_r[:, 0:K].unsqueeze(2).to_broadcast([P, K, T])
                link(nc.vector.tensor_tensor(ohv, keys.unsqueeze(1).to_broadcast([P, K, T]), kb, ALU.is_equal))
                link(nc.vector.tensor_tensor_scan(cum, oh, oh, 0.0, ALU.add, ALU.max))
                ends = cumv[:, :, T - 1]
                link(nc.vector.tensor_copy(cnt, ends))
                link(nc.vector.tensor_tensor(tmp[:, 1:K], cnt[:, 1:K], cnt[:, 0:K - 1], ALU.subtract))
                link(nc.vector.tensor_copy(tmp[:, 0:1], cnt[:, 0:1]))
                link(nc.vector.tensor_tensor(d, cnt, tmp, ALU.subtract))
                nc.vector.tensor_copy(cnt, tmp).then_inc(rank_counts, 1)
                yield
                dve.wait_ge(rank_sums, n + 1)
                link(nc.vector.scalar_tensor_tensor(d, B[7][:, 0:K], -1.0, d, ALU.add, ALU.subtract))
                ti = tot.bitcast(i32)
                link(nc.vector.tensor_scalar(ti, B[7][:, K:2 * K], float(P - 1), None, ALU.add))
                link(nc.vector.tensor_scalar(ti, ti, 7, None, ALU.arith_shift_right))
                link(nc.vector.tensor_copy(tiles, ti))
                link(nc.vector.tensor_tensor_scan(tinc, tiles, tiles, 0.0, ALU.add, ALU.max))
                link(nc.vector.tensor_tensor(tmp, tinc, tiles, ALU.subtract))
                link(nc.vector.scalar_tensor_tensor(d, tmp, float(P), d, ALU.mult, ALU.add))
                for lo, hi in zip((0,) + cuts, cuts + (T,)):
                    c, o, r, n = cumv[:, :, lo:hi], ohv[:, :, lo:hi], row[:, lo:hi], hi - lo
                    link(nc.vector.tensor_tensor(c, c, d.unsqueeze(2).to_broadcast([P, K, n]), ALU.add))
                    link(nc.vector.tensor_tensor(c, c, o, ALU.mult))
                    link(nc.vector.tensor_reduce(r.bitcast(fp32), c.rearrange("p k t -> p t k"), X, ALU.add))
                    if filling is not None:
                        last = r[:, n // 2 - 1::n // 2].bitcast(fp32)
                        link(nc.vector.tensor_tensor(last, last, filling, ALU.add))
                    link(nc.vector.tensor_copy(r, r.bitcast(fp32)))
                    if swizzle:
                        q, j = ohv[:, 0, lo:hi].bitcast(i32), ohv[:, 1, lo:hi].bitcast(i32)
                        link(nc.vector.tensor_scalar(q, r, P - 1, None, ALU.bitwise_and))
                        link(nc.vector.tensor_scalar(j, r, 7, None, ALU.arith_shift_right))
                        link(nc.vector.scalar_tensor_tensor(r, q, float(slots), j, ALU.mult, ALU.add))
                    yield

            def owners(K, slots, owner, scale, area, room):
                tinc = small[0:1, 3, 0:K]
                n = min(slots, room // (K + 1))
                for j in range(0, slots, n):
                    m = min(n, slots - j)
                    own = area[0:1, 0:m * K].rearrange("p (j k) -> p j k", k=K)
                    own_f = area[0:1, n * K:n * K + m]
                    link(nc.vector.tensor_tensor(own, iota_r[0:1, j:j + m].unsqueeze(2).to_broadcast([1, m, K]),
                                                 tinc.unsqueeze(1).to_broadcast([1, m, K]), ALU.is_ge))
                    link(nc.vector.tensor_reduce(own_f, own, X, ALU.add))
                    link(nc.vector.tensor_scalar(owner[:, j:j + m], own_f, float(K - 1), float(scale),
                                                 ALU.min, ALU.mult))

            lns = [0]

            def norm_columns():
                me, ve, mo, vo = (stats[:, :, i] for i in (1, 2, 4, 5))
                link(nc.vector.tensor_tensor(t0, me, mo, ALU.add))
                link(nc.vector.tensor_scalar(mean, t0, 0.5, None, ALU.mult))
                link(nc.vector.tensor_tensor(t1, me, mo, ALU.subtract))
                link(nc.vector.scalar_tensor_tensor(t1, t1, 0.25, t1, ALU.mult, ALU.mult))
                link(nc.vector.tensor_tensor(t0, ve, vo, ALU.add))
                link(nc.vector.scalar_tensor_tensor(t0, t0, 1.0 / C, t1, ALU.mult, ALU.add))
                nc.vector.tensor_scalar(var, t0, EPS, None, ALU.add).then_inc(var_ready, 1)
                lns[0] += 1
                dve.wait_ge(root_ready, lns[0])
                link(nc.vector.reciprocal(t0, root))
                link(nc.vector.tensor_tensor(t1, t0, t0, ALU.mult))
                link(nc.vector.scalar_tensor_tensor(t1, var, -0.5, t1, ALU.mult, ALU.mult))
                link(nc.vector.scalar_tensor_tensor(rstd, t1, 1.5, t0, ALU.add, ALU.mult))

            def normalise(o, i, t):
                return nc.vector.tensor_scalar(o, i, mean[:, ds(t, 1)], rstd[:, ds(t, 1)], ALU.subtract, ALU.mult)

            def tile_of(a, t):
                return a[:, ds(t * C, C)]

            dve.wait_ge(src_in, 16)
            dve.wait_ge(constants, CONSTANTS)
            link(nc.vector.tensor_scalar(src_part, row_e[:, :], P - 1, None, ALU.bitwise_and))
            link(nc.vector.tensor_copy(rec[:, :, 1].bitcast(fp32), src_part))
            link(nc.vector.tensor_scalar(src_part, row_e[:, :], 7, None, ALU.arith_shift_right))
            link(nc.vector.tensor_copy(key_e, src_part))
            r = rank(key_e, TT, EC, EDGE_SLOTS, oh_e, cum_e, row_e[:, :], True, cuts=(HS,))
            next(r)
            dve.wait_ge(edges_in, 32)
            link(nc.vector.tensor_copy(rec[:, :, 0], dst_in))
            link(nc.vector.tensor_copy(rec[:, :, 2].bitcast(fp32), weight_in))
            for _ in range(2):
                next(r)
                dve.sem_inc(edge_rows, 1)

            dve.wait_ge(weights_in, 16 * 15)
            for v in range(2):
                for k in range(KC):
                    nc.vector.tensor_copy(vbc[:, v, k, :], vecs[:, 1 + v, k:k + 1].to_broadcast([P, P])) \
                        .then_inc(fold_inputs, 1)
            for k in range(KC):
                dve.wait_ge(fold_products, k + 1)
                nc.vector.tensor_copy(wraw[:, k, :], B[k][:, 0:QKV]).then_inc(fold_inputs, 1)
            dve.wait_ge(fold_inputs, 6)
            for k in range(KC):
                link(nc.vector.tensor_scalar(wfold[:, k, :], wraw[:, k, :], vecs[:, 0, k:k + 1], None, ALU.mult))
            dve.wait_ge(bias_product, 1)
            nc.vector.tensor_copy(bqkv[:, :], B[2][:, 0:QKV]).then_inc(folded, 1)
            dve.wait_ge(b1_product, 1)
            link(nc.vector.tensor_tensor(b1[:, :], B[6][:, 0:FT], b1[:, :], ALU.add))
            for k in range(KC):
                link(nc.vector.tensor_scalar(w1[:, k, :], w1[:, k, :], vecs[:, 3, k:k + 1], None, ALU.mult))
            nc.vector.memset(q_ring[:, :, HR:P], 1.0).then_inc(mlp_weights, 1)

            dve.wait_ge(x_in, 16)
            with dve.Fori(0, TT // CH) as c:
                for i in range(CH):
                    t = c * CH + i
                    nc.vector.bn_stats(stats[:, ds(t, 1), :], tile_of(xs, t)).then_inc(x_stats, 1)
            dve.wait_ge(x_stats, TT)
            norm_columns()
            with dve.Fori(0, TT // CH) as c:
                for i in range(CH):
                    normalise(tile_of(M, c * CH + i), tile_of(xs, c * CH + i), c * CH + i).then_inc(xn_ready, 1)
                for i in range(CH):
                    t = c * CH + i
                    dve.wait_ge(xn_ready, t + 1)
                    nc.vector.bn_stats(stats[:, ds(t, 1), :], tile_of(M, t)).then_inc(x_stats, 1)
            dve.wait_ge(x_stats, 2 * TT)
            norm_columns()

            def z_tile(t, s):
                dve.wait_ge(transposed, t + 1)
                normalise(z_ring[:, s, :], tile_of(M, t), t).then_inc(z_ready, 1)

            def products_out(t, s):
                dve.wait_ge(token_products, t + 1)
                nc.vector.tensor_copy(tile_of(sup_all, t), B[2 + s][:, 0:C]).then_inc(support_ready, 1)
                nc.vector.tensor_tensor(qkv[:, ds(t, 1), :], B[4 + s][:, 0:QKV].unsqueeze(1), bqkv.unsqueeze(1),
                                        ALU.add).then_inc(qkv_ready, 1)
                nc.vector.tensor_tensor(tile_of(xs, t), tile_of(xs, t), b2[:, :], ALU.add).then_inc(x_plus_b2, 1)

            dve.wait_ge(folded, 1)
            dve.sem_inc(transposed, 2)
            dve.sem_inc(support_ready, 2)
            dve.sem_inc(qkv_ready, 2)
            staggered(dve, z_tile, products_out, first=z_tile)
            dve.wait_ge(qkv_ready, TT + 2)

            q_v = qkv[:, :, C:C + HR]
            k_v = qkv[:, :, C + HR:QKV]
            link(nc.vector.tensor_scalar(k_v[:, TT - 1, :], k_v[:, TT - 1, :], padneg[:, 0:1], None, ALU.add))
            nc.vector.tensor_reduce(kmax[:, :], k_v.rearrange("p t c -> p c t"), X, ALU.max).then_inc(kmax_ready, 1)
            dve.wait_ge(kmax_transposed, 1)
            link(nc.vector.tensor_reduce(kmax_t[:, :], B[6][0:HR, 0:P], X, ALU.max))
            nc.vector.tensor_scalar(diag[:, :], ident[0:HR, 0:HR], kmax_t[:, 0:1], None, ALU.mult) \
                .then_inc(kmax_diagonal, 1)
            q4 = q_v.rearrange("p t (h r) -> p t h r", r=KR)
            link(nc.vector.tensor_reduce(q_red[:, :, :], q4, X, ALU.max))
            nc.vector.tensor_tensor(q4, q4, q_red[:, :, :].unsqueeze(3).to_broadcast([P, TT, HEADS, KR]),
                                    ALU.subtract).then_inc(exp_input, 1)
            dve.wait_ge(kmax_spread, 1)
            nc.vector.tensor_tensor(k_v, k_v, B[7][:, 0:HR].unsqueeze(1).to_broadcast([P, TT, HR]),
                                    ALU.subtract).then_inc(exp_input, 1)
            dve.wait_ge(exp_done, 1)
            nc.vector.tensor_reduce(kmax[:, :], k_v.rearrange("p t c -> p c t"), X, ALU.add).then_inc(k_summed, 1)
            link(nc.vector.tensor_reduce(q_red[:, :, :], q4, X, ALU.add))
            link(nc.vector.reciprocal(q_red[:, :, :], q_red[:, :, :]))
            dve.wait_ge(kv_product, 1)
            link(nc.vector.reciprocal(kden[:, :], B[4][:, 0:HR]))
            for k in range(KC):
                link(nc.vector.tensor_tensor(kvT[:, k, :], B[2 + k][:, 0:HR],
                                             kvmask[:, k, :, :].rearrange("p h r -> p (h r)"), ALU.mult))
                nc.vector.tensor_tensor(kvT[:, k, :], kvT[:, k, :], kden[:, :], ALU.mult).then_inc(kv_ready, 1)
            dve.wait_ge(attn_product, 1)
            nc.vector.tensor_copy(attn_w[0:HR, :], B[5][0:HR, 0:C]).then_inc(attn_weights, 1)

            def q_tile(t, s):
                dve.wait_ge(q_transposed, t + 1)
                nc.vector.tensor_tensor(q_ring[:, s, 0:HR].rearrange("p (h r) -> p h r", r=KR),
                                        qkv[:, ds(t, 1), C:C + HR].rearrange("p o (h r) -> p (o h) r", r=KR),
                                        q_red[:, ds(t, 1), :].rearrange("p o h -> p (o h)").unsqueeze(2)
                                        .to_broadcast([P, HEADS, KR]), ALU.mult).then_inc(q_ready, 1)

            def fx_tile(t, s):
                dve.wait_ge(attn_rows, t + 1)
                nc.vector.tensor_tensor(tile_of(M, t), B[2 + s][:, 0:C], tile_of(M, t), ALU.add) \
                    .then_inc(residual_ready, 1)
                dve.wait_ge(residual_ready, t + 3)
                nc.vector.bn_stats(stats[:, ds(t, 1), :], tile_of(M, t)).then_inc(x_stats, 1)

            dve.sem_inc(q_transposed, 2)
            dve.sem_inc(residual_ready, 2)
            staggered(dve, q_tile, fx_tile, first=q_tile)
            dve.wait_ge(x_stats, 3 * TT)
            norm_columns()

            def z2_tile(t, s):
                dve.wait_ge(z2_transposed, t + 1)
                normalise(z_ring[:, s, :], tile_of(M, t), t).then_inc(z2_ready, 1)

            dve.wait_ge(x_plus_b2, TT)
            dve.sem_inc(z2_transposed, 2)
            pairs(dve, z2_tile)
            dve.wait_ge(z2_ready, TT)
            nc.vector.tensor_tensor(M[:, :], M[:, :], xs, ALU.add).then_inc(mix_residual, 1)
            dve.wait_ge(mix_residual, 1)
            owners(TT, EDGE_SLOTS, edge_owner, C, xs, TT * C)
            dve.sem_inc(x_free, 1)
            nc.vector.memset(acc_odd[:, behind - odd0:], 0.0).then_inc(acc_odd_zeroed, 1)

            dve.sem_inc(down_added, 4)
            with dve.Fori(0, TT // CH) as c:
                for i in range(CH):
                    dve.wait_ge(down_product, c * CH + i + 1)
                    nc.vector.tensor_tensor(tile_of(M, c * CH + i), B[4 + i % 4][:, 0:C], tile_of(M, c * CH + i),
                                            ALU.add).then_inc(down_added, 1)
            dve.wait_ge(down_added, 4 + TT)

            tabw = tab[:, :].bitcast(fp32)

            def onehots(col, h):
                for k in range(HALF):
                    at = (col + k) * RECORD
                    nc.vector.tensor_scalar(S[:, h * HALF + k, :], iota_r[:, 0:P], tabw[:, ds(at + 1, 1)],
                                            tabw[:, ds(at + 2, 1)], ALU.is_equal, ALU.mult).then_inc(edge_onehots, 1)

            def add_up(col, offsets):
                for k in range(HALF):
                    dve.wait_ge(edge_products, col + k + 1)
                    dve.wait_ge(acc_added, col + k - 1 + HALF)
                    part = (acc, acc_odd)[k % 2][:, ds(offsets[k], C)]
                    nc.vector.tensor_tensor(part, B[k][:, 0:C], part, ALU.add).then_inc(acc_added, 1)

            nc.vector.memset(acc_odd[:, 0:behind - odd0], 0.0).then_inc(acc_odd_zeroed, 1)
            dve.wait_ge(acc_odd_zeroed, 2)
            dve.wait_ge(records_in, 16)
            dve.wait_ge(trash_zeroed, 16)
            dve.wait_ge(records_zeroed, 16)
            dve.sem_inc(acc_added, HALF)
            onehots(0, 0)
            def edge_turn(i, last=False):
                onehots(2 * i * HALF + HALF, 1)
                _, offsets = nc.values_load_multi_w_load_instructions(
                    edge_owner[0:1, ds(2 * i * HALF, 2 * HALF)], engines=[mybir.EngineType.DVE],
                    min_val=0, max_val=(TT - 1) * C)
                add_up(2 * i * HALF, offsets[:HALF])
                if not last:
                    onehots(2 * i * HALF + 2 * HALF, 0)
                add_up(2 * i * HALF + HALF, offsets[HALF:])

            with dve.Fori(0, turns - 1) as i:
                edge_turn(i)
            edge_turn(turns - 1, last=True)
            dve.wait_ge(acc_added, EDGE_SLOTS + HALF)

            with dve.Fori(0, TT // CH) as c:
                part = ds(c * CH * C, CH * C)
                nc.vector.tensor_tensor(acc[:, part], acc[:, part], acc_odd[:, part], ALU.add).then_inc(sums_joined, 1)
                dve.wait_ge(sums_joined, c + 1)
                nc.vector.scalar_tensor_tensor(M[:, part], acc[:, part], 0.0, M[:, part], ALU.max, ALU.add) \
                    .then_inc(x1_ready, 1)
            dve.wait_ge(x1_ready, TT // CH)
            with dve.Fori(0, TT // CH) as c:
                for i in range(CH):
                    nc.vector.bn_stats(stats[:, ds(c * CH + i, 1), :], tile_of(M, c * CH + i)).then_inc(x_stats, 1)
            dve.wait_ge(x_stats, 4 * TT)
            norm_columns()
            nc.vector.scalar_tensor_tensor(shift, mean, -1.0, rstd, ALU.mult, ALU.mult).then_inc(norm2_columns, 1)

            dve.wait_ge(router_product, RP + 2)
            top, total = small[:, 0:2, :], small[:, 2, :]

            def wide(a):
                return a.unsqueeze(2).to_broadcast([P, TT, EXPERTS])

            experts = iota_r[:, 0:EXPERTS].unsqueeze(1).to_broadcast([P, TT, EXPERTS])
            products = B[3][:, 0:TT * EXPERTS].rearrange("p (t e) -> p t e", e=EXPERTS)
            r_sums = B[3][:, TT * EXPERTS:(TT + 1) * EXPERTS].unsqueeze(1).to_broadcast([P, TT, EXPERTS])
            link(nc.vector.tensor_tensor(pick[:, 0, :, :], wide(mean), r_sums, ALU.mult))
            link(nc.vector.tensor_tensor(probs[:, :, :], products, pick[:, 0, :, :], ALU.subtract))
            link(nc.vector.tensor_tensor(probs[:, :, :], probs[:, :, :], wide(rstd), ALU.mult))
            link(nc.vector.tensor_reduce(top[:, 0, :], probs[:, :, :], X, ALU.max))
            nc.vector.tensor_tensor(probs[:, :, :], probs[:, :, :], wide(top[:, 0, :]), ALU.subtract) \
                .then_inc(exp_input, 1)
            dve.wait_ge(exp_done, 2)
            link(nc.vector.tensor_reduce(total, probs[:, :, :], X, ALU.add))
            link(nc.vector.reciprocal(total, total))
            link(nc.vector.tensor_tensor(probs[:, :, :], probs[:, :, :], wide(total), ALU.mult))
            for k in range(2):
                key = keys_m[:, k * TT:(k + 1) * TT]
                link(nc.vector.tensor_reduce(top[:, k, :], probs[:, :, :], X, ALU.max))
                link(nc.vector.tensor_tensor(pick[:, 0, :, :], probs[:, :, :], wide(top[:, k, :]), ALU.is_lt))
                link(nc.vector.scalar_tensor_tensor(pick[:, 0, :, :], pick[:, 0, :, :], float(EXPERTS), experts,
                                                    ALU.mult, ALU.add))
                link(nc.vector.tensor_reduce(key, pick[:, 0, :, :], X, ALU.min))
                if k == 0:
                    link(nc.vector.tensor_tensor(pick[:, 1, :, :], experts, wide(key), ALU.is_equal))
                    link(nc.vector.scalar_tensor_tensor(probs[:, :, :], pick[:, 1, :, :], -2.0, probs[:, :, :],
                                                        ALU.mult, ALU.add))
            link(nc.vector.tensor_tensor(total, top[:, 0, :], top[:, 1, :], ALU.add))
            link(nc.vector.tensor_scalar(total, total, 1e-9, None, ALU.add))
            link(nc.vector.reciprocal(total, total))
            for k in range(2):
                link(nc.vector.tensor_tensor(gates[:, k, :], top[:, k, :], total, ALU.mult))
            last_keys = keys_m[:, TT - 1::TT]
            link(nc.vector.tensor_scalar(last_keys, last_keys, pad_key[:, 0:1], None, ALU.add))
            r = rank(keys_m[:, :], EXPERTS, PICKS, MOE_SLOTS, oh_m, cum_m, row_m[:, :], False, filling=pad_rows[:, :])
            for _ in r:
                pass
            tile_i, place_i = slot_j[:, :].bitcast(i32), slot_q[:, :].bitcast(i32)
            link(nc.vector.tensor_scalar(tile_i, row_m[:, :], 7, None, ALU.arith_shift_right))
            link(nc.vector.tensor_scalar(place_i, row_m[:, :], P - 1, None, ALU.bitwise_and))
            link(nc.vector.tensor_copy(slot_j[:, :], tile_i))
            link(nc.vector.tensor_copy(slot_q[:, :], place_i))

            def over_tiles(a):
                return a.unsqueeze(2).to_broadcast([P, TT, MOE_SLOTS])

            tiles = iota_r[:, 0:MOE_SLOTS].unsqueeze(1).to_broadcast([P, TT, MOE_SLOTS])
            tokens, gated = pick_j[:, 0:TT, 0, :], pick_j[:, 0:TT, 1, :]
            link(nc.vector.tensor_tensor(gated, tiles, over_tiles(slot_j[:, 0:TT]), ALU.is_equal))
            link(nc.vector.tensor_tensor(tokens, gated, over_tiles(token_ids[:, :]), ALU.mult))
            nc.vector.tensor_tensor(gated, gated, over_tiles(gates[:, 0, :]), ALU.mult).then_inc(picks_spread, 1)
            for n in range(0, PICKS, SPREAD):
                if n == SPREAD:
                    nc.vector.tensor_tensor(pick_j[:, TT:PICKS, 1, :], iota_r[:, 0:MOE_SLOTS].unsqueeze(1)
                                            .to_broadcast([P, TT, MOE_SLOTS]), over_tiles(slot_j[:, TT:PICKS]),
                                            ALU.is_equal).then_inc(slot_places, 1)
                m = min(SPREAD, PICKS - n)
                at = n % (2 * SPREAD)
                if n >= 2 * SPREAD:
                    dve.wait_ge(map_products, n - SPREAD)
                nc.vector.tensor_tensor(pick_q[:, at:at + m, :], iota_r[:, 0:P].unsqueeze(1).to_broadcast([P, m, P]),
                                        slot_q[:, n:n + m].unsqueeze(2).to_broadcast([P, m, P]),
                                        ALU.is_equal).then_inc(pick_onehots, 1)
            dve.wait_ge(map_products, PICKS)
            ids = B[7][:, 0:MOE_SLOTS]
            nc.vector.tensor_scalar(slot_src[:, :], ids, -1.0, 0.0, ALU.add, ALU.max).then_inc(slots_known, 1)
            nc.vector.tensor_scalar(slot_fill[:, :], ids, 0.0, trash[:, 0:1], ALU.is_equal,
                                    ALU.mult).then_inc(slot_filled, 1)
            nc.vector.tensor_copy(slot_gate[:, :], B[7][:, MOE_SLOTS:2 * MOE_SLOTS]).then_inc(slots_known, 1)
            dve.wait_ge(slot_filled, 1)
            nc.vector.scalar_tensor_tensor(slot_dst[:, :], ids, -1.0, slot_fill[:, :], ALU.add,
                                           ALU.add).then_inc(slots_known, 1)

            dve.sem_inc(half1_copied, 1)
            dve.sem_inc(down_copied, 1)

            def gate(j, a):
                dve.wait_ge((half0_silu, half1_silu)[a], j + 1)
                nc.vector.tensor_tensor(h_ring[:, a, :], g_ring[:, a, :], B[2 * a + 1][:, 0:HH], ALU.mult) \
                    .then_inc((half0_gated, half1_gated)[a], 1)

            def expert_rows(j, s, i, free=True, more=2):
                if more:
                    dve.wait_ge(half0_transposed, j + 1)
                    gate(j + 1, 0)
                dve.wait_ge(half1_transposed, j + 1)
                nc.vector.tensor_copy(hT_ring[:, 3:6, :].rearrange("p f c -> p (f c)"), B[5][0:HB, 0:3 * P]) \
                    .then_inc(half1_copied, 1)
                if more:
                    gate(j + 1, 1)
                if free:
                    dve.wait_ge(rows_added, 16 * (j - 1))
                dve.wait_ge(down_rows, j + 1)
                nc.vector.tensor_scalar(y_ring[:, s, :], B[7][:, 0:C], slot_gate[:, ds(j, 1)], None,
                                        ALU.mult).then_inc(down_copied, 1)

            owners(EXPERTS, MOE_SLOTS, slot_expert, 1, WM[:, 2048:4096], 2048)
            dve.wait_ge(slots_known, 3)
            dve.sem_inc(slots_known, 1)
            gate(0, 0)
            gate(0, 1)
            expert_rows(0, 0, 0, free=False)
            expert_rows(1, 1, 0, free=False)
            with dve.Fori(1, MOE_SLOTS // 2 - 1) as i:
                for s in range(2):
                    expert_rows(2 * i + s, s, i)
            expert_rows(MOE_SLOTS - 2, 0, None, more=1)
            expert_rows(MOE_SLOTS - 1, 1, None, more=0)

        @block.scalar
        def _(act):
            roots = [0]

            def square_root():
                roots[0] += 1
                act.wait_ge(var_ready, roots[0])
                nc.scalar.activation(root, var, ACT.Sqrt).then_inc(root_ready, 1)

            square_root()
            square_root()

            def copy_xn(t, s):
                act.wait_ge(transposed, t + 1)
                nc.scalar.activation(xn_ring[:, s, :], M[:, ds(t * C, C)], ACT.Copy).then_inc(xn_copied, 1)

            def copy_transposes(t, s):
                act.wait_ge(transposed, t + 3)
                nc.scalar.activation(tr_ring[:, s, :, :].rearrange("p q c -> p (q c)"), B[s][:, :], ACT.Copy) \
                    .then_inc(transposes_copied, 1)

            act.wait_ge(folded, 1)
            act.sem_inc(transposes_copied, 2)
            staggered(act, copy_xn, copy_transposes)

            act.wait_ge(exp_input, 2)
            nc.scalar.activation(qkv[:, :, C:QKV], qkv[:, :, C:QKV], ACT.Exp).then_inc(exp_done, 1)

            def copy_q(t, s):
                act.wait_ge(q_transposed, t + 3)
                nc.scalar.activation(qT_ring[:, s, :], B[s][0:HR + 1, 0:P], ACT.Copy).then_inc(q_copied, 1)

            act.sem_inc(q_copied, 2)
            pairs(act, copy_q)
            square_root()
            act.wait_ge(support_stored, 16)

            def copy_z2(t, s):
                act.wait_ge(z2_transposed, t + 3)
                nc.scalar.activation(z2T[:, :, ds(t * P, P)], B[s][:, 0:C].rearrange("p (k n) -> p k n", k=KC),
                                     ACT.Copy).then_inc(z2_copied, 1)

            act.sem_inc(z2_copied, 2)
            pairs(act, copy_z2)

            act.wait_ge(mlp_weights, 1)
            act.sem_inc(gelu_done, 4)
            with act.Fori(0, TT // CH) as c:
                for f in range(FT):
                    for half in range(2):
                        act.wait_ge(up_product, 16 * c + 2 * f + half + 1)
                        nc.scalar.activation(hidT[:, f, half * CN:(half + 1) * CN], B[(2 * f + half) % 4][:, 0:CN],
                                             ACT.Gelu, bias=b1[:, f:f + 1]).then_inc(gelu_done, 1)


            def copy_x1T(r, s, n=2):
                act.wait_ge(x1_transposed, r + 1)
                act.wait_ge(router_product, r + 1)
                nc.scalar.activation(x1T_ring[:, s, 0:n, :, :].rearrange("p t k c -> p (t k c)"),
                                     B[s][:, 0:n * C], ACT.Copy).then_inc(x1_transposes_copied, 1)

            nc.scalar.activation(warm[:, 0:1], ones[:, 0:1], ACT.Sqrt)
            act.sem_inc(router_product, 2)
            act.sem_inc(x1_transposes_copied, 2)
            pairs(act, copy_x1T, TT // 2)
            copy_x1T(RP - 1, (RP - 1) % 2, n=TT % 2)
            square_root()
            act.wait_ge(exp_input, 3)
            nc.scalar.activation(probs[:, :, :], probs[:, :, :], ACT.Exp).then_inc(exp_done, 1)

            act.wait_ge(norm2_columns, 1)
            act.wait_ge(x1_stored, 16 * (TT // CH))
            act.wait_ge(router_product, RP + 2)
            with act.Fori(0, TT // CH) as c:
                for i in range(CH):
                    t = c * CH + i
                    nc.scalar.activation(M[:, ds(t * C, C)], M[:, ds(t * C, C)], ACT.Identity,
                                         scale=rstd[:, ds(t, 1)], bias=shift[:, ds(t, 1)]).then_inc(xn2_ready, 1)

            nc.scalar.activation(warm[:, 1:2], ones[:, 0:1], ACT.Silu)

            act.sem_inc(half0_copied, 1)

            def copy_slot(j, s):
                act.wait_ge(slot_transposed, j + 1)
                nc.scalar.activation(exT_ring[:, s, :, :].rearrange("p k c -> p (k c)"), B[6][:, 0:C], ACT.Copy) \
                    .then_inc(slot_copied, 1)

            def silu(j, a, first=False):
                act.wait_ge((half0_product, half1_product)[a], j + 1)
                if not first:
                    act.wait_ge((half0_gated, half1_gated)[a], j)
                nc.scalar.activation(g_ring[:, a, :], B[2 * a][:, 0:HH], ACT.Silu) \
                    .then_inc((half0_silu, half1_silu)[a], 1)

            def expert_copies(j, s, more=2):
                if more:
                    silu(j + 1, 0)
                act.wait_ge(half0_transposed, j + 1)
                nc.scalar.activation(hT_ring[:, 0:3, :].rearrange("p f c -> p (f c)"), B[4][0:HB, 0:3 * P],
                                     ACT.Copy).then_inc(half0_copied, 1)
                if more == 2:
                    copy_slot(j + 2, s)
                if more:
                    silu(j + 1, 1)

            copy_slot(0, 0)
            copy_slot(1, 1)
            silu(0, 0, first=True)
            silu(0, 1, first=True)
            pairs(act, expert_copies, MOE_SLOTS - 2)
            expert_copies(MOE_SLOTS - 2, 0, more=1)
            expert_copies(MOE_SLOTS - 1, 1, more=0)

        @block.tensor
        def _(pe):
            mm = nc.tensor.matmul
            ranked = [0]

            def count_sums(K):
                ranked[0] += 1
                pe.wait_ge(rank_counts, ranked[0])
                mm(B[7][:, 0:K], upper[:, :], small[:, 0, 0:K], start=True, stop=True)
                mm(B[7][:, K:2 * K], ones[:, :], small[:, 0, 0:K], start=True, stop=True).then_inc(rank_sums, 1)

            pe.wait_ge(constants, CONSTANTS)
            count_sums(TT)

            pe.wait_ge(weights_in, 16 * 15)
            for m in range(KC):
                for k in range(KC):
                    ins = mm(B[m][:, 0:QKV], wxt[:, k, m * P:(m + 1) * P], wqkv[:, k, :],
                             start=(k == 0), stop=(k == KC - 1))
                ins.then_inc(fold_products, 1)
            pe.wait_ge(fold_inputs, 6)
            for k in range(KC):
                mm(B[2][:, 0:QKV], vbc[:, 0, k, :], wraw[:, k, :], start=(k == 0), stop=False)
            for k in range(KC):
                ins = mm(B[2][:, 0:QKV], vbc[:, 1, k, :], wqkv[:, k, :], start=False, stop=(k == KC - 1))
            ins.then_inc(bias_product, 1)
            for f in range(FT):
                for k in range(KC):
                    ins = mm(B[6][:, f:f + 1], w1[:, k, f * P:(f + 1) * P], vecs[:, 4, k:k + 1],
                             start=(k == 0), stop=(k == KC - 1))
            ins.then_inc(b1_product, 1)
            pe.wait_ge(folded, 1)

            def transpose_tokens(t, s):
                pe.wait_ge(xn_copied, t + 1)
                pe.wait_ge(z_ready, t + 1)
                pe.wait_ge(transposes_copied, t + 1)
                for q, ring in enumerate((xn_ring, xn_ring, z_ring, z_ring)):
                    c = q % 2 * P
                    ins = nc.tensor.transpose(B[s][:, q * P:(q + 1) * P], ring[:, s, c:c + P], ident[:, :])
                ins.then_inc(transposed, 1)

            def token_product(t, s):
                pe.wait_ge(transposes_copied, t + 3)
                pe.wait_ge(support_ready, t + 1)
                pe.wait_ge(qkv_ready, t + 1)
                for k in range(KC):
                    mm(B[2 + s][:, 0:C], tr_ring[:, s, k, :], wg[:, k, :], start=(k == 0), stop=(k == KC - 1))
                for k in range(KC):
                    ins = mm(B[4 + s][:, 0:QKV], tr_ring[:, s, KC + k, :], wfold[:, k, :],
                             start=(k == 0), stop=(k == KC - 1))
                ins.then_inc(token_products, 1)

            staggered(pe, transpose_tokens, token_product)

            pe.wait_ge(kmax_ready, 1)
            nc.tensor.transpose(B[6][0:HR, 0:P], kmax[:, :], ident[:, :]).then_inc(kmax_transposed, 1)
            pe.wait_ge(kmax_diagonal, 1)
            mm(B[7][:, 0:HR], ones[0:HR, :], diag[:, :], start=True, stop=True).then_inc(kmax_spread, 1)
            pe.wait_ge(exp_done, 1)
            pe.wait_ge(qkv_ready, TT + 2)
            for t in range(TT):
                kt = qkv[:, t, C + HR:QKV]
                for b, left in ((2, qkv[:, t, 0:P]), (3, qkv[:, t, P:C])):
                    ins = mm(B[b][:, 0:HR], left, kt, start=(t == 0), stop=(t == TT - 1))
            pe.wait_ge(k_summed, 1)
            mm(B[4][:, 0:HR], ones[:, :], kmax[:, :], start=True, stop=True).then_inc(kv_product, 1)
            pe.wait_ge(kv_ready, KC)
            for k in range(KC):
                ins = mm(B[5][0:HR, 0:C], kvT[:, k, :], wo[:, k, :], start=(k == 0), stop=(k == KC - 1))
            ins.then_inc(attn_product, 1)
            pe.wait_ge(attn_weights, 1)

            def transpose_q(t, s):
                pe.wait_ge(q_ready, t + 1)
                pe.wait_ge(q_copied, t + 1)
                nc.tensor.transpose(B[s][:, 0:P], q_ring[:, s, :], ident[:, :]).then_inc(q_transposed, 1)

            def attn_product_of(t, s):
                pe.wait_ge(q_copied, t + 3)
                pe.wait_ge(residual_ready, t + 1)
                mm(B[2 + s][:, 0:C], qT_ring[:, s, :], attn_w[:, :], start=True, stop=True).then_inc(attn_rows, 1)

            staggered(pe, transpose_q, attn_product_of)

            def transpose_z2(t, s):
                pe.wait_ge(z2_ready, t + 1)
                pe.wait_ge(z2_copied, t + 1)
                for k in range(KC):
                    ins = nc.tensor.transpose(B[s][:, k * P:(k + 1) * P], z_ring[:, s, k * P:(k + 1) * P], ident[:, :])
                ins.then_inc(z2_transposed, 1)

            pairs(pe, transpose_z2)

            pe.wait_ge(mlp_weights, 1)
            pe.wait_ge(z2_copied, TT + 2)
            with pe.Fori(0, TT // CH) as c:
                for g in range(2 * FT):
                    f, half = g // 2, g % 2
                    pe.wait_ge(gelu_done, 2 * FT * c + g + 1)
                    for k in range(KC):
                        ins = mm(B[g % 4][:, 0:CN], w1[:, k, f * P:(f + 1) * P],
                                 z2T[:, k, ds(c * 2 * CN + half * CN, CN)], start=(k == 0), stop=(k == KC - 1))
                    ins.then_inc(up_product, 1)
                pe.wait_ge(gelu_done, 2 * FT * c + 2 * FT + 4)
                for i in range(CH):
                    pe.wait_ge(down_added, CH * c + (i + 1 if i else 4))
                    for f in range(FT):
                        ins = mm(B[4 + i % 4][:, 0:C], hidT[:, f, i * P:(i + 1) * P], w2[:, f, :],
                                 start=(f == 0), stop=(f == FT - 1))
                    ins.then_inc(down_product, 1)

            pe.wait_ge(down_added, 4 + TT)
            with pe.Fori(0, EDGE_SLOTS // (2 * HALF)) as i:
                for n in range(2 * HALF):
                    j, k = 2 * HALF * i + n, n % HALF
                    if k == 0:
                        pe.wait_ge(rows_gathered[n // HALF], 16 * HALF * (i + 1))
                    pe.wait_ge(edge_onehots, j + 1)
                    pe.wait_ge(acc_added, j + 1)
                    mm(B[k][:, 0:C], S[:, n, :], gathered[:, n, :], start=True, stop=True) \
                        .then_inc(edge_products, 1)

            def transpose_x1(r):
                tiles = range(2 * r, min(2 * r + 2, TT))
                pe.wait_ge(x1_ready, tiles[-1] // CH + 1)
                pe.wait_ge(x1_transposes_copied, r + 1)
                for i, t in enumerate(tiles):
                    for k in range(KC):
                        ins = nc.tensor.transpose(B[r % 2][:, (i * KC + k) * P:(i * KC + k + 1) * P],
                                                  M[:, t * C + k * P:t * C + (k + 1) * P], ident[:, :])
                ins.then_inc(x1_transposed, 1)

            def route(r):
                pe.wait_ge(x1_transposes_copied, r + 3)
                for i, t in enumerate(range(2 * r, min(2 * r + 2, TT))):
                    for k in range(KC):
                        ins = mm(B[3][:, t * EXPERTS:(t + 1) * EXPERTS], x1T_ring[:, r % 2, i, k, :], rt[:, k, :],
                                 start=(k == 0), stop=(k == KC - 1))
                ins.then_inc(router_product, 1)

            transpose_x1(0)
            for k in range(KC):
                mm(B[3][:, TT * EXPERTS:(TT + 1) * EXPERTS], ones[:, :], rt[:, k, :],
                   start=(k == 0), stop=(k == KC - 1))
            for r in range(1, RP):
                transpose_x1(r)
                route(r - 1)
            route(RP - 1)
            count_sums(EXPERTS)
            for n in range(PICKS):
                if n % TT == 0:
                    pe.wait_ge((picks_spread, second_spread)[n // TT], 1)
                pe.wait_ge(pick_onehots, n // SPREAD + 1)
                mm(B[7][:, 0:2 * MOE_SLOTS], pick_q[:, n % (2 * SPREAD), :],
                   pick_j[:, n, :, :].rearrange("p a j -> p (a j)"),
                   start=(n == 0), stop=(n == PICKS - 1)).then_inc(map_products, 1)
            pe.wait_ge(slots_known, 4)

            def transpose_slot(j, s, arrivals, first=False):
                pe.wait_ge(slot_rows_in[s], 16 * arrivals)
                if not first:
                    pe.wait_ge(slot_copied, j)
                for k in range(KC):
                    ins = nc.tensor.transpose(B[6][:, k * P:(k + 1) * P], ex_ring[:, s, k * P:(k + 1) * P], ident[:, :])
                ins.then_inc(slot_transposed, 1)

            def up_half(e, j, s, a, first=False):
                pe.wait_ge(slot_copied, j + 1)
                if not first:
                    pe.wait_ge((half0_gated, half1_gated)[a], j)
                for part in (2 * a, 2 * a + 1):
                    for k in range(KC):
                        ins = mm(B[part][:, 0:HH], exT_ring[:, s, k, :],
                                 R1[:, ds(e * (KC * W13) + (k * W13 + part * HH), HH)],
                                 start=(k == 0), stop=(k == KC - 1))
                ins.then_inc((half0_product, half1_product)[a], 1)

            def transpose_half(j, a):
                pe.wait_ge((half0_gated, half1_gated)[a], j + 1)
                pe.wait_ge((half0_copied, half1_copied)[a], j + 1)
                for f in range(3):
                    ins = nc.tensor.transpose(B[4 + a][0:HB, f * P:(f + 1) * P], h_ring[:, a, f * HB:(f + 1) * HB],
                                              ident[:, :])
                ins.then_inc((half0_transposed, half1_transposed)[a], 1)

            def expert_of(j):
                return pe.value_load(slot_expert[0:1, ds(j, 1)], min_val=0, max_val=EXPERTS - 1)

            def down(j):
                e = expert_of(j)
                pe.wait_ge(half0_copied, j + 2)
                pe.wait_ge(half1_copied, j + 2)
                pe.wait_ge(down_copied, j + 1)
                for f in range(NHB):
                    ins = mm(B[7][:, 0:C], hT_ring[:, f, :], w2_e[:, ds(e * (NHB * C) + f * C, C)],
                             start=(f == 0), stop=(f == NHB - 1))
                ins.then_inc(down_rows, 1)

            def expert(j, s, i=None, more=2):
                if more:
                    e = expert_of(j + 1)
                    up_half(e, j + 1, 1 - s, 0)
                for a in range(2):
                    transpose_half(j, a)
                if more == 2:
                    transpose_slot(j + 2, s, i + 2)
                if more:
                    up_half(e, j + 1, 1 - s, 1)
                down(j)

            pe.wait_ge(experts_up_in, 16 * (UP_LOADS + 1))
            transpose_slot(0, 0, 1, first=True)
            transpose_slot(1, 1, 1)
            e0 = expert_of(0)
            up_half(e0, 0, 0, 0, first=True)
            up_half(e0, 0, 0, 1, first=True)
            pe.wait_ge(experts_down_in, 32)
            with pe.Fori(0, MOE_SLOTS // 2 - 1) as i:
                for s in range(2):
                    expert(2 * i + s, s, i)
            expert(MOE_SLOTS - 2, 0, more=1)
            expert(MOE_SLOTS - 1, 1, more=0)


def kernel(**inputs):
    import numpy as np
    import concourse.bacc as bacc
    from concourse.bass_utils import run_bass_kernel_spmd

    a = {k: np.asarray(v) for k, v in inputs.items()}

    def by_partition(v, dt=np.float32):
        return np.ascontiguousarray(v.reshape(-1, P).T)

    xp = np.zeros((TOKENS, C), np.float32)
    xp[:NODES] = a["x"]

    def edges(v):
        e = np.zeros(P * EC, v.dtype)
        e[:EDGES] = v
        return e.reshape(P, EC)

    w_qkv = np.zeros((C, QKV), np.float32)
    for h in range(HEADS):
        rows = slice(h * DH, (h + 1) * DH)
        w_qkv[rows, h * DH:(h + 1) * DH] = a["L0_mix_Wv"]
        w_qkv[rows, C + h * KR:C + (h + 1) * KR] = a["L0_mix_Wq"]
        w_qkv[rows, C + HR + h * KR:C + HR + (h + 1) * KR] = a["L0_mix_Wk"]

    up = np.zeros((2, EXPERTS, 2 * HH, C), np.float32)
    up[0, :, :H], up[1, :, :H] = a["L0_ffn_w1"], a["L0_ffn_w3"]
    up = up.reshape(2, EXPERTS, 2, HH, KC, P)
    w_13 = np.ascontiguousarray(up.transpose(5, 1, 4, 2, 0, 3)).reshape(P, EXPERTS, KC * W13)
    down = np.zeros((EXPERTS, C, 2 * HH), np.float32)
    down[:, :, :H] = a["L0_ffn_w2"]
    w_down = np.ascontiguousarray(down.reshape(EXPERTS, C, NHB, HB).transpose(3, 0, 2, 1)).reshape(HB, -1)

    arrays = {
        "x": xp, "src": edges(a["src"]), "dst": edges(a["dst"]), "edge_w": edges(a["edge_weight"]),
        "w_gnn": a["L0_gnn_weight"], "wx_t": np.ascontiguousarray(a["L0_mix_Wx"].T), "w_qkv": w_qkv,
        "ln1_g": by_partition(a["L0_mix_ln1_g"]), "ln1_b": by_partition(a["L0_mix_ln1_b"]),
        "bx": by_partition(a["L0_mix_bx"]), "w_o": a["L0_mix_Wo"], "b_o": a["L0_mix_bo"].reshape(1, C),
        "ln2_g": by_partition(a["L0_mix_ln2_g"]), "ln2_b": by_partition(a["L0_mix_ln2_b"]),
        "w_1": a["L0_mix_W1"], "b_1": by_partition(a["L0_mix_b1"]), "w_2": a["L0_mix_W2"], "b_2": a["L0_mix_b2"],
        "router_t": np.ascontiguousarray(a["L0_ffn_router_w"].T), "w_13": w_13, "w_down": w_down,
    }
    nc = bacc.Bacc("TRN2", target_bir_lowering=False, num_devices=1)
    aps = {k: nc.dram_tensor(f"in_{k}", v.shape, mybir.dt.from_np(v.dtype), kind="ExternalInput").ap()
           for k, v in arrays.items()}
    out = nc.dram_tensor("out_rows_dram", (NODES, C), mybir.dt.float32, kind="ExternalOutput").ap()
    gps_layer(nc, out=out, **aps)
    r = run_bass_kernel_spmd(nc, [{f"in_{k}": v for k, v in arrays.items()}], core_ids=[0])
    return r.results[0]["out_rows_dram"]
```
